# Optimizing a Trainium2 kernel written in Bass

```python
import numpy as np
import jax
import jax.numpy as jnp

def _softmax(x, axis=-1):
    return jax.nn.softmax(x, axis=axis)

def _gelu(x):
    return jax.nn.gelu(x, approximate=True)

def _silu(x):
    return jax.nn.silu(x)

def _sigmoid(x):
    return jax.nn.sigmoid(x)

def _layernorm(x, axis=-1, eps=1e-05):
    m = jnp.mean(x, axis=axis, keepdims=True)
    v = jnp.var(x, axis=axis, keepdims=True)
    return (x - m) / jnp.sqrt(v + eps)

def _scatter_add(tgt, idx, src, axis=0):
    return tgt.at[idx].add(src)

def _segment_sum(src, seg, n):
    return jax.ops.segment_sum(src, seg, n)
kernel_name = 'mk_metaformer_d2_conv_nhwc256_r2_eaafd2'

def setup_inputs(seed: int=0):
    np.random.seed(seed)
    _w = jnp.asarray

    def _rec_inputs():
        import jax
        import jax.numpy as jnp
        _gk = jax.random.key(seed)
        x = -0.0003929 + 0.9999 * jax.random.normal(jax.random.fold_in(_gk, 1), (1, 256, 64, 128), jnp.float32)
        return x
    x = _rec_inputs()

    def _L0_conv_setup():
        import jax, jax.numpy as jnp
        import numpy as np
        EPS = 1e-05

        def _ln(x, w):
            m = jnp.mean(x, axis=-1, keepdims=True)
            v = jnp.mean((x - m) ** 2, axis=-1, keepdims=True)
            return (x - m) * jax.lax.rsqrt(v + EPS) * w
        key = jax.random.key(seed)
        ks = jax.random.split(key, 16)
        B, NP, NC, E, C = (1, 256, 64, 128, 64)
        s = 0.02
        return {'z': jax.random.normal(ks[0], (B, NP, NC, E), jnp.float32), 'protein_pair': jax.random.normal(ks[1], (B, NP, NP, E), jnp.float32), 'compound_pair': jax.random.normal(ks[2], (B, NC, NC, E), jnp.float32), 'z_mask': jnp.ones((B, NP, NC, 1), jnp.float32), 'ln_w': jnp.ones((E,), jnp.float32), 'lnc_w': jnp.ones((C,), jnp.float32), 'gw1': jax.random.normal(ks[3], (E, C), jnp.float32) * s, 'gw2': jax.random.normal(ks[4], (E, C), jnp.float32) * s, 'w1': jax.random.normal(ks[5], (E, C), jnp.float32) * s, 'b1': jax.random.normal(ks[6], (C,), jnp.float32) * s, 'w2': jax.random.normal(ks[7], (E, C), jnp.float32) * s, 'b2': jax.random.normal(ks[8], (C,), jnp.float32) * s, 'we': jax.random.normal(ks[9], (E, E), jnp.float32) * s, 'be': jax.random.normal(ks[10], (E,), jnp.float32) * s, 'ws': jax.random.normal(ks[11], (C, E), jnp.float32) * s, 'bs': jax.random.normal(ks[12], (E,), jnp.float32) * s}
    _L0_conv_all = _L0_conv_setup()
    _L0_conv_in = {k: v for k, v in _L0_conv_all.items() if k in ('protein_pair', 'compound_pair', 'z_mask', 'ln_w', 'lnc_w', 'gw1', 'gw2', 'w1', 'b1', 'w2', 'b2', 'we', 'be', 'ws', 'bs')}
    del _L0_conv_all

    def _L0_ffn_setup():
        import jax, jax.numpy as jnp
        import numpy as np
        TOP_K = 2
        LN_EPS = 1e-05
        key = jax.random.key(seed)
        ks = jax.random.split(key, 8)
        B, S, D, E, H = (16, 512, 128, 8, 512)
        x = jax.random.normal(ks[0], (B, S, D), dtype=jnp.float32)
        Wr = jax.random.normal(ks[1], (D, E), dtype=jnp.float32) * 0.1
        br = jnp.zeros((E,), dtype=jnp.float32)
        ln_g = jnp.ones((E, D), dtype=jnp.float32)
        ln_b = jnp.zeros((E, D), dtype=jnp.float32)
        W1 = jax.random.normal(ks[2], (E, D, H), dtype=jnp.float32) * (1.0 / np.sqrt(D))
        b1 = jnp.zeros((E, H), dtype=jnp.float32)
        W2 = jax.random.normal(ks[3], (E, H, D), dtype=jnp.float32) * (1.0 / np.sqrt(H))
        b2 = jnp.zeros((E, D), dtype=jnp.float32)
        return {'x': x, 'Wr': Wr, 'br': br, 'ln_g': ln_g, 'ln_b': ln_b, 'W1': W1, 'b1': b1, 'W2': W2, 'b2': b2}
    _L0_ffn_all = _L0_ffn_setup()
    _L0_ffn_in = {k: v for k, v in _L0_ffn_all.items() if k in ('Wr', 'br', 'ln_g', 'ln_b', 'W1', 'b1', 'W2', 'b2')}
    del _L0_ffn_all

    def _L1_conv_setup():
        import jax, jax.numpy as jnp
        import numpy as np
        E = 128
        C = 64
        B, NP, NC = (1, 256, 64)

        def layernorm(x, w, b, eps=1e-05):
            m = jnp.mean(x, axis=-1, keepdims=True)
            v = jnp.mean(jnp.square(x - m), axis=-1, keepdims=True)
            return (x - m) * jax.lax.rsqrt(v + eps) * w + b
        key = jax.random.key(seed)
        ks = jax.random.split(key, 12)
        s = 0.02
        return {'z': jax.random.normal(ks[0], (B, NP, NC, E), jnp.float32), 'protein_pair': jax.random.normal(ks[1], (B, NP, NP, C), jnp.float32), 'compound_pair': jax.random.normal(ks[2], (B, NC, NC, C), jnp.float32), 'z_mask': jax.random.randint(ks[3], (B, NP, NC, 1), 0, 2).astype(jnp.float32), 'ln_w': jnp.ones((E,), jnp.float32), 'ln_b': jnp.zeros((E,), jnp.float32), 'lnc_w': jnp.ones((C,), jnp.float32), 'lnc_b': jnp.zeros((C,), jnp.float32), 'gate_w': jax.random.normal(ks[4], (E, C), jnp.float32) * s, 'gate_b': jnp.zeros((C,), jnp.float32), 'lin_w': jax.random.normal(ks[5], (E, C), jnp.float32) * s, 'lin_b': jnp.zeros((C,), jnp.float32), 'eg_w': jax.random.normal(ks[6], (E, E), jnp.float32) * s, 'eg_b': jnp.zeros((E,), jnp.float32), 'as_w': jax.random.normal(ks[7], (C, E), jnp.float32) * s, 'as_b': jnp.zeros((E,), jnp.float32)}
    _L1_conv_all = _L1_conv_setup()
    _L1_conv_in = {k: v for k, v in _L1_conv_all.items() if k in ('protein_pair', 'compound_pair', 'z_mask', 'ln_w', 'ln_b', 'lnc_w', 'lnc_b', 'gate_w', 'gate_b', 'lin_w', 'lin_b', 'eg_w', 'eg_b', 'as_w', 'as_b')}
    del _L1_conv_all

    def _L1_ffn_setup():
        import jax, jax.numpy as jnp
        import numpy as np
        from jax import lax
        key = jax.random.key(seed)
        B, T, I, H = (32, 1024, 128, 128)
        ks = jax.random.split(key, 13)
        s = 1.0 / np.sqrt(H)

        def w(k, shape):
            return jax.random.uniform(k, shape, jnp.float32, -s, s)
        return {'x': jax.random.normal(ks[0], (B, T, I), jnp.float32), 'U_i': w(ks[1], (I, H)), 'V_i': w(ks[2], (H, H)), 'b_i': w(ks[3], (H,)), 'U_f': w(ks[4], (I, H)), 'V_f': w(ks[5], (H, H)), 'b_f': w(ks[6], (H,)), 'U_c': w(ks[7], (I, H)), 'V_c': w(ks[8], (H, H)), 'b_c': w(ks[9], (H,)), 'U_o': w(ks[10], (I, H)), 'V_o': w(ks[11], (H, H)), 'b_o': w(ks[12], (H,))}
    _L1_ffn_all = _L1_ffn_setup()
    _L1_ffn_in = {k: v for k, v in _L1_ffn_all.items() if k in ('U_i', 'V_i', 'b_i', 'U_f', 'V_f', 'b_f', 'U_c', 'V_c', 'b_c', 'U_o', 'V_o', 'b_o')}
    del _L1_ffn_all
    return {'x': x, 'L0_conv_protein_pair': _L0_conv_in['protein_pair'], 'L0_conv_compound_pair': _L0_conv_in['compound_pair'], 'L0_conv_z_mask': _L0_conv_in['z_mask'], 'L0_conv_ln_w': _L0_conv_in['ln_w'], 'L0_conv_lnc_w': _L0_conv_in['lnc_w'], 'L0_conv_gw1': _L0_conv_in['gw1'], 'L0_conv_gw2': _L0_conv_in['gw2'], 'L0_conv_w1': _L0_conv_in['w1'], 'L0_conv_b1': _L0_conv_in['b1'], 'L0_conv_w2': _L0_conv_in['w2'], 'L0_conv_b2': _L0_conv_in['b2'], 'L0_conv_we': _L0_conv_in['we'], 'L0_conv_be': _L0_conv_in['be'], 'L0_conv_ws': _L0_conv_in['ws'], 'L0_conv_bs': _L0_conv_in['bs'], 'L0_ffn_Wr': _L0_ffn_in['Wr'], 'L0_ffn_br': _L0_ffn_in['br'], 'L0_ffn_ln_g': _L0_ffn_in['ln_g'], 'L0_ffn_ln_b': _L0_ffn_in['ln_b'], 'L0_ffn_W1': _L0_ffn_in['W1'], 'L0_ffn_b1': _L0_ffn_in['b1'], 'L0_ffn_W2': _L0_ffn_in['W2'], 'L0_ffn_b2': _L0_ffn_in['b2'], 'L1_conv_protein_pair': _L1_conv_in['protein_pair'], 'L1_conv_compound_pair': _L1_conv_in['compound_pair'], 'L1_conv_z_mask': _L1_conv_in['z_mask'], 'L1_conv_ln_w': _L1_conv_in['ln_w'], 'L1_conv_ln_b': _L1_conv_in['ln_b'], 'L1_conv_lnc_w': _L1_conv_in['lnc_w'], 'L1_conv_lnc_b': _L1_conv_in['lnc_b'], 'L1_conv_gate_w': _L1_conv_in['gate_w'], 'L1_conv_gate_b': _L1_conv_in['gate_b'], 'L1_conv_lin_w': _L1_conv_in['lin_w'], 'L1_conv_lin_b': _L1_conv_in['lin_b'], 'L1_conv_eg_w': _L1_conv_in['eg_w'], 'L1_conv_eg_b': _L1_conv_in['eg_b'], 'L1_conv_as_w': _L1_conv_in['as_w'], 'L1_conv_as_b': _L1_conv_in['as_b'], 'L1_ffn_U_i': _L1_ffn_in['U_i'], 'L1_ffn_V_i': _L1_ffn_in['V_i'], 'L1_ffn_b_i': _L1_ffn_in['b_i'], 'L1_ffn_U_f': _L1_ffn_in['U_f'], 'L1_ffn_V_f': _L1_ffn_in['V_f'], 'L1_ffn_b_f': _L1_ffn_in['b_f'], 'L1_ffn_U_c': _L1_ffn_in['U_c'], 'L1_ffn_V_c': _L1_ffn_in['V_c'], 'L1_ffn_b_c': _L1_ffn_in['b_c'], 'L1_ffn_U_o': _L1_ffn_in['U_o'], 'L1_ffn_V_o': _L1_ffn_in['V_o'], 'L1_ffn_b_o': _L1_ffn_in['b_o']}

def reference(x, L0_conv_protein_pair, L0_conv_compound_pair, L0_conv_z_mask, L0_conv_ln_w, L0_conv_lnc_w, L0_conv_gw1, L0_conv_gw2, L0_conv_w1, L0_conv_b1, L0_conv_w2, L0_conv_b2, L0_conv_we, L0_conv_be, L0_conv_ws, L0_conv_bs, L0_ffn_Wr, L0_ffn_br, L0_ffn_ln_g, L0_ffn_ln_b, L0_ffn_W1, L0_ffn_b1, L0_ffn_W2, L0_ffn_b2, L1_conv_protein_pair, L1_conv_compound_pair, L1_conv_z_mask, L1_conv_ln_w, L1_conv_ln_b, L1_conv_lnc_w, L1_conv_lnc_b, L1_conv_gate_w, L1_conv_gate_b, L1_conv_lin_w, L1_conv_lin_b, L1_conv_eg_w, L1_conv_eg_b, L1_conv_as_w, L1_conv_as_b, L1_ffn_U_i, L1_ffn_V_i, L1_ffn_b_i, L1_ffn_U_f, L1_ffn_V_f, L1_ffn_b_f, L1_ffn_U_c, L1_ffn_V_c, L1_ffn_b_c, L1_ffn_U_o, L1_ffn_V_o, L1_ffn_b_o):
    import jax
    import jax.numpy as jnp

    def _L0_conv_ref(z, protein_pair, compound_pair, z_mask, ln_w, lnc_w, gw1, gw2, w1, b1, w2, b2, we, be, ws, bs):
        import jax, jax.numpy as jnp
        import numpy as np
        EPS = 1e-05

        def _ln(x, w):
            m = jnp.mean(x, axis=-1, keepdims=True)
            v = jnp.mean((x - m) ** 2, axis=-1, keepdims=True)
            return (x - m) * jax.lax.rsqrt(v + EPS) * w
        z = _ln(z, ln_w)
        pp = _ln(protein_pair, ln_w)
        cp = _ln(compound_pair, ln_w)
        ab1 = jax.nn.sigmoid(z @ gw1) * (z @ w1 + b1) * z_mask
        ab2 = jax.nn.sigmoid(z @ gw2) * (z @ w2 + b2) * z_mask
        pp = jax.nn.sigmoid(pp @ gw2) * (pp @ w2 + b2)
        cp = jax.nn.sigmoid(cp @ gw1) * (cp @ w1 + b1)
        g = jax.nn.sigmoid(z @ we + be)
        block1 = jnp.einsum('bikc,bkjc->bijc', pp, ab1)
        block2 = jnp.einsum('bikc,bjkc->bijc', ab2, cp)
        out = g * (_ln(block1 + block2, lnc_w) @ ws + bs) * z_mask
        return out

    def _L0_ffn_ref(x, Wr, br, ln_g, ln_b, W1, b1, W2, b2):
        import jax, jax.numpy as jnp
        import numpy as np
        TOP_K = 2
        LN_EPS = 1e-05
        B, S, D = x.shape
        N = B * S
        xt = x.reshape(N, D)
        logits = xt @ Wr + br
        probs = jax.nn.softmax(logits, axis=-1)
        top_p, top_idx = jax.lax.top_k(probs, TOP_K)
        weights = top_p / top_p.sum(axis=-1, keepdims=True)
        mu = xt.mean(axis=-1, keepdims=True)
        var = ((xt - mu) ** 2).mean(axis=-1, keepdims=True)
        xn = (xt - mu) * jax.lax.rsqrt(var + LN_EPS)
        xe = xn[None, :, :] * ln_g[:, None, :] + ln_b[:, None, :]
        h = jax.nn.gelu(jnp.einsum('end,edh->enh', xe, W1) + b1[:, None, :], approximate=False)
        y = jnp.einsum('enh,ehd->end', h, W2) + b2[:, None, :]
        y_tok = jnp.transpose(y, (1, 0, 2))
        sel = jnp.take_along_axis(y_tok, top_idx[:, :, None], axis=1)
        out = (weights[:, :, None] * sel).sum(axis=1)
        return out.reshape(B, S, D)

    def _L1_conv_ref(z, protein_pair, compound_pair, z_mask, ln_w, ln_b, lnc_w, lnc_b, gate_w, gate_b, lin_w, lin_b, eg_w, eg_b, as_w, as_b):
        import jax, jax.numpy as jnp
        import numpy as np
        E = 128
        C = 64
        B, NP, NC = (1, 256, 64)

        def layernorm(x, w, b, eps=1e-05):
            m = jnp.mean(x, axis=-1, keepdims=True)
            v = jnp.mean(jnp.square(x - m), axis=-1, keepdims=True)
            return (x - m) * jax.lax.rsqrt(v + eps) * w + b
        z = layernorm(z, ln_w, ln_b)
        ab = jax.nn.sigmoid(z @ gate_w + gate_b) * (z @ lin_w + lin_b) * z_mask
        g = jax.nn.sigmoid(z @ eg_w + eg_b)
        block1 = jnp.einsum('bikc,bkjc->bijc', protein_pair, ab)
        block2 = jnp.einsum('bikc,bjkc->bijc', ab, compound_pair)
        out = g * (layernorm(block1 + block2, lnc_w, lnc_b) @ as_w + as_b) * z_mask
        return out

    def _L1_ffn_ref(x, U_i, V_i, b_i, U_f, V_f, b_f, U_c, V_c, b_c, U_o, V_o, b_o):
        import jax, jax.numpy as jnp
        import numpy as np
        from jax import lax
        B, T, _ = x.shape
        H = U_i.shape[1]
        xt = jnp.swapaxes(x, 0, 1)
        xi = xt @ U_i + b_i
        xf = xt @ U_f + b_f
        xg = xt @ U_c + b_c
        xo = xt @ U_o + b_o
        h0 = jnp.zeros((B, H), x.dtype)
        c0 = jnp.zeros((B, H), x.dtype)

        def step(carry, xs):
            h, c = carry
            xi_t, xf_t, xg_t, xo_t = xs
            i_t = jax.nn.sigmoid(xi_t + h @ V_i)
            f_t = jax.nn.sigmoid(xf_t + h @ V_f)
            g_t = jnp.tanh(xg_t + h @ V_c)
            o_t = jax.nn.sigmoid(xo_t + h @ V_o)
            c_new = h * c + i_t * g_t
            h_new = o_t * jnp.tanh(c_new)
            return ((h_new, c_new), h_new)
        (_, _), hs = lax.scan(step, (h0, c0), (xi, xf, xg, xo))
        return jnp.swapaxes(hs, 0, 1)

    def _gn(v, G=32, eps=1e-05):
        B_, H_, W_, C_ = v.shape
        g = v.reshape(B_, H_, W_, G, C_ // G)
        m = jnp.mean(g, axis=(1, 2, 4), keepdims=True)
        s = jnp.var(g, axis=(1, 2, 4), keepdims=True)
        return ((g - m) / jnp.sqrt(s + eps)).reshape(v.shape)

    def _ln_c(v, eps=1e-06):
        m = jnp.mean(v, axis=-1, keepdims=True)
        s = jnp.var(v, axis=-1, keepdims=True)
        return (v - m) / jnp.sqrt(s + eps)

    def _ln_t(v, eps=1e-05):
        m = jnp.mean(v, axis=-1, keepdims=True)
        s = jnp.var(v, axis=-1, keepdims=True)
        return (v - m) / jnp.sqrt(s + eps)

    def _to_tokens(v):
        B_, H_, W_, C_ = v.shape
        return v.reshape(B_, H_ * W_, C_)

    def _from_tokens(t, like):
        return t.reshape(like.shape)
    x = x + _L0_conv_ref(_ln_c(x), L0_conv_protein_pair, L0_conv_compound_pair, L0_conv_z_mask, L0_conv_ln_w, L0_conv_lnc_w, L0_conv_gw1, L0_conv_gw2, L0_conv_w1, L0_conv_b1, L0_conv_w2, L0_conv_b2, L0_conv_we, L0_conv_be, L0_conv_ws, L0_conv_bs)
    t = _to_tokens(x)
    t = t + _L0_ffn_ref(_ln_t(t), L0_ffn_Wr, L0_ffn_br, L0_ffn_ln_g, L0_ffn_ln_b, L0_ffn_W1, L0_ffn_b1, L0_ffn_W2, L0_ffn_b2)
    x = _from_tokens(t, x)
    x = x + _L1_conv_ref(_ln_c(x), L1_conv_protein_pair, L1_conv_compound_pair, L1_conv_z_mask, L1_conv_ln_w, L1_conv_ln_b, L1_conv_lnc_w, L1_conv_lnc_b, L1_conv_gate_w, L1_conv_gate_b, L1_conv_lin_w, L1_conv_lin_b, L1_conv_eg_w, L1_conv_eg_b, L1_conv_as_w, L1_conv_as_b)
    t = _to_tokens(x)
    t = t + _L1_ffn_ref(_ln_t(t), L1_ffn_U_i, L1_ffn_V_i, L1_ffn_b_i, L1_ffn_U_f, L1_ffn_V_f, L1_ffn_b_f, L1_ffn_U_c, L1_ffn_V_c, L1_ffn_b_c, L1_ffn_U_o, L1_ffn_V_o, L1_ffn_b_o)
    x = _from_tokens(t, x)
    return x

_drawn_inputs = setup_inputs


def setup_inputs(seed=0):
    import zlib

    import numpy as np

    out = dict(_drawn_inputs(seed))
    spreads = {'L0_conv_ln_w': (1.0, 0.2),
     'L0_conv_lnc_w': (1.0, 0.2),
     'L0_ffn_br': (0.0, 0.1),
     'L0_ffn_ln_g': (1.0, 0.2),
     'L0_ffn_ln_b': (0.0, 0.1),
     'L0_ffn_b1': (0.0, 0.1),
     'L0_ffn_b2': (0.0, 0.1),
     'L1_conv_ln_w': (1.0, 0.6),
     'L1_conv_ln_b': (0.0, 0.8),
     'L1_conv_lnc_w': (1.0, 0.6),
     'L1_conv_lnc_b': (0.0, 0.8),
     'L1_conv_gate_b': (0.0, 2.0),
     'L1_conv_lin_b': (0.0, 0.376),
     'L1_conv_eg_b': (0.0, 2.0),
     'L1_conv_as_b': (0.0, 0.1)}
    factors = {'L0_conv_be': 5.679,
     'L1_conv_gate_w': 8.0,
     'L1_conv_eg_w': 8.0,
     'L1_ffn_V_i': 8.0,
     'L1_ffn_b_i': 8.0,
     'L1_ffn_V_c': 4.283,
     'L1_ffn_b_c': 5.163,
     'L1_ffn_V_o': 8.0,
     'L1_ffn_b_o': 8.0}
    for name, (base, spread) in spreads.items():
        noise = np.random.default_rng([zlib.crc32(name.encode()), seed]).standard_normal(out[name].shape)
        drawn = base * np.exp(spread * noise) if base else spread * noise
        out[name] = jnp.asarray(drawn.astype(out[name].dtype))
    for name, factor in factors.items():
        out[name] = (out[name] * factor).astype(out[name].dtype)
    return out
```

```python
from contextlib import ExitStack

import concourse.bass as bass
from concourse import mybir

F32 = mybir.dt.float32
BF16 = mybir.dt.bfloat16
I32 = mybir.dt.int32
U32 = mybir.dt.uint32
ALU = mybir.AluOpType
ACT = mybir.ActivationFunctionType
AX = mybir.AxisListType

P = 128
NP_, NC_, E, C = 256, 64, 128, 64
TILES = NP_ * NC_ // P
G = 4
GROUPS = TILES // G
EXPERTS, HID = 8, 512
HC = HID // P
ICS = NP_ // P
EPS_LN = 1e-5
EPS_LNC = 1e-6
CHUNK_TOL = 2.0 ** -19
WARM = 64



def engine_loop(eng, total, unroll, stages):
    lag = max(l for _, l in stages)
    head = min(total, -(-lag // unroll) * unroll)

    for t in range(head):
        for stage, l in stages:
            if t >= l:
                stage(t - l, (t - l) % unroll)
    if total > head:
        with eng.Fori(head // unroll, total // unroll) as i:
            for u in range(unroll):
                for stage, l in stages:
                    stage(i * unroll + (u - l), (u - l) % unroll)
    for t in range(total, total + lag):
        for stage, l in stages:
            if 0 <= t - l < total:
                stage(t - l, (t - l) % unroll)


class Flow:

    def __init__(self, chip, name, depth=0):
        self.sem, self.depth = chip.sem(name), depth

    def open(self, eng):
        eng.sem_inc(self.sem, self.depth)

    def done(self, ins):
        ins.then_inc(self.sem, 1)

    def ready(self, eng, n):
        eng.wait_ge(self.sem, n + (1 + self.depth))

    def free(self, eng, n):
        eng.wait_ge(self.sem, n + 1)


class Chain:

    def __init__(self, chip, name, eng=None):
        self.sem, self.n = chip.sem(name), 0

    def on(self, eng):
        self.eng = eng
        return self

    def __call__(self, ins):
        self.n += 1
        ins.then_inc(self.sem, 1)
        self.eng.wait_ge(self.sem, self.n)


class Chip:

    def __init__(self, nc, ctx):
        self.nc, self.ctx, self.sems = nc, ctx, []
        sb = self.sb
        self.x = sb("x_tiles", [P, TILES, E])
        self.ab = sb("ab_tiles", [P, TILES, 2, C])
        self.work = sb("work", [P, 2 * NC_ * P])
        self.ident = sb("ident", [P, P])
        self.cols = sb("cols", [P, 64])
        self.ones3 = sb("ones3", [3, P], BF16)
        self.small = sb("small", [P, 3740])
        self.banks = ctx.enter_context(nc.psum_tensor("banks", [P, 8, 512], F32))

    def sb(self, name, shape, dt=F32):
        return self.ctx.enter_context(self.nc.sbuf_tensor(name, shape, dt))

    def sem(self, name):
        self.sems.append(self.nc.alloc_semaphore(name=f"{self.tag}_{name}"))
        return self.sems[-1]

    def bank(self, b):
        return self.banks[:, b, :]

    def phase(self, tag):
        self.tag = tag
        return ExitStack()

    def recycle(self):
        self.nc.clear_and_free_semaphores(self.sems)
        self.nc.all_engine_barrier()
        self.sems = []


class Carve:

    def __init__(self, base):
        self.base, self.at = base, 0

    def __call__(self, *dims, parts=P, dt=F32):
        n = 1
        for d in dims:
            n *= d
        words = n if dt in (F32, I32, U32) else (n + 1) // 2
        ap = self.base[0:parts, self.at:self.at + words]
        self.at += words
        assert self.at <= self.base.shape[1], "region too small"
        if dt != F32:
            ap = ap.bitcast(dt)
        names = "abcd"[:len(dims)]
        if len(dims) > 1:
            ap = ap.rearrange(f"p ({' '.join(names)}) -> p {' '.join(names)}", **dict(zip(names, dims)))
        return ap


def row(v):
    return v.rearrange("(a n) -> a n", a=1)


COL = {"l0_ln_w": 0, "l1_ln_w": 1, "l1_ln_b": 2, "l0_lnc_w": 3, "l1_lnc_w": 4, "l1_lnc_b": 5,
       "moe_g": 8, "moe_b": 16, "moe_b1": 24}
N_COLS = 56


def setup(nc, chip, par):
    rows = chip.small[0:N_COLS, 0:P]
    one_row = {"l0_ln_w": par["l0_ln_w"], "l1_ln_w": par["l1_ln_w"], "l1_ln_b": par["l1_ln_b"]}
    half_row = {"l0_lnc_w": par["l0_lnc_w"], "l1_lnc_w": par["l1_lnc_w"], "l1_lnc_b": par["l1_lnc_b"]}
    n_dma = len(one_row) + 2 * len(half_row) + 3
    with chip.phase("setup"):
        rows_in, zeroed, ident_made, turned, ones_made = (
            chip.sem(n) for n in ("rows_in", "zeroed", "ident", "turned", "ones"))
        with nc.Block() as block:
            @block.sync
            def _(sp):
                sp.wait_ge(zeroed, 1)
                for k, v in one_row.items():
                    sp.dma_start(rows[COL[k]:COL[k] + 1, :], row(v)).then_inc(rows_in, 16)
                for k, v in half_row.items():
                    for h in range(2):
                        sp.dma_start(rows[COL[k]:COL[k] + 1, h * C:(h + 1) * C], row(v)).then_inc(rows_in, 16)
                for k, v in (("moe_g", par["moe_ln_g"]), ("moe_b", par["moe_ln_b"])):
                    sp.dma_start(rows[COL[k]:COL[k] + EXPERTS, :], v).then_inc(rows_in, 16)
                sp.dma_start(rows[COL["moe_b1"]:COL["moe_b1"] + EXPERTS * HC, :],
                             par["moe_b1"].rearrange("e (h p) -> (e h) p", p=P)).then_inc(rows_in, 16)

            @block.gpsimd
            def _(pool):
                pool.memset(chip.ident[:, :], 0.0).then_inc(ident_made, 1)
                pool.wait_ge(ident_made, 1)
                pool.affine_select(out=chip.ident[:, :], in_=chip.ident[:, :], compare_op=ALU.not_equal,
                                   fill=1.0, base=0, pattern=[[-1, P]], channel_multiplier=1
                                   ).then_inc(ident_made, 1)

            @block.vector
            def _(dve):
                dve.memset(rows, 0.0).then_inc(zeroed, 1)
                dve.memset(chip.ones3[:, :], 1.0).then_inc(ones_made, 1)
                dve.wait_ge(turned, 1)
                dve.tensor_copy(chip.cols[:, 0:N_COLS], chip.banks[:, 0, 0:N_COLS]).then_inc(ones_made, 1)

            @block.tensor
            def _(pe):
                pe.wait_ge(rows_in, 16 * n_dma)
                pe.wait_ge(ident_made, 2)
                pe.transpose(chip.banks[:, 0, 0:N_COLS], rows, chip.ident[0:N_COLS, 0:N_COLS]).then_inc(turned, 1)


def col(chip, name, k=0, lo=0, hi=P):
    c = COL[name] + k
    return chip.cols[lo:hi, c:c + 1]


class Linear:

    def __init__(self, chip, carve, tag, weights, biases, g, b, bank, copies=1, scratch=None):
        self.chip, self.weights, self.biases, self.g, self.b = chip, weights, biases, g, b
        self.n = n = sum(w.shape[1] for w in weights)
        self.k = weights[0].shape[0]
        self.copies = copies
        self.w = carve(n)
        self.bias3 = carve(n, parts=3, dt=BF16)
        scratch = carve if scratch is None else scratch
        self.raw = scratch(n)
        self.total, self.rest = scratch(n, parts=1), scratch(n, parts=1)
        self.pieces = [scratch(n, parts=1, dt=BF16) for _ in range(3)]
        self.product = chip.banks[0:1, bank, 0:n]
        self.zeroed, self.loaded, self.folded, self.shifted, self.cut, self.spread = (
            chip.sem(f"{tag}_{s}") for s in ("zeroed", "loaded", "folded", "shifted", "cut", "spread"))
        self.n_loads = len(weights) * copies + sum(x is not None for x, _ in biases)
        self.chain = Chain(chip, f"{tag}_chain")

    def load(self, sp):
        sp.wait_ge(self.zeroed, 1)
        at = 0
        for w in self.weights:
            for h in range(self.copies):
                sp.dma_start(self.raw[h * self.k:(h + 1) * self.k, at:at + w.shape[1]], w).then_inc(self.loaded, 16)
            at += w.shape[1]
        at = 0
        for v, n in self.biases:
            if v is not None:
                sp.dma_start(self.total[0:1, at:at + n], row(v)).then_inc(self.loaded, 16)
            at += n
        sp.wait_ge(self.cut, 1)
        for k in range(3):
            sp.dma_start(self.bias3[k:k + 1, :], self.pieces[k]).then_inc(self.spread, 16)

    def fold(self, dve):
        chain = self.chain.on(dve)
        dve.memset(self.total, 0.0).then_inc(self.zeroed, 1)
        dve.wait_ge(self.loaded, 16 * self.n_loads)
        rows = self.k * self.copies
        dve.tensor_scalar(self.w[0:rows, :], self.raw[0:rows, :], self.g, None, ALU.mult).then_inc(self.folded, 1)
        if self.b is not None:
            dve.wait_ge(self.shifted, 1)
            chain(dve.tensor_tensor(self.total, self.total, self.product, ALU.add))
        for k in range(3):
            piece = dve.tensor_copy(self.pieces[k], self.total)
            if k == 2:
                piece.then_inc(self.cut, 1)
            else:
                chain(piece)
                chain(dve.tensor_tensor(self.rest, self.total, self.pieces[k], ALU.subtract))
                chain(dve.tensor_copy(self.total, self.rest))

    def shift(self, pe):
        if self.b is not None:
            pe.wait_ge(self.loaded, 16 * self.n_loads)
            pe.matmul(self.product, self.b, self.raw[0:self.k, :], start=True, stop=True).then_inc(self.shifted, 1)

    def await_ready(self, pe):
        pe.wait_ge(self.folded, 1)
        pe.wait_ge(self.spread, 48)


class Norm:

    def __init__(self, chip, carve, eps, banks, depth=2, zn=None, inverse=False, width=E):
        self.chip, self.eps, self.banks, self.depth = chip, eps, banks, depth
        self.width = width
        self.st = carve(depth, G, 6)
        self.mv = carve(depth, G, 2)
        self.r = carve(depth, G)
        self.inv = carve(depth, G) if inverse else None
        self.a, self.b, self.c = carve(G), carve(G), carve(G)
        self.const = carve(3, G)
        self.zn = carve(depth, G, width) if zn is None else zn
        self.zt = carve(2, G * P)
        self.stat, self.scaled = Flow(chip, "stat"), Flow(chip, "scaled")
        self.agg = Flow(chip, "agg")
        self.half, self.links, self.paced = chip.sem("half"), chip.sem("links"), chip.sem("paced")
        self.applied = Flow(chip, "applied")
        self.turned = Flow(chip, "turned", depth)
        self.kept = Flow(chip, "kept", len(set(banks)))

    def open_pool(self, pool):
        for k, v in enumerate((self.eps[0], self.eps[-1], -0.5)):
            pool.memset(self.const[:, k, :], v).then_inc(self.half, 1)
        pool.wait_ge(self.half, 3)

    def open_pe(self, pe):
        self.turned.open(pe)

    def open_act(self, act):
        self.kept.open(act)

    def stats(self, dve, src, n, u):
        for t in range(G):
            last = dve.bn_stats(self.st[:, u, t, :], src[:, t, :])
        self.stat.done(last)
        self.stat.ready(dve, n)
        dve.sem_inc(self.paced, 1)
        for t in range(G):
            last = dve.bn_aggr(self.mv[:, u, t, :], self.st[:, u, t, :])
        self.agg.done(last)

    def rstd(self, pool, n, u):
        var, r = self.mv[:, u, :, 1], self.r[:, u, :]
        a, b, c = self.a, self.b, self.c
        eps0, eps1, mhalf = (self.const[:, k, :] for k in (0, 1, 2))
        self.agg.ready(pool, n)
        steps = [(a, var, eps0, ALU.add)]
        if len(self.eps) == 1:
            steps += [(r, a, mhalf, ALU.pow)]
        else:
            steps += [(b, a, mhalf, ALU.pow), (c, b, b, ALU.mult), (a, c, var, ALU.mult), (c, a, eps1, ALU.add),
                      (a, c, mhalf, ALU.pow)]
            if self.inv is not None:
                steps += [(self.inv[:, u, :], c, a, ALU.mult)]
            steps += [(r, b, a, ALU.mult)]
        for k, (out, in0, in1, op) in enumerate(steps):
            step = pool.tensor_tensor(out, in0, in1, op)
            if k == len(steps) - 1:
                self.scaled.done(step)
                self.scaled.ready(pool, n)
            else:
                step.then_inc(self.links, 1)
                pool.wait_ge(self.links, n * (len(steps) - 1) + (k + 1))

    def apply(self, dve, src, n, u):
        self.scaled.ready(dve, n)
        self.turned.free(dve, n)
        for t in range(G):
            last = dve.tensor_scalar(self.zn[:, u, t, :], src[:, t, :], self.mv[:, u, t, 0:1],
                                     self.r[:, u, t:t + 1], ALU.subtract, ALU.mult)
        self.applied.done(last)

    def turn(self, pe, n, u):
        self.applied.ready(pe, n)
        self.kept.free(pe, n)
        w = self.width
        for k in range(G * w // P):
            src = self.zn[:, u, :, :].rearrange("p g e -> p (g e)")[:, k * P:(k + 1) * P]
            last = pe.transpose(self.chip.banks[:, self.banks[u % 2], k * P:(k + 1) * P], src, self.chip.ident[:, :])
        self.turned.done(last)

    def keep(self, act, n, u, out=None):
        self.turned.ready(act, n)
        cols = G * self.width
        if out is None:
            out = self.zt[:, u % 2, 0:cols]
        self.kept.done(act.copy(out, self.chip.banks[:, self.banks[u % 2], 0:cols]))


def load_tiles(sp, dst, src, arrived):
    for ic in range(ICS):
        for n in range(4):
            if ic:
                sp.wait_ge(arrived[n], 64)
            sp.dma_start(dst[:, (ic * 16 + n) * G:(ic * 16 + n + 1) * G, :],
                         src[:, ic, n * G:(n + 1) * G, :]).then_inc(arrived[n], 16)
        with sp.Fori(1, 4) as i:
            for u in range(4):
                sp.wait_ge(arrived[u], 16 * i + 64 * ic)
                sp.dma_start(dst[:, bass.ds((i * 4 + (u + ic * 16)) * G, G), :],
                             src[:, ic, bass.ds((i * 4 + u) * G, G), :]).then_inc(arrived[u], 16)


def await_tiles(eng, arrived, n, u):
    eng.wait_ge(arrived[u], 4 * n + (16 - 4 * u))


def project_tokens(nc, chip, tag, par, src):
    gates, lins, (edge, edge_b) = par["gates"], par["lins"], par["edge"]
    NG, NL = C * len(gates), C * len(lins)
    NS = NG + E
    carve = Carve(chip.work)
    xf = chip.x
    with chip.phase(f"{tag}_project"):
        lin = Linear(chip, carve, "w", [w for w, _ in gates] + [edge] + [w for w, _ in lins],
                     [(b, C) for _, b in gates] + [(edge_b, E)] + [(b, C) for _, b in lins],
                     par["ln_w"], par["ln_b"], bank=2)
        norm = Norm(chip, carve, (EPS_LNC, EPS_LN), banks=(0, 1), depth=2)
        sg = carve(2, 2, NS)
        mask = carve(TILES)
        mask_in = chip.sem("mask_in")
        x_in = [chip.sem(f"x_in{k}") for k in range(4)]
        projected = Flow(chip, "projected", 4)
        squashed = Flow(chip, "squashed")
        gated = Flow(chip, "gated", 2)
        masked = Flow(chip, "masked", 2)

        def tiles(n, k=0, m=G):
            return xf[:, bass.ds(n * G + k, m), :]

        with nc.Block() as block:
            @block.sync
            def _(sp):
                sp.dma_start(mask.rearrange("p (i j) -> p i j", i=ICS),
                             par["mask"].rearrange("(i p) j -> p i j", p=P)).then_inc(mask_in, 16)
                lin.load(sp)
                if src is not None:
                    load_tiles(sp, xf, src, x_in)

            @block.vector
            def _(dve):
                gated.open(dve)
                lin.fold(dve)
                dve.wait_ge(mask_in, 16)

                def stats(n, u):
                    if src is not None:
                        await_tiles(dve, x_in, n, u)
                    norm.stats(dve, tiles(n), n, u % 2)

                def apply(n, u):
                    norm.apply(dve, tiles(n), n, u % 2)

                def gate(n, u):
                    for h in range(2):
                        pair = n * 2 + h
                        projected.ready(dve, pair)
                        squashed.ready(dve, pair)
                        for t in range(2):
                            tile = n * G + (2 * h + t)
                            last = dve.scalar_tensor_tensor(
                                chip.ab[:, bass.ds(tile, 1), 0:NL // C, :].rearrange("p a b c -> p (a b c)"),
                                sg[:, h, t, 0:NG], mask[:, bass.ds(tile, 1)],
                                chip.banks[:, 4 + 2 * h + t, NS:NS + NL], ALU.mult, ALU.mult)
                        gated.done(last)

                engine_loop(dve, GROUPS, 4, [(stats, 0), (apply, 1), (gate, 3)])

            @block.gpsimd
            def _(pool):
                norm.open_pool(pool)
                masked.open(pool)
                pool.wait_ge(mask_in, 16)

                def edge_mask(n, u):
                    for h in range(2):
                        pair = n * 2 + h
                        squashed.ready(pool, pair)
                        masked.done(pool.tensor_tensor(
                            tiles(n, 2 * h, 2), sg[:, h, :, NG:NS],
                            mask[:, bass.ds(n * G + 2 * h, 2)].unsqueeze(2).to_broadcast([P, 2, E]), ALU.mult))

                engine_loop(pool, GROUPS, 2, [(lambda n, u: norm.rstd(pool, n, u), 0), (edge_mask, 2)])

            @block.scalar
            def _(act):
                norm.open_act(act)

                def squash(n, u):
                    for h in range(2):
                        pair = n * 2 + h
                        projected.ready(act, pair)
                        masked.free(act, pair)
                        gated.free(act, pair)
                        squashed.done(act.activation(sg[:, h, :, :], chip.banks[:, 4 + 2 * h:6 + 2 * h, 0:NS],
                                                     ACT.Sigmoid))

                def keep(n, u):
                    projected.free(act, n * 2 + 1)
                    norm.keep(act, n, u)

                engine_loop(act, GROUPS, 2, [(keep, 0), (squash, 1)])

            @block.tensor
            def _(pe):
                norm.open_pe(pe)
                projected.open(pe)
                lin.shift(pe)
                lin.await_ready(pe)

                def project(n, u):
                    norm.kept.ready(pe, n)
                    for h in range(2):
                        pair = n * 2 + h
                        gated.free(pe, pair)
                        for t in range(2):
                            out = chip.banks[:, 4 + 2 * h + t, 0:lin.n]
                            k = (2 * h + t) * P
                            pe.matmul(out, chip.ones3[:, :], lin.bias3, start=True, stop=False)
                            last = pe.matmul(out, norm.zt[:, u, k:k + P], lin.w, start=False, stop=True)
                        projected.done(last)

                engine_loop(pe, GROUPS, 2, [(lambda n, u: norm.turn(pe, n, u), 0), (project, 1)])


class PairStream:

    def __init__(self, chip, carve, carve_lin, gate_w, lin_w, lin_b, g, b=None, scratch=None):
        self.chip = chip
        self.stage = carve(4, G, E)
        self.norm = Norm(chip, carve, (EPS_LN,), banks=(0, 1), depth=4, zn=self.stage)
        self.lin = Linear(chip, carve_lin, "w", [gate_w, lin_w], [(None, C), (lin_b, C)], g, b, bank=2,
                          scratch=scratch)
        self.arrived = [chip.sem(f"arrived{u}") for u in range(4)]
        self.projected = Flow(chip, "projected", 2)
        self.squashed = Flow(chip, "squashed")
        self.gated = Flow(chip, "gated", 2)

    def out_bank(self, u):
        return self.chip.bank(2 + u % 2).rearrange("p (g s c) -> p g s c", g=G, s=2)

    def load(self, sp, srcs, n, u):
        self.norm.turned.free(sp, n)
        for lo, src in srcs:
            sp.dma_start(self.stage[lo:lo + src.shape[0], u, :, :], src).then_inc(self.arrived[u], 16 * (2 // len(srcs)))

    def stats(self, dve, n, u):
        dve.wait_ge(self.arrived[u], 8 * n + (32 - 8 * u))
        self.norm.stats(dve, self.stage[:, u, :, :], n, u)

    def apply(self, dve, n, u):
        self.norm.apply(dve, self.stage[:, u, :, :], n, u)

    def keep(self, act, n, u):
        self.projected.free(act, n)
        self.norm.keep(act, n, u)

    def project(self, pe, n, u):
        self.norm.kept.ready(pe, n)
        self.gated.free(pe, n)
        out = self.chip.bank(2 + u % 2)
        pe.matmul(out.rearrange("p (g n) -> p g n", g=G), self.chip.ones3[:, :],
                  self.lin.bias3.unsqueeze(1).to_broadcast([3, G, 2 * C]), start=True, stop=False)
        for t in range(G):
            last = pe.matmul(out[:, t * P:(t + 1) * P], self.norm.zt[:, u % 2, t * P:(t + 1) * P], self.lin.w,
                             start=False, stop=t == G - 1)
        self.projected.done(last)

    def squash(self, act, dest, n, u):
        self.projected.ready(act, n)
        self.squashed.done(act.activation(dest, self.out_bank(u)[:, :, 0, :], ACT.Sigmoid))

    def gate(self, dve, dest, n, u):
        self.squashed.ready(dve, n)
        self.gated.done(dve.tensor_tensor(dest, dest, self.out_bank(u)[:, :, 1, :], ALU.mult))


def compound_sums(nc, chip, tag, par, raw_pairs):
    half = 0 if raw_pairs else 1
    carve = Carve(chip.work)
    ab2t = carve(C, P)
    cp = carve(NC_, C)
    with chip.phase(f"{tag}_compound"):
        if raw_pairs:
            cp_in = chip.sem("cp_in")
        else:
            (gate_w, _), (lin_w, lin_b) = par["gates"][0], par["lins"][0]
            stream = PairStream(chip, carve, Carve(chip.small), gate_w, lin_w, lin_b, par["ln_w"])
        groups = NC_ // G
        ab_turned = Flow(chip, "ab_turned")
        ab_kept = Flow(chip, "ab_kept", 2)
        summed = Flow(chip, "summed")
        stored = Flow(chip, "stored", 2)
        cpv = par["compound"][0]

        with nc.Block() as block:
            @block.sync
            def _(sp):
                if raw_pairs:
                    for h in range(2):
                        sp.dma_start(cp[h * NC_:(h + 1) * NC_, :, :], cpv.rearrange("j k c -> k j c")).then_inc(cp_in, 16)
                    return
                stream.lin.load(sp)

                def load(n, u):
                    src = cpv[bass.ds(n * G, G), :, :].rearrange("j k e -> k j e")
                    stream.load(sp, [(0, src), (NC_, src)], n, u)
                engine_loop(sp, groups, 4, [(load, 0)])

            @block.gpsimd
            def _(pool):
                if not raw_pairs:
                    stream.norm.open_pool(pool)
                    engine_loop(pool, groups, 4, [(lambda n, u: stream.norm.rstd(pool, n, u), 0)])

            @block.vector
            def _(dve):
                if not raw_pairs:
                    stream.gated.open(dve)
                    stream.lin.fold(dve)
                ab_kept.open(dve)

                def keep_ab(n):
                    ab_turned.ready(dve, n)
                    ab_kept.done(dve.tensor_copy(ab2t[:, 4 * n:4 * n + 4, :].rearrange("p c i -> p (c i)"),
                                                 chip.bank(4 + n % 2)))
                for n in range(C // 4):
                    keep_ab(n)
                if not raw_pairs:
                    def gate(n, u):
                        stream.gate(dve, cp[:, bass.ds(n * G, G), :], n, u)
                    engine_loop(dve, groups, 4, [(lambda n, u: stream.stats(dve, n, u), 0),
                                                 (lambda n, u: stream.apply(dve, n, u), 1), (gate, 3)])

            @block.scalar
            def _(act):
                stored.open(act)
                if not raw_pairs:
                    stream.norm.open_act(act)

                    def squash(n, u):
                        stream.squash(act, cp[:, bass.ds(n * G, G), :], n, u)
                    engine_loop(act, groups, 4, [(lambda n, u: stream.keep(act, n, u), 0), (squash, 1)])
                for ic in range(ICS):
                    for c8 in range(C // 8):
                        n = ic * (C // 8) + c8
                        summed.ready(act, n)
                        stored.done(act.copy(chip.ab[:, ic * NC_:(ic + 1) * NC_, 1, c8 * 8:(c8 + 1) * 8],
                                             chip.bank(6 + n % 2).rearrange("p (c j) -> p j c", c=8)))

            @block.tensor
            def _(pe):
                if not raw_pairs:
                    stream.norm.open_pe(pe)
                    stream.projected.open(pe)
                for n in range(C // 4):
                    ab_kept.free(pe, n)
                    for k in range(4):
                        last = pe.transpose(chip.banks[:, 4 + n % 2, k * P:(k + 1) * P],
                                            chip.ab[:, :, half, 4 * n + k], chip.ident[:, :])
                    ab_turned.done(last)
                if raw_pairs:
                    pe.wait_ge(cp_in, 32)
                else:
                    stream.lin.shift(pe)
                    stream.lin.await_ready(pe)
                    engine_loop(pe, groups, 4, [(lambda n, u: stream.norm.turn(pe, n, u), 0),
                                                (lambda n, u: stream.project(pe, n, u), 1)])
                    stream.gated.ready(pe, groups - 1)
                ab_kept.ready(pe, C // 4 - 1)
                for ic in range(ICS):
                    k = slice(ic * NC_, (ic + 1) * NC_)
                    for c8 in range(C // 8):
                        n = ic * (C // 8) + c8
                        stored.free(pe, n)
                        for cc in range(8):
                            c = c8 * 8 + cc
                            last = pe.matmul(chip.banks[:, 6 + n % 2, cc * NC_:(cc + 1) * NC_], ab2t[k, c, :],
                                             cp[k, :, c], start=True, stop=True)
                        summed.done(last)


ROWS = 16


def protein_sums(nc, chip, tag, par, raw_pairs):
    carve = Carve(chip.work)
    pp = carve(2, ICS, C, C)
    per_chunk = ICS * C // G
    ppv = par["protein"][0]
    with chip.phase(f"{tag}_protein"):
        if raw_pairs:
            pp_in = [chip.sem(f"pp_in{h}") for h in range(2)]
        else:
            (gate_w, _), (lin_w, lin_b) = par["gates"][1], par["lins"][1]
            small = Carve(chip.small)
            scratch = Carve(chip.work[:, ICS * C * C:2 * ICS * C * C])
            stream = PairStream(chip, small, small, gate_w, lin_w, lin_b, par["ln_w"], scratch=scratch)
        blocked = Flow(chip, "blocked", 16)
        summed = Flow(chip, "summed", 4)

        def where(m, u, h):
            kc = u % 2
            return kc, (m - kc) * 2

        with nc.Block() as block:
            @block.sync
            def _(sp):
                if not raw_pairs:
                    stream.lin.load(sp)
                with sp.Fori(0, ICS) as ic:
                    for h in range(2):
                        if raw_pairs:
                            blocked.free(sp, (ic * 2 + h) * 8 + 7)
                            for kc in range(ICS):
                                for i in range(0, C, ROWS):
                                    sp.dma_start(pp[:, h, kc, i:i + ROWS, :],
                                                 ppv[bass.ds(ic * P + (h * C + i), ROWS), kc * P:(kc + 1) * P, :]
                                                 .rearrange("i k c -> k i c")).then_inc(pp_in[h], 16)
                            continue

                        def load(m, u):
                            kc, i = where(m, u, h)
                            src = ppv[bass.ds(ic * P + (i + h * C), G), kc * P:(kc + 1) * P, :]
                            stream.load(sp, [(0, src.rearrange("i k e -> k i e"))], (ic * 2 + h) * per_chunk + m, u)
                        engine_loop(sp, per_chunk, 4, [(load, 0)])

            @block.gpsimd
            def _(pool):
                if not raw_pairs:
                    stream.norm.open_pool(pool)
                    engine_loop(pool, 4 * per_chunk, 4, [(lambda n, u: stream.norm.rstd(pool, n, u), 0)])

            @block.vector
            def _(dve):
                summed.open(dve)
                if not raw_pairs:
                    stream.gated.open(dve)
                    stream.lin.fold(dve)
                with dve.Fori(0, ICS) as ic:
                    for h in range(2):
                        if not raw_pairs:
                            base = (ic * 2 + h) * per_chunk

                            def gate(m, u):
                                kc, i = where(m, u, h)
                                stream.gate(dve, pp[:, h, kc, bass.ds(i, G), :], base + m, u)
                            engine_loop(dve, per_chunk, 4, [(lambda m, u: stream.stats(dve, base + m, u), 0),
                                                            (lambda m, u: stream.apply(dve, base + m, u), 1), (gate, 3)])
                        rows = slice(h * C, (h + 1) * C)
                        for c8 in range(C // 8):
                            n = (ic * 2 + h) * 8 + c8
                            sums = chip.ab[rows, bass.ds(ic * NC_, NC_), 1, c8 * 8:(c8 + 1) * 8]
                            blocked.ready(dve, n)
                            summed.done(dve.tensor_tensor(
                                sums, chip.banks[rows, 4 + c8 % 4, :].rearrange("p (c j) -> p j c", c=8), sums, ALU.add))

            @block.scalar
            def _(act):
                if raw_pairs:
                    return
                stream.norm.open_act(act)
                with act.Fori(0, ICS) as ic:
                    for h in range(2):
                        base = (ic * 2 + h) * per_chunk
                        blocked.free(act, (ic * 2 + h) * 8 + 7)

                        def squash(m, u):
                            kc, i = where(m, u, h)
                            stream.squash(act, pp[:, h, kc, bass.ds(i, G), :], base + m, u)
                        engine_loop(act, per_chunk, 4, [(lambda m, u: stream.keep(act, base + m, u), 0), (squash, 1)])

            @block.tensor
            def _(pe):
                blocked.open(pe)
                if not raw_pairs:
                    stream.norm.open_pe(pe)
                    stream.projected.open(pe)
                    stream.lin.shift(pe)
                    stream.lin.await_ready(pe)
                with pe.Fori(0, ICS) as ic:
                    for h in range(2):
                        if raw_pairs:
                            pe.wait_ge(pp_in[h], (ic + 1) * (16 * ICS * C // ROWS))
                        else:
                            base = (ic * 2 + h) * per_chunk
                            engine_loop(pe, per_chunk, 4, [(lambda m, u: stream.norm.turn(pe, base + m, u), 0),
                                                           (lambda m, u: stream.project(pe, base + m, u), 1)])
                            stream.gated.ready(pe, base + (per_chunk - 1))
                        for c8 in range(C // 8):
                            n = (ic * 2 + h) * 8 + c8
                            summed.free(pe, n)
                            for cc in range(8):
                                c = c8 * 8 + cc
                                for kc in range(ICS):
                                    last = pe.matmul(chip.banks[h * C:(h + 1) * C, 4 + c8 % 4, cc * NC_:(cc + 1) * NC_],
                                                     pp[:, h, kc, :, c], chip.ab[:, kc * NC_:(kc + 1) * NC_, 0, c],
                                                     start=kc == 0, stop=kc == ICS - 1)
                            blocked.done(last)


def combine(nc, chip, tag, par, src):
    small = Carve(chip.small)
    before = chip.work[:, :].rearrange("p (t e) -> p t e", e=E)
    with chip.phase(f"{tag}_combine"):
        norm = Norm(chip, small, (EPS_LN,), banks=(0, 1), width=C)
        lin = Linear(chip, small, "w", [par["out"][0]], [(par["out"][1], E)], par["lnc_w"], par["lnc_b"], bank=2, copies=2)
        x_in = [chip.sem(f"x_in{k}") for k in range(4)]
        projected = Flow(chip, "projected", 2)
        gated = Flow(chip, "gated", 2)
        added = Flow(chip, "added")

        def group(n):
            return chip.x[:, bass.ds(n * G, G), :]

        def sums(n):
            return chip.ab[:, bass.ds(n * G, G), 1, :]

        def halves(u):
            return chip.banks[:, 4 + 2 * (u % 2):6 + 2 * (u % 2), 0:2 * E]

        with nc.Block() as block:
            @block.sync
            def _(sp):
                lin.load(sp)
                load_tiles(sp, before, src, x_in)

            @block.gpsimd
            def _(pool):
                norm.open_pool(pool)

                def add(n, u):
                    await_tiles(pool, x_in, n, u)
                    pool.sem_inc(norm.paced, 1)
                    gated.ready(pool, n)
                    added.done(pool.tensor_tensor(group(n), group(n), before[:, bass.ds(n * G, G), :], ALU.add))
                engine_loop(pool, GROUPS, 4, [(lambda n, u: norm.rstd(pool, n, u % 2), 0), (add, 2)])

            @block.vector
            def _(dve):
                gated.open(dve)
                lin.fold(dve)

                def gate(n, u):
                    projected.ready(dve, n)
                    x = group(n).rearrange("p (k h) e -> p k h e", h=2)
                    gated.done(dve.tensor_tensor(x, halves(u).rearrange("p h (k e) -> p k h e", k=2), x, ALU.mult))
                engine_loop(dve, GROUPS, 2, [(lambda n, u: norm.stats(dve, sums(n), n, u), 0),
                                             (lambda n, u: norm.apply(dve, sums(n), n, u), 1), (gate, 3)])

            @block.scalar
            def _(act):
                norm.open_act(act)

                def keep(n, u):
                    projected.free(act, n)
                    norm.keep(act, n, u)
                engine_loop(act, GROUPS, 2, [(keep, 0)])

            @block.tensor
            def _(pe):
                norm.open_pe(pe)
                projected.open(pe)
                lin.shift(pe)
                lin.await_ready(pe)

                def project(n, u):
                    norm.kept.ready(pe, n)
                    gated.free(pe, n)
                    for h in range(2):
                        pe.matmul(halves(u)[:, h, :].rearrange("p (k n) -> p k n", k=2), chip.ones3[:, :],
                                  lin.bias3.unsqueeze(1).to_broadcast([3, 2, E]), start=True, stop=False)
                    for k in range(2):
                        for h in range(2):
                            c = slice(h * C, (h + 1) * C)
                            last = pe.matmul(halves(u)[:, h, k * P:(k + 1) * P], norm.zt[c, u % 2, k * P:(k + 1) * P],
                                             lin.w[c, :], start=False, stop=k == 1)
                    projected.done(last)
                engine_loop(pe, GROUPS, 2, [(lambda n, u: norm.turn(pe, n, u), 0), (project, 1)])


def mixture(nc, chip, p, keep_in):
    with chip.phase("moe"):
        carve = Carve(chip.ab[:, :, :, :].rearrange("p t s c -> p (t s c)"))
        w1 = carve(EXPERTS, HID)
        w2 = carve(EXPERTS * HC, E)
        hidden = carve(2, HC, G * P)
        work = Carve(chip.work)
        norm = Norm(chip, work, (EPS_LN, EPS_LN), banks=(6, 6), inverse=True)
        wr, br = work(EXPERTS), work(EXPERTS)
        b1 = work(EXPERTS * HC)
        total, rest = work(EXPERTS * E, parts=1), work(EXPERTS * E, parts=1)
        pieces = [work(EXPERTS * E, parts=1, dt=BF16) for _ in range(3)]
        b2 = work(EXPERTS, E, parts=3, dt=BF16)
        lane = work(EXPERTS)
        logits, top = work(G, EXPERTS), work(2, G, 8)
        which = work(G, 8, dt=U32)
        whichf = work(G, 2)
        lead, tanh = work(2, G), work(2, G)
        share = work(2, G)
        pick = work(2, G, EXPERTS)
        weight = work(2, G, EXPERTS)
        w_in, b_in = chip.sem("w_in"), chip.sem("b_in")
        shifted, folded, cut, spread, lanes = (chip.sem(s) for s in ("shifted", "folded", "cut", "spread", "lanes"))
        prep = Chain(chip, "prep")
        routed = Flow(chip, "routed", 1)
        led = Flow(chip, "led", 1)
        squashed = Flow(chip, "squashed")
        links = chip.sem("route_links")
        lifted = Flow(chip, "lifted", 2 * EXPERTS * HC)
        bent = Flow(chip, "bent", 4)
        lowered = Flow(chip, "lowered", 2)
        mixed = Flow(chip, "mixed", 2)
        stored = [chip.sem(f"stored{u}") for u in range(2)]

        def group(n):
            return chip.x[:, bass.ds(n * G, G), :]

        with nc.Block() as block:
            @block.sync
            def _(sp):
                sp.dma_start(w1, p["W1"].rearrange("e d h -> d e h")).then_inc(w_in, 16)
                for e in range(EXPERTS):
                    sp.dma_start(w2[:, e * HC:(e + 1) * HC, :],
                                 p["W2"][e].rearrange("(h p) d -> p h d", p=P)).then_inc(w_in, 16)
                sp.dma_start(wr, p["Wr"]).then_inc(w_in, 16)
                sp.dma_start(br, row(p["br"]).to_broadcast([P, EXPERTS])).then_inc(w_in, 16)
                sp.dma_start(total, p["b2"].rearrange("(a e) d -> a (e d)", a=1)).then_inc(b_in, 16)
                sp.wait_ge(cut, 1)
                for k in range(3):
                    sp.dma_start(b2[k:k + 1, :, :].rearrange("a e d -> a (e d)"), pieces[k]).then_inc(spread, 16)
                for ic in range(ICS):
                    with sp.Fori(0, GROUPS // ICS // 2) as i:
                        for u in range(2):
                            n = i * 2 + (u + ic * (GROUPS // ICS))
                            mixed.ready(sp, n * EXPERTS + (EXPERTS - 1))
                            sp.dma_start(keep_in[:, ic, bass.ds((i * 2 + u) * G, G), :], group(n)).then_inc(stored[u], 16)
                for u in range(2):
                    sp.wait_ge(stored[u], 16 * GROUPS // 2)

            @block.gpsimd
            def _(pool):
                pool.iota(lane, pattern=[[1, EXPERTS]], base=0, channel_multiplier=0,
                          allow_small_or_imprecise_dtypes=True).then_inc(lanes, 1)
                norm.open_pool(pool)
                engine_loop(pool, GROUPS, 2, [(lambda n, u: norm.rstd(pool, n, u), 0)])

            @block.vector
            def _(dve):
                led.open(dve)
                mixed.open(dve)
                chain = prep.on(dve)
                dve.wait_ge(w_in, 16 * (EXPERTS + 3))
                dve.wait_ge(shifted, 1)
                dve.tensor_tensor(b1, chip.banks[:, 0, 0:EXPERTS * HC],
                                  chip.cols[:, COL["moe_b1"]:COL["moe_b1"] + EXPERTS * HC], ALU.add).then_inc(folded, 1)
                for e in range(EXPERTS):
                    dve.tensor_scalar(w1[:, e, :], w1[:, e, :], col(chip, "moe_g", e), None, ALU.mult).then_inc(folded, 1)
                dve.wait_ge(b_in, 16)
                for k in range(3):
                    piece = dve.tensor_copy(pieces[k], total)
                    if k == 2:
                        piece.then_inc(cut, 1)
                    else:
                        chain(piece)
                        chain(dve.tensor_tensor(rest, total, pieces[k], ALU.subtract))
                        chain(dve.tensor_copy(total, rest))
                dve.wait_ge(lanes, 1)

                STEPS = 9

                def link(ins, n, k):
                    ins.then_inc(links, 1)
                    dve.wait_ge(links, n * STEPS + k)

                def lead_of(n, u):
                    routed.ready(dve, n)
                    link(dve.tensor_tensor(logits, chip.banks[:, 7, 0:G * EXPERTS].rearrange("p (g e) -> p g e", g=G),
                                           norm.inv[:, u, :].unsqueeze(2).to_broadcast([P, G, EXPERTS]), ALU.mult), n, 1)
                    link(dve.tensor_tensor(logits, logits, br.unsqueeze(1).to_broadcast([P, G, EXPERTS]), ALU.add), n, 2)
                    dve.sem_inc(norm.paced, 1)
                    for t in range(G):
                        last = dve.max(top[:, u, t, :], logits[:, t, :])
                    link(last, n, 3)
                    dve.sem_inc(norm.paced, 1)
                    for t in range(G):
                        last = dve.max_index(which[:, t, :], top[:, u, t, :], logits[:, t, :])
                    link(last, n, 4)
                    led.done(dve.tensor_tensor(lead[:, u, :], top[:, u, :, 0], top[:, u, :, 1], ALU.subtract))
                    link(dve.tensor_copy(whichf, which[:, :, 0:2]), n, 5)

                def weigh(n, u):
                    squashed.ready(dve, n)
                    for k, sign in enumerate((0.5, -0.5)):
                        last = dve.tensor_scalar(share[:, k, :], tanh[:, u, :], sign, 0.5, ALU.mult, ALU.add)
                    link(last, n, 6)
                    for k in range(2):
                        last = dve.tensor_tensor(pick[:, k, :, :], lane.unsqueeze(1).to_broadcast([P, G, EXPERTS]),
                                                 whichf[:, :, k].unsqueeze(2).to_broadcast([P, G, EXPERTS]), ALU.is_equal)
                    link(last, n, 7)
                    for k in range(2):
                        last = dve.tensor_tensor(pick[:, k, :, :], pick[:, k, :, :],
                                                 share[:, k, :].unsqueeze(2).to_broadcast([P, G, EXPERTS]), ALU.mult)
                    link(last, n, 8)
                    link(dve.tensor_tensor(weight[:, u, :, :], pick[:, 0, :, :], pick[:, 1, :, :], ALU.add), n, 9)

                def mix(n, u):
                    for e in range(EXPERTS):
                        lowered.ready(dve, n * EXPERTS + e)
                        for t in range(G):
                            if t == 0:
                                mixed.free(dve, n * EXPERTS + (e + 1))
                            tile = chip.x[:, bass.ds(n * G + t, 1), :].rearrange("p a e -> p (a e)")
                            last = dve.scalar_tensor_tensor(tile, chip.banks[:, 4 + e % 2, t * P:(t + 1) * P],
                                                            weight[:, u, t, e:e + 1], tile, ALU.mult, ALU.add)
                        mixed.done(last)

                engine_loop(dve, GROUPS, 2, [(lambda n, u: norm.stats(dve, group(n), n, u), 0),
                                             (lambda n, u: norm.apply(dve, group(n), n, u), 0),
                                             (mix, 2), (lead_of, 1), (weigh, 1)])

            @block.scalar
            def _(act):
                norm.open_act(act)
                bent.open(act)
                act.wait_ge(folded, 1 + EXPERTS)

                def keep(n, u):
                    lifted.free(act, n * (EXPERTS * HC) + (EXPERTS * HC - 1))
                    norm.keep(act, n, u)

                def bend(n, u):
                    for e in range(EXPERTS):
                        for h in range(HC):
                            k = n * (EXPERTS * HC) + (e * HC + h)
                            lifted.ready(act, k)
                            if h == 0:
                                lowered.free(act, n * EXPERTS + e)
                                act.sem_inc(norm.paced, 1)
                            bent.done(act.activation(hidden[:, e % 2, h, :], chip.bank(h), ACT.Gelu,
                                                     bias=b1[:, e * HC + h:e * HC + h + 1]))

                def squash(n, u):
                    led.ready(act, n)
                    squashed.done(act.activation(tanh[:, u, :], lead[:, u, :], ACT.Tanh, scale=0.5))

                engine_loop(act, GROUPS, 2, [(keep, 0), (bend, 1), (squash, 0)])

            @block.tensor
            def _(pe):
                norm.open_pe(pe)
                routed.open(pe)
                lifted.open(pe)
                lowered.open(pe)
                pe.wait_ge(w_in, 16 * (EXPERTS + 3))
                for e in range(EXPERTS):
                    for h in range(HC):
                        last = pe.matmul(chip.banks[:, 0, e * HC + h:e * HC + h + 1], w1[:, e, h * P:(h + 1) * P],
                                         col(chip, "moe_b", e), start=True, stop=True)
                last.then_inc(shifted, 1)
                pe.wait_ge(folded, 1 + EXPERTS)
                pe.wait_ge(spread, 48)

                def lift(n, u, e):
                    for h in range(HC):
                        k = n * (EXPERTS * HC) + (e * HC + h)
                        bent.free(pe, k)
                        lifted.done(pe.matmul(chip.bank(h), w1[:, e, h * P:(h + 1) * P], norm.zt[:, u, :],
                                              start=True, stop=True))

                def lower(n, u, e):
                    k = n * EXPERTS + e
                    mixed.free(pe, k)
                    out = chip.bank(4 + e % 2)
                    pe.matmul(out.rearrange("p (g n) -> p g n", g=G), chip.ones3[:, :],
                              b2[:, e, :].unsqueeze(1).to_broadcast([3, G, E]), start=True, stop=False)
                    for h in range(HC):
                        bent.ready(pe, n * (EXPERTS * HC) + (e * HC + h))
                        for t in range(G):
                            last = pe.matmul(out[:, t * P:(t + 1) * P], hidden[:, e % 2, h, t * P:(t + 1) * P],
                                             w2[:, e * HC + h, :], start=False, stop=h == HC - 1 and t == G - 1)
                    lowered.done(last)

                def route(n, u):
                    norm.kept.ready(pe, n)
                    led.free(pe, n)
                    for t in range(G):
                        last = pe.matmul(chip.banks[:, 7, t * EXPERTS:(t + 1) * EXPERTS],
                                         norm.zt[:, u, t * P:(t + 1) * P], wr, start=True, stop=True)
                    routed.done(last)

                def experts(first):
                    def stage(n, u):
                        for e in range(first, first + EXPERTS // 2):
                            if e == 0:
                                norm.kept.ready(pe, n)
                                lift(n, u, 0)
                            if e + 1 < EXPERTS:
                                lift(n, u, e + 1)
                            lower(n, u, e)
                    return stage

                engine_loop(pe, GROUPS, 2, [(lambda n, u: norm.turn(pe, n, u), 0), (experts(0), 1), (route, 0),
                                            (experts(EXPERTS // 2), 1)])


def turn_tokens(nc, chip):
    xt = chip.ab[:, :, :, :].rearrange("p t s c -> p t (s c)")
    with chip.phase("turn"):
        norm = Norm(chip, Carve(chip.small), (EPS_LN,), banks=(0, 1))

        def group(n):
            return chip.x[:, bass.ds(n * G, G), :]

        with nc.Block() as block:
            @block.gpsimd
            def _(pool):
                norm.open_pool(pool)
                engine_loop(pool, GROUPS, 2, [(lambda n, u: norm.rstd(pool, n, u), 0)])

            @block.vector
            def _(dve):
                engine_loop(dve, GROUPS, 2, [(lambda n, u: norm.stats(dve, group(n), n, u), 0),
                                             (lambda n, u: norm.apply(dve, group(n), n, u), 1)])

            @block.scalar
            def _(act):
                norm.open_act(act)

                def keep(n, u):
                    norm.keep(act, n, u, out=xt[:, bass.ds(n * G, G), :].rearrange("p g n -> p (g n)"))
                engine_loop(act, GROUPS, 2, [(keep, 0)])

            @block.tensor
            def _(pe):
                norm.open_pe(pe)
                engine_loop(pe, GROUPS, 2, [(lambda n, u: norm.turn(pe, n, u), 0)])


GATES = ("c", "i", "o")
UNROLL = 8
HALVES = 2
CHUNKS, STEPS = NP_, NC_


class Pass:

    def __init__(self, cell, tag, first, stores):
        self.cell, self.first, self.stores = cell, first, stores
        self.steps = STEPS - first
        chip = cell.chip
        self.summed = Flow(chip, f"{tag}_summed")
        self.read = Flow(chip, f"{tag}_read", 4)
        self.carried = Flow(chip, f"{tag}_carried")
        self.bounded = Flow(chip, f"{tag}_bounded")
        self.stepped = Flow(chip, f"{tag}_stepped")
        self.links = chip.sem(f"{tag}_links")
        self.saved = Flow(chip, f"{tag}_saved", 4)

    def each_step(self, eng, stage):
        with eng.Fori(self.first // UNROLL, STEPS // UNROLL) as i:
            for u in range(UNROLL):
                step = i * UNROLL + u
                stage(step - self.first if self.first else step, step, u % 2)

    def tensor(self, pe, base, base_h):
        cell, banks = self.cell, self.cell.chip.banks

        def bank(s, par, g):
            return banks[:, 4 + 2 * s + par, 0:P] if g == 0 else banks[:, 2 * s + par, (g - 1) * P:g * P]

        def prime(k, step, par, s):
            self.read.free(pe, base + (k * HALVES + s))
            for g, gate in enumerate(GATES):
                pe.matmul(bank(s, par, g), cell.bias3[:, g, :], cell.chip.ones3[:, :], start=g < 2, stop=False)
            for g, gate in enumerate(GATES):
                pe.matmul(bank(s, par, g), cell.u_w[gate], cell.xt[:, bass.ds(step + s * STEPS, 1), :]
                          .rearrange("p a n -> p (a n)"), start=False, stop=False)

        def finish(k, par, s):
            self.stepped.ready(pe, base_h + (k * HALVES + s))
            for g, gate in enumerate(GATES):
                last = pe.matmul(bank(s, par, g), cell.v_w[gate], cell.h[:, 1 - par, s, :], start=False, stop=g != 1)
                if g != 1:
                    self.summed.done(last)

        def body(i, last):
            for u in range(UNROLL):
                step = i * UNROLL + u
                k = step - self.first
                for s in range(HALVES):
                    finish(k, u % 2, s)
                    if not (last and u == UNROLL - 1):
                        prime(k + 1, step + 1, (u + 1) % 2, s)

        for s in range(HALVES):
            prime(0, self.first, 0, s)
        with pe.Fori(self.first // UNROLL, STEPS // UNROLL - 1) as i:
            body(i, False)
        body(STEPS // UNROLL - 1, True)

    def scalar(self, act, base):
        cell, banks = self.cell, self.cell.chip.banks

        def stage(k, step, par):
            for s in range(HALVES):
                n = base + (k * HALVES + s)
                self.summed.ready(act, n * 2)
                act.activation(cell.g[:, s, :], banks[:, 4 + 2 * s + par, 0:P], ACT.Tanh)
                self.summed.ready(act, n * 2 + 1)
                self.read.done(act.activation(cell.io[:, s, :, :].rearrange("p a n -> p (a n)"), banks[:, 2 * s + par, 0:2 * P],
                                              ACT.Sigmoid))
                self.carried.ready(act, n)
                self.bounded.done(act.activation(cell.g[:, s, :], cell.c[:, s, :], ACT.Tanh))
        self.each_step(act, stage)

    def vector(self, dve, base, base_h):
        cell = self.cell

        def stage(k, step, par):
            for s in range(HALVES):
                n, nh = base + (k * HALVES + s), base_h + (k * HALVES + s)
                i, o = cell.io[:, s, 0, :], cell.io[:, s, 1, :]
                self.stepped.ready(dve, nh)
                dve.tensor_tensor(cell.hc[:, s, :], cell.h[:, 1 - par, s, :], cell.c[:, s, :], ALU.mult
                                  ).then_inc(self.links, 1)
                dve.wait_ge(self.read.sem, n + 5)
                dve.tensor_tensor(cell.ig[:, s, :], i, cell.g[:, s, :], ALU.mult).then_inc(self.links, 1)
                dve.wait_ge(self.links, n * 2 + 2)
                self.carried.done(dve.tensor_tensor(cell.c[:, s, :], cell.hc[:, s, :], cell.ig[:, s, :], ALU.add))
                self.bounded.ready(dve, n)
                if self.stores:
                    self.saved.free(dve, n)
                    dve.sem_inc(cell.paced, 1)
                self.stepped.done(dve.tensor_tensor(cell.h[:, par, s, :], o, cell.g[:, s, :], ALU.mult))
        self.each_step(dve, stage)

    def gpsimd(self, pool, base, base_h):
        cell = self.cell
        if not self.stores:
            return

        def stage(k, step, par):
            for s in range(HALVES):
                self.stepped.ready(pool, base_h + (k * HALVES + (s + HALVES)))
                self.saved.done(pool.tensor_copy(cell.hs[:, bass.ds(step + s * STEPS, 1), :].rearrange("p a n -> p (a n)"),
                                                 cell.h[:, par, s, :]))
        self.each_step(pool, stage)

    def begin(self, dve, fresh, base_h):
        cell = self.cell
        if fresh:
            dve.memset(cell.start, 0.0).then_inc(cell.begun, 1)
            dve.wait_ge(cell.begun, 1)
        else:
            ends = self.ends()
            cell.chain(dve.tensor_copy(cell.start[:, 0, 1:CHUNKS], ends[0][:, 0:CHUNKS - 1]))
            cell.chain(dve.tensor_copy(cell.start[:, 1, 1:CHUNKS], ends[1][:, 0:CHUNKS - 1]))
        dve.tensor_copy(self.ends()[1], cell.start[:, 1, :])
        for s in range(HALVES):
            self.stepped.done(dve.tensor_copy(cell.h[:, 1, s, :], cell.start[:, 0, s * P:(s + 1) * P]))

    def ends(self):
        cell = self.cell
        return (cell.h[:, 1, :, :].rearrange("p s n -> p (s n)"), cell.c.rearrange("p s n -> p (s n)"))


class Links:

    def __init__(self, sem):
        self.sem, self.eng, self.base, self.n = sem, None, 0, 0

    def at(self, eng, base):
        self.eng, self.base, self.n = eng, base, 0

    def __call__(self, ins):
        self.n += 1
        ins.then_inc(self.sem, 1)
        self.eng.wait_ge(self.sem, self.base + self.n)


class Cell:

    def __init__(self, chip):
        self.chip = chip
        carve, scratch = Carve(chip.small), Carve(chip.work)
        self.u_w = {g: carve(P) for g in GATES}
        self.v_w = {g: carve(P) for g in GATES}
        self.bias3 = carve(3, P, parts=3, dt=BF16)
        self.start = carve(2, CHUNKS)
        self.h = carve(2, HALVES, P)
        self.c = carve(HALVES, P)
        self.io = carve(HALVES, 2, P)
        self.g = carve(HALVES, P)
        products = carve(2, HALVES, P)
        self.ig, self.hc = products[:, 0, :, :], products[:, 1, :, :]
        self.flag = carve(1, dt=I32)
        self.met, self.ones = carve(1), carve(1)
        self.total, self.rest = scratch(3 * P, parts=1), scratch(3 * P, parts=1)
        self.pieces = [scratch(3 * P, parts=1, dt=BF16) for _ in range(3)]
        self.xt = chip.ab[:, :, :, :].rearrange("p t s c -> p t (s c)")
        self.hs = chip.work[:, :].rearrange("p (t n) -> p t n", n=P)
        self.moved = self.io.rearrange("p s a n -> p (s a n)").rearrange("p (q n) -> p q n", q=2)[:, :, 0:CHUNKS - 1]
        self.size = products.rearrange("p a s n -> p a (s n)")[:, :, 0:CHUNKS - 1]
        self.paced, self.begun = chip.sem("paced"), chip.sem("begun")
        self.chain = Links(chip.sem("chain"))
        self.tested = chip.sem("tested")
        self.counted = chip.sem("counted")
        self.flagged = chip.sem("flagged")

    def compare(self, dve, run, turn):
        chain = self.chain
        ends = run.ends()
        for q in range(2):
            last = dve.tensor_tensor(self.moved[:, q, :], ends[q][:, 0:CHUNKS - 1], self.start[:, q, 1:CHUNKS],
                                     ALU.subtract)
        chain(last)
        for q in range(2):
            last = dve.tensor_tensor(self.size[:, q, :], ends[q][:, 0:CHUNKS - 1], ends[q][:, 0:CHUNKS - 1], ALU.mult)
        chain(last)
        chain(dve.tensor_tensor(self.moved, self.moved, self.moved, ALU.mult))
        chain(dve.tensor_scalar(self.size, self.size, 1.0, CHUNK_TOL ** 2, ALU.add, ALU.mult))
        chain(dve.tensor_tensor(self.moved, self.moved, self.size, ALU.is_le))
        dve.tensor_reduce(self.met, self.moved, AX.XY, ALU.min).then_inc(self.tested, 1)
        dve.wait_ge(self.counted, turn + 1)
        dve.tensor_copy(self.flag[0:1, :], self.chip.banks[0:1, 0, 0:1]).then_inc(self.flagged, 1)

    TEST_LINKS = 5

    def count(self, pe, turn):
        pe.wait_ge(self.tested, turn + 1)
        pe.matmul(self.chip.banks[0:1, 0, 0:1], self.met, self.ones, start=True, stop=True).then_inc(self.counted, 1)

    def flag_value(self, eng, turn):
        eng.wait_ge(self.flagged, turn + 1)
        eng.sem_inc(self.paced, 1)
        return eng.value_load(self.flag[0:1, 0:1], min_val=0, max_val=P)


def recur(nc, chip, p):
    with chip.phase("cell"):
        cell = Cell(chip)
        w_in, b_in, zeroed, cut, spread = (chip.sem(s) for s in ("w_in", "b_in", "zeroed", "cut", "spread"))
        prep = Chain(chip, "prep")
        warm = Pass(cell, "warm", STEPS - WARM, False)
        main = Pass(cell, "main", 0, True)
        more = Pass(cell, "more", 0, True)
        per, per_h = STEPS * HALVES, (STEPS + 1) * HALVES

        def rounds(eng, run, skipped=None):
            with eng.If(cell.flag_value(eng, 0) < P):
                with eng.Fori(0, CHUNKS - 2) as t:
                    with eng.If(cell.flag_value(eng, t) < P):
                        run(t)
                    with eng.Else():
                        if skipped is not None:
                            skipped()
                        else:
                            eng.sem_inc(cell.paced, 1)
                    eng.sem_inc(cell.paced, 1)
                eng.sem_inc(cell.paced, 1)

        with nc.Block() as block:
            @block.sync
            def _(sp):
                for gate in GATES:
                    sp.dma_start(cell.u_w[gate], p[f"U_{gate}"]).then_inc(w_in, 16)
                    sp.dma_start(cell.v_w[gate], p[f"V_{gate}"]).then_inc(w_in, 16)
                for g, gate in enumerate(GATES):
                    sp.dma_start(cell.total[:, g * P:(g + 1) * P], row(p[f"b_{gate}"])).then_inc(b_in, 16)
                sp.wait_ge(cut, 1)
                for k in range(3):
                    sp.dma_start(cell.bias3[k:k + 1, :, :].rearrange("a g n -> a (g n)"), cell.pieces[k]).then_inc(spread, 16)

            @block.gpsimd
            def _(pool):
                main.saved.open(pool)
                more.saved.open(pool)
                pool.wait_ge(spread, 48)
                main.gpsimd(pool, 0, 0)
                rounds(pool, lambda t: more.gpsimd(pool, t * per, t * per_h))

            @block.vector
            def _(dve):
                dve.memset(cell.ones, 1.0).then_inc(zeroed, 1)
                chain = prep.on(dve)
                dve.wait_ge(b_in, 48)
                for k in range(3):
                    piece = dve.tensor_copy(cell.pieces[k], cell.total)
                    if k == 2:
                        piece.then_inc(cut, 1)
                    else:
                        chain(piece)
                        chain(dve.tensor_tensor(cell.rest, cell.total, cell.pieces[k], ALU.subtract))
                        chain(dve.tensor_copy(cell.total, cell.rest))
                warm.begin(dve, True, 0)
                warm.vector(dve, 0, 0)
                cell.chain.at(dve, 0)
                warm.stepped.ready(dve, (WARM + 1) * HALVES - 1)
                main.begin(dve, False, 0)
                main.vector(dve, 0, 0)
                main.stepped.ready(dve, per_h - 1)
                cell.compare(dve, main, 0)
                main.saved.ready(dve, per - 1)

                def again(t):
                    cell.chain.at(dve, t * (2 + cell.TEST_LINKS) + (2 + cell.TEST_LINKS))
                    more.begin(dve, False, t * per_h)
                    more.vector(dve, t * per, t * per_h)
                    more.stepped.ready(dve, t * per_h + (per_h - 1))
                    cell.compare(dve, more, t + 1)
                    more.saved.ready(dve, t * per + (per - 1))
                    dve.sem_inc(cell.paced, 1)
                rounds(dve, again, skipped=lambda: dve.sem_inc(cell.flagged, 1))

            @block.scalar
            def _(act):
                for run in (warm, main, more):
                    run.read.open(act)
                warm.scalar(act, 0)
                main.scalar(act, 0)
                rounds(act, lambda t: more.scalar(act, t * per))

            @block.tensor
            def _(pe):
                pe.wait_ge(w_in, 96)
                pe.wait_ge(spread, 48)
                pe.wait_ge(zeroed, 1)
                warm.tensor(pe, 0, 0)
                main.tensor(pe, 0, 0)
                cell.count(pe, 0)

                def again(t):
                    more.tensor(pe, t * per, t * per_h)
                    cell.count(pe, t + 1)
                rounds(pe, again)


def finish(nc, chip, out):
    hs = chip.work[:, :].rearrange("p (t n) -> p t n", n=P)
    carve = Carve(chip.small)
    with chip.phase("finish"):
        flat = carve(2, G, P)
        copied = Flow(chip, "copied")
        turned = Flow(chip, "turned", 2)
        added = Flow(chip, "added", 2)
        stored = [chip.sem(f"stored{u}") for u in range(2)]

        def group(n):
            return chip.x[:, bass.ds(n * G, G), :]

        with nc.Block() as block:
            @block.sync
            def _(sp):
                for ic in range(ICS):
                    with sp.Fori(0, GROUPS // ICS // 2) as i:
                        for u in range(2):
                            n = i * 2 + (u + ic * (GROUPS // ICS))
                            added.ready(sp, n)
                            sp.dma_start(out[:, ic, bass.ds((i * 2 + u) * G, G), :], group(n)).then_inc(stored[u], 16)
                for u in range(2):
                    sp.wait_ge(stored[u], 16 * GROUPS // 2)

            @block.scalar
            def _(act):
                def copy(n, u):
                    turned.free(act, n)
                    copied.done(act.copy(flat[:, u, :, :], hs[:, bass.ds(n * G, G), :]))
                engine_loop(act, GROUPS, 2, [(copy, 0)])

            @block.tensor
            def _(pe):
                turned.open(pe)

                def turn(n, u):
                    copied.ready(pe, n)
                    added.free(pe, n)
                    for t in range(G):
                        last = pe.transpose(chip.banks[:, u, t * P:(t + 1) * P], flat[:, u, t, :], chip.ident[:, :])
                    turned.done(last)
                engine_loop(pe, GROUPS, 2, [(turn, 0)])

            @block.vector
            def _(dve):
                added.open(dve)

                def add(n, u):
                    turned.ready(dve, n)
                    added.done(dve.tensor_tensor(group(n), group(n), chip.bank(u).rearrange("p (g e) -> p g e", g=G), ALU.add))
                engine_loop(dve, GROUPS, 2, [(add, 0)])


def metaformer(nc, D, out):
    tokens = "(i p) j e -> p i j e"
    x0 = D["x"][0].rearrange(tokens, p=P)
    x1 = nc.dram_tensor("after_mixture", (NP_, NC_, E), F32).ap().rearrange(tokens, p=P)
    with ExitStack() as ctx:
        chip = Chip(nc, ctx)
        setup(nc, chip, setup_par(D))
        for layer, src in (("l0", x0), ("l1", x1)):
            par = conv_par(chip, D, layer)
            raw_pairs = layer == "l1"
            project_tokens(nc, chip, layer, par, src if layer == "l0" else None)
            compound_sums(nc, chip, layer, par, raw_pairs)
            protein_sums(nc, chip, layer, par, raw_pairs)
            combine(nc, chip, layer, par, src)
            if layer == "l0":
                chip.recycle()
                mixture(nc, chip, {k.removeprefix("L0_ffn_"): v for k, v in D.items() if k.startswith("L0_ffn_")}, x1)
        turn_tokens(nc, chip)
        recur(nc, chip, {k.removeprefix("L1_ffn_"): v for k, v in D.items() if k.startswith("L1_ffn_")})
        finish(nc, chip, out[0].rearrange(tokens, p=P))


def setup_par(D):
    return {"l0_ln_w": D["L0_conv_ln_w"], "l1_ln_w": D["L1_conv_ln_w"], "l1_ln_b": D["L1_conv_ln_b"],
            "l0_lnc_w": D["L0_conv_lnc_w"], "l1_lnc_w": D["L1_conv_lnc_w"], "l1_lnc_b": D["L1_conv_lnc_b"],
            "moe_ln_g": D["L0_ffn_ln_g"], "moe_ln_b": D["L0_ffn_ln_b"], "moe_b1": D["L0_ffn_b1"]}


def conv_par(chip, D, layer):
    if layer == "l0":
        q = {k.removeprefix("L0_conv_"): v for k, v in D.items() if k.startswith("L0_conv_")}
        return {"gates": [(q["gw1"], None), (q["gw2"], None)], "lins": [(q["w1"], q["b1"]), (q["w2"], q["b2"])],
                "edge": (q["we"], q["be"]), "out": (q["ws"], q["bs"]), "mask": q["z_mask"].rearrange("b i j c -> (b i) (j c)"),
                "ln_w": col(chip, "l0_ln_w"), "ln_b": None, "lnc_w": col(chip, "l0_lnc_w"), "lnc_b": None,
                "protein": q["protein_pair"], "compound": q["compound_pair"]}
    q = {k.removeprefix("L1_conv_"): v for k, v in D.items() if k.startswith("L1_conv_")}
    return {"gates": [(q["gate_w"], q["gate_b"])], "lins": [(q["lin_w"], q["lin_b"])],
            "edge": (q["eg_w"], q["eg_b"]), "out": (q["as_w"], q["as_b"]), "mask": q["z_mask"].rearrange("b i j c -> (b i) (j c)"),
            "ln_w": col(chip, "l1_ln_w"), "ln_b": col(chip, "l1_ln_b"),
            "lnc_w": col(chip, "l1_lnc_w"), "lnc_b": col(chip, "l1_lnc_b", hi=C),
            "protein": q["protein_pair"], "compound": q["compound_pair"]}


def kernel(**inputs):
    import numpy as np
    import concourse.bacc as bacc
    from concourse.bass_utils import run_bass_kernel_spmd

    nc = bacc.Bacc("TRN2", target_bir_lowering=False, num_devices=1)
    arrays, D = {}, {}
    for name, a in inputs.items():
        if name in ("L1_ffn_U_f", "L1_ffn_V_f", "L1_ffn_b_f"):
            continue
        arrays[name] = np.ascontiguousarray(a)
        D[name] = nc.dram_tensor(name, arrays[name].shape, F32, kind="ExternalInput").ap()
    out = nc.dram_tensor("out", (1, NP_, NC_, E), F32, kind="ExternalOutput").ap()
    metaformer(nc, D, out)
    return run_bass_kernel_spmd(nc, [arrays], core_ids=[0]).results[0]["out"]
```

```python
from contextlib import ExitStack

import concourse.bass as bass
from concourse import mybir

F32 = mybir.dt.float32
BF16 = mybir.dt.bfloat16
I32 = mybir.dt.int32
U32 = mybir.dt.uint32
ALU = mybir.AluOpType
ACT = mybir.ActivationFunctionType
AX = mybir.AxisListType

P = 128
NP_, NC_, E, C = 256, 64, 128, 64
TILES = NP_ * NC_ // P
G = 4
GROUPS = TILES // G
EXPERTS, HID = 8, 512
HC = HID // P
ICS = NP_ // P
EPS_LN = 1e-5
EPS_LNC = 1e-6
CHUNK_TOL = 2.0 ** -19
WARM = 64



def engine_loop(eng, total, unroll, stages, peel=0):
    lag = max(l for _, l in stages)
    head = min(total, -(-max(lag, peel) // unroll) * unroll)

    for t in range(head):
        for stage, l in stages:
            if t >= l:
                stage(t - l, (t - l) % unroll)
    if total > head:
        with eng.Fori(head // unroll, total // unroll) as i:
            for u in range(unroll):
                for stage, l in stages:
                    stage(i * unroll + (u - l), (u - l) % unroll)
    for t in range(total, total + lag):
        for stage, l in stages:
            if 0 <= t - l < total:
                stage(t - l, (t - l) % unroll)


class Flow:

    def __init__(self, chip, name, depth=0):
        self.sem, self.depth = chip.sem(name), depth

    def open(self, eng):
        eng.sem_inc(self.sem, self.depth)

    def done(self, ins):
        ins.then_inc(self.sem, 1)

    def ready(self, eng, n):
        eng.wait_ge(self.sem, n + (1 + self.depth))

    def free(self, eng, n):
        eng.wait_ge(self.sem, n + 1)


class Chain:

    def __init__(self, chip, name, eng=None):
        self.sem, self.n = chip.sem(name), 0

    def on(self, eng):
        self.eng = eng
        return self

    def __call__(self, ins):
        self.n += 1
        ins.then_inc(self.sem, 1)
        self.eng.wait_ge(self.sem, self.n)


class Chip:

    def __init__(self, nc, ctx):
        self.nc, self.ctx, self.sems = nc, ctx, []
        sb = self.sb
        self.x = sb("x_tiles", [P, TILES, E])
        self.ab = sb("ab_tiles", [P, TILES, 2, C])
        self.work = sb("work", [P, 2 * NC_ * P])
        self.ident = sb("ident", [P, P])
        self.cols = sb("cols", [P, 64])
        self.ones3 = sb("ones3", [3, P], BF16)
        self.small = sb("small", [P, 3740])
        self.banks = ctx.enter_context(nc.psum_tensor("banks", [P, 8, 512], F32))

    def sb(self, name, shape, dt=F32):
        return self.ctx.enter_context(self.nc.sbuf_tensor(name, shape, dt))

    def sem(self, name):
        self.sems.append(self.nc.alloc_semaphore(name=f"{self.tag}_{name}"))
        return self.sems[-1]

    def bank(self, b):
        return self.banks[:, b, :]

    def phase(self, tag):
        self.tag = tag
        return ExitStack()

    def recycle(self):
        self.nc.clear_and_free_semaphores(self.sems)
        self.nc.all_engine_barrier()
        self.sems = []


class Carve:

    def __init__(self, base):
        self.base, self.at = base, 0

    def __call__(self, *dims, parts=P, dt=F32):
        n = 1
        for d in dims:
            n *= d
        words = n if dt in (F32, I32, U32) else (n + 1) // 2
        ap = self.base[0:parts, self.at:self.at + words]
        self.at += words
        assert self.at <= self.base.shape[1], "region too small"
        if dt != F32:
            ap = ap.bitcast(dt)
        names = "abcd"[:len(dims)]
        if len(dims) > 1:
            ap = ap.rearrange(f"p ({' '.join(names)}) -> p {' '.join(names)}", **dict(zip(names, dims)))
        return ap


def row(v):
    return v.rearrange("(a n) -> a n", a=1)


COL = {"l0_ln_w": 0, "l1_ln_w": 1, "l1_ln_b": 2, "l0_lnc_w": 3, "l1_lnc_w": 4, "l1_lnc_b": 5,
       "moe_g": 8, "moe_b": 16, "moe_b1": 24}
N_COLS = 56


def setup(nc, chip, par):
    rows = chip.small[0:N_COLS, 0:P]
    one_row = {"l0_ln_w": par["l0_ln_w"], "l1_ln_w": par["l1_ln_w"], "l1_ln_b": par["l1_ln_b"]}
    half_row = {"l0_lnc_w": par["l0_lnc_w"], "l1_lnc_w": par["l1_lnc_w"], "l1_lnc_b": par["l1_lnc_b"]}
    n_dma = len(one_row) + 2 * len(half_row) + 3
    with chip.phase("setup"):
        rows_in, zeroed, ident_made, turned, ones_made = (
            chip.sem(n) for n in ("rows_in", "zeroed", "ident", "turned", "ones"))
        with nc.Block() as block:
            @block.sync
            def _(sp):
                sp.wait_ge(zeroed, 1)
                for k, v in one_row.items():
                    sp.dma_start(rows[COL[k]:COL[k] + 1, :], row(v)).then_inc(rows_in, 16)
                for k, v in half_row.items():
                    for h in range(2):
                        sp.dma_start(rows[COL[k]:COL[k] + 1, h * C:(h + 1) * C], row(v)).then_inc(rows_in, 16)
                for k, v in (("moe_g", par["moe_ln_g"]), ("moe_b", par["moe_ln_b"])):
                    sp.dma_start(rows[COL[k]:COL[k] + EXPERTS, :], v).then_inc(rows_in, 16)
                sp.dma_start(rows[COL["moe_b1"]:COL["moe_b1"] + EXPERTS * HC, :],
                             par["moe_b1"].rearrange("e (h p) -> (e h) p", p=P)).then_inc(rows_in, 16)

            @block.gpsimd
            def _(pool):
                pool.memset(chip.ident[:, :], 0.0).then_inc(ident_made, 1)
                pool.wait_ge(ident_made, 1)
                pool.affine_select(out=chip.ident[:, :], in_=chip.ident[:, :], compare_op=ALU.not_equal,
                                   fill=1.0, base=0, pattern=[[-1, P]], channel_multiplier=1
                                   ).then_inc(ident_made, 1)

            @block.vector
            def _(dve):
                dve.memset(rows, 0.0).then_inc(zeroed, 1)
                dve.memset(chip.ones3[:, :], 1.0).then_inc(ones_made, 1)
                dve.wait_ge(turned, 1)
                dve.tensor_copy(chip.cols[:, 0:N_COLS], chip.banks[:, 0, 0:N_COLS]).then_inc(ones_made, 1)

            @block.tensor
            def _(pe):
                pe.wait_ge(rows_in, 16 * n_dma)
                pe.wait_ge(ident_made, 2)
                pe.transpose(chip.banks[:, 0, 0:N_COLS], rows, chip.ident[0:N_COLS, 0:N_COLS]).then_inc(turned, 1)


def col(chip, name, k=0, lo=0, hi=P):
    c = COL[name] + k
    return chip.cols[lo:hi, c:c + 1]


class Linear:

    def __init__(self, chip, carve, tag, weights, biases, g, b, bank, copies=1, scratch=None):
        self.chip, self.weights, self.biases, self.g, self.b = chip, weights, biases, g, b
        self.n = n = sum(w.shape[1] for w in weights)
        self.k = weights[0].shape[0]
        self.copies = copies
        self.w = carve(n)
        self.bias3 = carve(n, parts=3, dt=BF16)
        scratch = carve if scratch is None else scratch
        self.raw = scratch(n)
        self.total, self.rest = scratch(n, parts=1), scratch(n, parts=1)
        self.pieces = [scratch(n, parts=1, dt=BF16) for _ in range(3)]
        self.product = chip.banks[0:1, bank, 0:n]
        self.zeroed, self.loaded, self.folded, self.shifted, self.cut, self.spread = (
            chip.sem(f"{tag}_{s}") for s in ("zeroed", "loaded", "folded", "shifted", "cut", "spread"))
        self.n_loads = len(weights) * copies + sum(x is not None for x, _ in biases)
        self.chain = Chain(chip, f"{tag}_chain")

    def load(self, sp):
        sp.wait_ge(self.zeroed, 1)
        at = 0
        for w in self.weights:
            for h in range(self.copies):
                sp.dma_start(self.raw[h * self.k:(h + 1) * self.k, at:at + w.shape[1]], w).then_inc(self.loaded, 16)
            at += w.shape[1]
        at = 0
        for v, n in self.biases:
            if v is not None:
                sp.dma_start(self.total[0:1, at:at + n], row(v)).then_inc(self.loaded, 16)
            at += n
        sp.wait_ge(self.cut, 1)
        for k in range(3):
            sp.dma_start(self.bias3[k:k + 1, :], self.pieces[k]).then_inc(self.spread, 16)

    def fold(self, dve):
        chain = self.chain.on(dve)
        dve.memset(self.total, 0.0).then_inc(self.zeroed, 1)
        dve.wait_ge(self.loaded, 16 * self.n_loads)
        rows = self.k * self.copies
        dve.tensor_scalar(self.w[0:rows, :], self.raw[0:rows, :], self.g, None, ALU.mult).then_inc(self.folded, 1)
        if self.b is not None:
            dve.wait_ge(self.shifted, 1)
            chain(dve.tensor_tensor(self.total, self.total, self.product, ALU.add))
        for k in range(3):
            piece = dve.tensor_copy(self.pieces[k], self.total)
            if k == 2:
                piece.then_inc(self.cut, 1)
            else:
                chain(piece)
                chain(dve.tensor_tensor(self.rest, self.total, self.pieces[k], ALU.subtract))
                chain(dve.tensor_copy(self.total, self.rest))

    def shift(self, pe):
        if self.b is not None:
            pe.wait_ge(self.loaded, 16 * self.n_loads)
            pe.matmul(self.product, self.b, self.raw[0:self.k, :], start=True, stop=True).then_inc(self.shifted, 1)

    def await_ready(self, pe):
        pe.wait_ge(self.folded, 1)
        pe.wait_ge(self.spread, 48)


class Norm:

    def __init__(self, chip, carve, eps, banks, depth=2, zn=None, width=E, by_act=0):
        self.by_act = by_act
        self.chip, self.banks, self.depth = chip, banks, depth
        self.affine = (1.0, eps[0]) if len(eps) == 1 else (1.0 + eps[1], eps[0] * eps[1])
        self.width = width
        self.st = carve(depth, G, 6)
        self.mv = carve(depth, G, 2)
        self.r = carve(depth, G)
        self.var, self.shift = carve(depth, G), carve(depth, G)
        self.shifted, self.applied_act = Flow(chip, "norm_shifted"), Flow(chip, "applied_act", depth)
        self.mhalf = carve(G)
        self.zn = carve(depth, G, width) if zn is None else zn
        self.zt = carve(2, G * P)
        self.stat, self.scaled = Flow(chip, "stat"), Flow(chip, "scaled")
        self.agg = Flow(chip, "agg")
        self.half, self.links, self.paced = chip.sem("half"), chip.sem("links"), chip.sem("paced")
        self.applied = Flow(chip, "applied")
        self.turned = Flow(chip, "turned", depth)
        self.kept = Flow(chip, "kept", len(set(banks)))

    def open_pool(self, pool):
        pool.memset(self.mhalf, -0.5).then_inc(self.half, 1)
        pool.wait_ge(self.half, 1)

    def open_pe(self, pe):
        self.turned.open(pe)

    def open_act(self, act):
        self.kept.open(act)
        if self.by_act:
            self.applied_act.open(act)

    def stats(self, dve, src, n, u):
        for t in range(G):
            last = dve.bn_stats(self.st[:, u, t, :], src[:, t, :])
        self.stat.done(last)
        self.stat.ready(dve, n)
        dve.sem_inc(self.paced, 1)
        for t in range(G):
            last = dve.bn_aggr(self.mv[:, u, t, :], self.st[:, u, t, :])
        last.then_inc(self.links, 1)
        dve.wait_ge(self.links, n + 1)
        self.agg.done(dve.tensor_scalar(self.var[:, u, :], self.mv[:, u, :, 1], self.affine[0], self.affine[1],
                                        ALU.mult, ALU.add))

    def rstd(self, pool, n, u):
        if self.by_act:
            self.applied_act.free(pool, n)
        self.agg.ready(pool, n)
        self.scaled.done(pool.tensor_tensor(self.r[:, u, :], self.var[:, u, :], self.mhalf, ALU.pow))

    def apply(self, dve, src, n, u):
        self.scaled.ready(dve, n)
        if self.by_act:
            self.shifted.done(dve.scalar_tensor_tensor(self.shift[:, u, :], self.mv[:, u, :, 0], -1.0,
                                                       self.r[:, u, :], ALU.mult, ALU.mult))
        self.turned.free(dve, n)
        for t in range(G - self.by_act):
            last = dve.tensor_scalar(self.zn[:, u, t, :], src[:, t, :], self.mv[:, u, t, 0:1],
                                     self.r[:, u, t:t + 1], ALU.subtract, ALU.mult)
        self.applied.done(last)

    def apply_act(self, act, src, n, u):
        self.shifted.ready(act, n)
        self.turned.free(act, n)
        for t in range(G - self.by_act, G):
            last = act.activation(self.zn[:, u, t, :], src[:, t, :], ACT.Identity, bias=self.shift[:, u, t:t + 1],
                                  scale=self.r[:, u, t:t + 1])
        self.applied_act.done(last)

    def turn(self, pe, n, u):
        self.applied.ready(pe, n)
        if self.by_act:
            self.applied_act.ready(pe, n)
        self.kept.free(pe, n)
        w = self.width
        for k in range(G * w // P):
            src = self.zn[:, u, :, :].rearrange("p g e -> p (g e)")[:, k * P:(k + 1) * P]
            last = pe.transpose(self.chip.banks[:, self.banks[u % 2], k * P:(k + 1) * P], src, self.chip.ident[:, :])
        self.turned.done(last)

    def keep(self, act, n, u, out=None):
        self.turned.ready(act, n)
        cols = G * self.width
        if out is None:
            out = self.zt[:, u % 2, 0:cols]
        self.kept.done(act.copy(out, self.chip.banks[:, self.banks[u % 2], 0:cols]))


def load_tiles(sp, dst, src, arrived):
    for ic in range(ICS):
        for n in range(4):
            if ic:
                sp.wait_ge(arrived[n], 64)
            sp.dma_start(dst[:, (ic * 16 + n) * G:(ic * 16 + n + 1) * G, :],
                         src[:, ic, n * G:(n + 1) * G, :]).then_inc(arrived[n], 16)
        with sp.Fori(1, 4) as i:
            for u in range(4):
                sp.wait_ge(arrived[u], 16 * i + 64 * ic)
                sp.dma_start(dst[:, bass.ds((i * 4 + (u + ic * 16)) * G, G), :],
                             src[:, ic, bass.ds((i * 4 + u) * G, G), :]).then_inc(arrived[u], 16)


def await_tiles(eng, arrived, n, u):
    eng.wait_ge(arrived[u], 4 * n + (16 - 4 * u))


def project_tokens(nc, chip, tag, par, src, choices=None, keep_in=None):
    gates, lins, (edge, edge_b) = par["gates"], par["lins"], par["edge"]
    NG, NL = C * len(gates), C * len(lins)
    NS = NG + E
    carve = Carve(chip.work)
    xf = chip.x
    with chip.phase(f"{tag}_project"):
        lin = Linear(chip, carve, "w", [w for w, _ in gates] + [edge] + [w for w, _ in lins],
                     [(b, C) for _, b in gates] + [(edge_b, E)] + [(b, C) for _, b in lins],
                     par["ln_w"], par["ln_b"], bank=2)
        norm = Norm(chip, carve, (EPS_LNC, EPS_LN), banks=(0, 1), depth=2)
        sg = carve(2, 2, NS)
        mask = carve(TILES)
        mask_in = chip.sem("mask_in")
        if choices is not None:
            pair = carve(4, G, 2, E)
            pair_in = [chip.sem(f"pair_in{k}") for k in range(4)]
            stored = [chip.sem(f"stored{k}") for k in range(4)]
            merged = Flow(chip, "merged", 4)
            links = chip.sem("merge_links")
        x_in = [chip.sem(f"x_in{k}") for k in range(4)]
        projected = Flow(chip, "projected", 4)
        squashed = Flow(chip, "squashed")
        gated = Flow(chip, "gated", 2)
        masked = Flow(chip, "masked", 2)

        def tiles(n, k=0, m=G):
            return xf[:, bass.ds(n * G + k, m), :]

        with nc.Block() as block:
            @block.sync
            def _(sp):
                sp.dma_start(mask.rearrange("p (i j) -> p i j", i=ICS),
                             par["mask"].rearrange("(i p) j -> p i j", p=P)).then_inc(mask_in, 16)
                lin.load(sp)
                if src is not None:
                    load_tiles(sp, xf, src, x_in)
                    return

                def load(n, u):
                    merged.free(sp, n)
                    sp.dma_start(pair[:, u, :, :, :], choices[:, bass.ds(n * G, G), :, :]).then_inc(pair_in[u], 16)

                def store(n, u):
                    merged.ready(sp, n)
                    sp.dma_start(keep_in[:, bass.ds(n * G, G), :], tiles(n)).then_inc(stored[u], 16)
                engine_loop(sp, GROUPS, 4, [(load, 0), (store, 3)])
                for u in range(4):
                    sp.wait_ge(stored[u], 16 * GROUPS // 4)

            @block.vector
            def _(dve):
                gated.open(dve)
                if choices is not None:
                    merged.open(dve)
                lin.fold(dve)
                dve.wait_ge(mask_in, 16)

                def stats(n, u):
                    if src is not None:
                        await_tiles(dve, x_in, n, u)
                    else:
                        await_tiles(dve, pair_in, n, u)
                        dve.tensor_tensor(pair[:, u, :, 0, :], pair[:, u, :, 0, :], pair[:, u, :, 1, :],
                                          ALU.add).then_inc(links, 1)
                        dve.wait_ge(links, n + 1)
                        merged.done(dve.tensor_tensor(tiles(n), tiles(n), pair[:, u, :, 0, :], ALU.add))
                        merged.ready(dve, n)
                        dve.sem_inc(norm.paced, 1)
                    norm.stats(dve, tiles(n), n, u % 2)

                def apply(n, u):
                    norm.apply(dve, tiles(n), n, u % 2)

                def gate(n, u):
                    for h in range(2):
                        pair = n * 2 + h
                        projected.ready(dve, pair)
                        squashed.ready(dve, pair)
                        for t in range(2):
                            tile = n * G + (2 * h + t)
                            last = dve.scalar_tensor_tensor(
                                chip.ab[:, bass.ds(tile, 1), 0:NL // C, :].rearrange("p a b c -> p (a b c)"),
                                sg[:, h, t, 0:NG], mask[:, bass.ds(tile, 1)],
                                chip.banks[:, 4 + 2 * h + t, NS:NS + NL], ALU.mult, ALU.mult)
                        gated.done(last)

                engine_loop(dve, GROUPS, 4, [(stats, 0), (apply, 1), (gate, 3)])

            @block.gpsimd
            def _(pool):
                norm.open_pool(pool)
                masked.open(pool)
                pool.wait_ge(mask_in, 16)

                def edge_mask(n, u):
                    if choices is not None:
                        await_tiles(pool, stored, n, u)
                        pool.sem_inc(norm.paced, 1)
                    for h in range(2):
                        pair = n * 2 + h
                        squashed.ready(pool, pair)
                        masked.done(pool.tensor_tensor(
                            tiles(n, 2 * h, 2), sg[:, h, :, NG:NS],
                            mask[:, bass.ds(n * G + 2 * h, 2)].unsqueeze(2).to_broadcast([P, 2, E]), ALU.mult))

                engine_loop(pool, GROUPS, 4, [(lambda n, u: norm.rstd(pool, n, u % 2), 0), (edge_mask, 2)])

            @block.scalar
            def _(act):
                norm.open_act(act)

                def squash(n, u):
                    for h in range(2):
                        pair = n * 2 + h
                        projected.ready(act, pair)
                        masked.free(act, pair)
                        gated.free(act, pair)
                        squashed.done(act.activation(sg[:, h, :, :], chip.banks[:, 4 + 2 * h:6 + 2 * h, 0:NS],
                                                     ACT.Sigmoid))

                def keep(n, u):
                    projected.free(act, n * 2 + 1)
                    norm.keep(act, n, u)

                engine_loop(act, GROUPS, 2, [(keep, 0), (squash, 1)])

            @block.tensor
            def _(pe):
                norm.open_pe(pe)
                projected.open(pe)
                lin.shift(pe)
                lin.await_ready(pe)

                def project(n, u):
                    norm.kept.ready(pe, n)
                    for h in range(2):
                        pair = n * 2 + h
                        gated.free(pe, pair)
                        for t in range(2):
                            out = chip.banks[:, 4 + 2 * h + t, 0:lin.n]
                            k = (2 * h + t) * P
                            pe.matmul(out, chip.ones3[:, :], lin.bias3, start=True, stop=False)
                            last = pe.matmul(out, norm.zt[:, u, k:k + P], lin.w, start=False, stop=True)
                        projected.done(last)

                engine_loop(pe, GROUPS, 2, [(lambda n, u: norm.turn(pe, n, u), 0), (project, 1)])


class PairStream:

    def __init__(self, chip, carve, carve_lin, gate_w, lin_w, lin_b, g, b=None, scratch=None):
        self.chip = chip
        self.stage = carve(4, G, E)
        self.norm = Norm(chip, carve, (EPS_LN,), banks=(0, 1), depth=4, zn=self.stage, by_act=2)
        self.lin = Linear(chip, carve_lin, "w", [gate_w, lin_w], [(None, C), (lin_b, C)], g, b, bank=2,
                          scratch=scratch)
        self.arrived = [chip.sem(f"arrived{u}") for u in range(4)]
        self.projected = Flow(chip, "projected", 2)
        self.squashed = Flow(chip, "squashed")
        self.gated = Flow(chip, "gated", 2)

    def out_bank(self, u):
        return self.chip.bank(2 + u % 2).rearrange("p (g s c) -> p g s c", g=G, s=2)

    def load(self, sp, srcs, n, u):
        self.norm.turned.free(sp, n)
        for lo, src in srcs:
            sp.dma_start(self.stage[lo:lo + src.shape[0], u, :, :], src).then_inc(self.arrived[u], 16 * (2 // len(srcs)))

    def stats(self, dve, n, u):
        dve.wait_ge(self.arrived[u], 8 * n + (32 - 8 * u))
        self.norm.stats(dve, self.stage[:, u, :, :], n, u)

    def apply(self, dve, n, u):
        self.norm.apply(dve, self.stage[:, u, :, :], n, u)

    def apply_act(self, act, n, u):
        self.norm.apply_act(act, self.stage[:, u, :, :], n, u)

    def keep(self, act, n, u):
        self.projected.free(act, n)
        self.norm.keep(act, n, u)

    def project(self, pe, n, u):
        self.norm.kept.ready(pe, n)
        self.gated.free(pe, n)
        out = self.chip.bank(2 + u % 2)
        pe.matmul(out.rearrange("p (g n) -> p g n", g=G), self.chip.ones3[:, :],
                  self.lin.bias3.unsqueeze(1).to_broadcast([3, G, 2 * C]), start=True, stop=False)
        for t in range(G):
            last = pe.matmul(out[:, t * P:(t + 1) * P], self.norm.zt[:, u % 2, t * P:(t + 1) * P], self.lin.w,
                             start=False, stop=t == G - 1)
        self.projected.done(last)

    def squash(self, act, dest, n, u):
        self.projected.ready(act, n)
        self.squashed.done(act.activation(dest, self.out_bank(u)[:, :, 0, :], ACT.Sigmoid))

    def gate(self, dve, dest, n, u):
        self.squashed.ready(dve, n)
        self.gated.done(dve.tensor_tensor(dest, dest, self.out_bank(u)[:, :, 1, :], ALU.mult))


def compound_sums(nc, chip, tag, par, raw_pairs):
    half = 0 if raw_pairs else 1
    carve = Carve(chip.work)
    ab2t = carve(C, P)
    cp = carve(NC_, C)
    with chip.phase(f"{tag}_compound"):
        if raw_pairs:
            cp_in = chip.sem("cp_in")
        else:
            (gate_w, _), (lin_w, lin_b) = par["gates"][0], par["lins"][0]
            stream = PairStream(chip, carve, Carve(chip.small), gate_w, lin_w, lin_b, par["ln_w"])
        groups = NC_ // G
        ab_turned = Flow(chip, "ab_turned")
        ab_kept = Flow(chip, "ab_kept", 2)
        summed = Flow(chip, "summed")
        stored = Flow(chip, "stored", 2)
        cpv = par["compound"][0]

        with nc.Block() as block:
            @block.sync
            def _(sp):
                if raw_pairs:
                    for h in range(2):
                        sp.dma_start(cp[h * NC_:(h + 1) * NC_, :, :], cpv.rearrange("j k c -> k j c")).then_inc(cp_in, 16)
                    return
                stream.lin.load(sp)

                def load(n, u):
                    src = cpv[bass.ds(n * G, G), :, :].rearrange("j k e -> k j e")
                    stream.load(sp, [(0, src), (NC_, src)], n, u)
                engine_loop(sp, groups, 4, [(load, 0)])

            @block.gpsimd
            def _(pool):
                if not raw_pairs:
                    stream.norm.open_pool(pool)
                    engine_loop(pool, groups, 4, [(lambda n, u: stream.norm.rstd(pool, n, u), 0)])

            @block.vector
            def _(dve):
                if not raw_pairs:
                    stream.gated.open(dve)
                    stream.lin.fold(dve)
                ab_kept.open(dve)

                def keep_ab(n):
                    ab_turned.ready(dve, n)
                    ab_kept.done(dve.tensor_copy(ab2t[:, 4 * n:4 * n + 4, :].rearrange("p c i -> p (c i)"),
                                                 chip.bank(4 + n % 2)))
                for n in range(C // 4):
                    keep_ab(n)
                if not raw_pairs:
                    def gate(n, u):
                        stream.gate(dve, cp[:, bass.ds(n * G, G), :], n, u)
                    engine_loop(dve, groups, 4, [(lambda n, u: stream.stats(dve, n, u), 0),
                                                 (lambda n, u: stream.apply(dve, n, u), 1), (gate, 4)])

            @block.scalar
            def _(act):
                stored.open(act)
                if not raw_pairs:
                    stream.norm.open_act(act)

                    def squash(n, u):
                        stream.squash(act, cp[:, bass.ds(n * G, G), :], n, u)
                    engine_loop(act, groups, 4, [(lambda n, u: stream.apply_act(act, n, u), 0),
                                                 (lambda n, u: stream.keep(act, n, u), 1), (squash, 2)])
                for ic in range(ICS):
                    for c8 in range(C // 8):
                        n = ic * (C // 8) + c8
                        summed.ready(act, n)
                        stored.done(act.copy(chip.ab[:, ic * NC_:(ic + 1) * NC_, 1, c8 * 8:(c8 + 1) * 8],
                                             chip.bank(6 + n % 2).rearrange("p (c j) -> p j c", c=8)))

            @block.tensor
            def _(pe):
                if not raw_pairs:
                    stream.norm.open_pe(pe)
                    stream.projected.open(pe)
                for n in range(C // 4):
                    ab_kept.free(pe, n)
                    for k in range(4):
                        last = pe.transpose(chip.banks[:, 4 + n % 2, k * P:(k + 1) * P],
                                            chip.ab[:, :, half, 4 * n + k], chip.ident[:, :])
                    ab_turned.done(last)
                if raw_pairs:
                    pe.wait_ge(cp_in, 32)
                else:
                    stream.lin.shift(pe)
                    stream.lin.await_ready(pe)
                    engine_loop(pe, groups, 4, [(lambda n, u: stream.norm.turn(pe, n, u), 0),
                                                (lambda n, u: stream.project(pe, n, u), 1)])
                    stream.gated.ready(pe, groups - 1)
                ab_kept.ready(pe, C // 4 - 1)
                for ic in range(ICS):
                    k = slice(ic * NC_, (ic + 1) * NC_)
                    for c8 in range(C // 8):
                        n = ic * (C // 8) + c8
                        stored.free(pe, n)
                        for cc in range(8):
                            c = c8 * 8 + cc
                            last = pe.matmul(chip.banks[:, 6 + n % 2, cc * NC_:(cc + 1) * NC_], ab2t[k, c, :],
                                             cp[k, :, c], start=True, stop=True)
                        summed.done(last)


ROWS = 16


def protein_sums(nc, chip, tag, par, raw_pairs):
    carve = Carve(chip.work)
    pp = carve(2, ICS, C, C)
    per_chunk = ICS * C // G
    ppv = par["protein"][0]
    with chip.phase(f"{tag}_protein"):
        if raw_pairs:
            pp_in = [chip.sem(f"pp_in{h}") for h in range(2)]
        else:
            (gate_w, _), (lin_w, lin_b) = par["gates"][1], par["lins"][1]
            small = Carve(chip.small)
            scratch = Carve(chip.work[:, ICS * C * C:2 * ICS * C * C])
            stream = PairStream(chip, small, small, gate_w, lin_w, lin_b, par["ln_w"], scratch=scratch)
        blocked = Flow(chip, "blocked", 16)
        summed = Flow(chip, "summed", 4)

        def where(m, u, h):
            kc = u % 2
            return kc, (m - kc) * 2

        with nc.Block() as block:
            @block.sync
            def _(sp):
                if not raw_pairs:
                    stream.lin.load(sp)
                with sp.Fori(0, ICS) as ic:
                    for h in range(2):
                        if raw_pairs:
                            blocked.free(sp, (ic * 2 + h) * 8 + 7)
                            for kc in range(ICS):
                                for i in range(0, C, ROWS):
                                    sp.dma_start(pp[:, h, kc, i:i + ROWS, :],
                                                 ppv[bass.ds(ic * P + (h * C + i), ROWS), kc * P:(kc + 1) * P, :]
                                                 .rearrange("i k c -> k i c")).then_inc(pp_in[h], 16)
                            continue

                        def load(m, u):
                            kc, i = where(m, u, h)
                            src = ppv[bass.ds(ic * P + (i + h * C), G), kc * P:(kc + 1) * P, :]
                            stream.load(sp, [(0, src.rearrange("i k e -> k i e"))], (ic * 2 + h) * per_chunk + m, u)
                        engine_loop(sp, per_chunk, 4, [(load, 0)])

            @block.gpsimd
            def _(pool):
                if not raw_pairs:
                    stream.norm.open_pool(pool)
                    engine_loop(pool, 4 * per_chunk, 4, [(lambda n, u: stream.norm.rstd(pool, n, u), 0)])

            @block.vector
            def _(dve):
                summed.open(dve)
                if not raw_pairs:
                    stream.gated.open(dve)
                    stream.lin.fold(dve)
                with dve.Fori(0, ICS) as ic:
                    for h in range(2):
                        if not raw_pairs:
                            base = (ic * 2 + h) * per_chunk

                            def gate(m, u):
                                kc, i = where(m, u, h)
                                stream.gate(dve, pp[:, h, kc, bass.ds(i, G), :], base + m, u)
                            engine_loop(dve, per_chunk, 4, [(lambda m, u: stream.stats(dve, base + m, u), 0),
                                                            (lambda m, u: stream.apply(dve, base + m, u), 1), (gate, 4)])
                        rows = slice(h * C, (h + 1) * C)
                        for c8 in range(C // 8):
                            n = (ic * 2 + h) * 8 + c8
                            sums = chip.ab[rows, bass.ds(ic * NC_, NC_), 1, c8 * 8:(c8 + 1) * 8]
                            blocked.ready(dve, n)
                            summed.done(dve.tensor_tensor(
                                sums, chip.banks[rows, 4 + c8 % 4, :].rearrange("p (c j) -> p j c", c=8), sums, ALU.add))

            @block.scalar
            def _(act):
                if raw_pairs:
                    return
                stream.norm.open_act(act)
                with act.Fori(0, ICS) as ic:
                    for h in range(2):
                        base = (ic * 2 + h) * per_chunk
                        blocked.free(act, (ic * 2 + h) * 8 + 7)

                        def squash(m, u):
                            kc, i = where(m, u, h)
                            stream.squash(act, pp[:, h, kc, bass.ds(i, G), :], base + m, u)
                        engine_loop(act, per_chunk, 4, [(lambda m, u: stream.apply_act(act, base + m, u), 0),
                                                        (lambda m, u: stream.keep(act, base + m, u), 1), (squash, 2)])

            @block.tensor
            def _(pe):
                blocked.open(pe)
                if not raw_pairs:
                    stream.norm.open_pe(pe)
                    stream.projected.open(pe)
                    stream.lin.shift(pe)
                    stream.lin.await_ready(pe)
                with pe.Fori(0, ICS) as ic:
                    for h in range(2):
                        if raw_pairs:
                            pe.wait_ge(pp_in[h], (ic + 1) * (16 * ICS * C // ROWS))
                        else:
                            base = (ic * 2 + h) * per_chunk
                            engine_loop(pe, per_chunk, 4, [(lambda m, u: stream.norm.turn(pe, base + m, u), 0),
                                                           (lambda m, u: stream.project(pe, base + m, u), 1)])
                            stream.gated.ready(pe, base + (per_chunk - 1))
                        for c8 in range(C // 8):
                            n = (ic * 2 + h) * 8 + c8
                            summed.free(pe, n)
                            for cc in range(8):
                                c = c8 * 8 + cc
                                for kc in range(ICS):
                                    last = pe.matmul(chip.banks[h * C:(h + 1) * C, 4 + c8 % 4, cc * NC_:(cc + 1) * NC_],
                                                     pp[:, h, kc, :, c], chip.ab[:, kc * NC_:(kc + 1) * NC_, 0, c],
                                                     start=kc == 0, stop=kc == ICS - 1)
                            blocked.done(last)


def combine(nc, chip, tag, par, src):
    small = Carve(chip.small)
    before = chip.work[:, :].rearrange("p (t e) -> p t e", e=E)
    with chip.phase(f"{tag}_combine"):
        norm = Norm(chip, small, (EPS_LN,), banks=(0, 1), width=C)
        lin = Linear(chip, small, "w", [par["out"][0]], [(par["out"][1], E)], par["lnc_w"], par["lnc_b"], bank=2, copies=2)
        x_in = [chip.sem(f"x_in{k}") for k in range(4)]
        projected = Flow(chip, "projected", 2)
        gated = Flow(chip, "gated", 2)
        added = Flow(chip, "added")

        def group(n):
            return chip.x[:, bass.ds(n * G, G), :]

        def sums(n):
            return chip.ab[:, bass.ds(n * G, G), 1, :]

        def halves(u):
            return chip.banks[:, 4 + 2 * (u % 2):6 + 2 * (u % 2), 0:2 * E]

        with nc.Block() as block:
            @block.sync
            def _(sp):
                lin.load(sp)
                load_tiles(sp, before, src, x_in)

            @block.gpsimd
            def _(pool):
                norm.open_pool(pool)

                def add(n, u):
                    await_tiles(pool, x_in, n, u)
                    pool.sem_inc(norm.paced, 1)
                    gated.ready(pool, n)
                    added.done(pool.tensor_tensor(group(n), group(n), before[:, bass.ds(n * G, G), :], ALU.add))
                engine_loop(pool, GROUPS, 4, [(lambda n, u: norm.rstd(pool, n, u % 2), 0), (add, 4)])

            @block.vector
            def _(dve):
                gated.open(dve)
                lin.fold(dve)

                def gate(n, u):
                    projected.ready(dve, n)
                    x = group(n).rearrange("p (k h) e -> p k h e", h=2)
                    gated.done(dve.tensor_tensor(x, halves(u).rearrange("p h (k e) -> p k h e", k=2), x, ALU.mult))
                engine_loop(dve, GROUPS, 2, [(lambda n, u: norm.stats(dve, sums(n), n, u), 0),
                                             (lambda n, u: norm.apply(dve, sums(n), n, u), 1), (gate, 3)])

            @block.scalar
            def _(act):
                norm.open_act(act)

                def keep(n, u):
                    projected.free(act, n)
                    norm.keep(act, n, u)
                engine_loop(act, GROUPS, 2, [(keep, 0)])

            @block.tensor
            def _(pe):
                norm.open_pe(pe)
                projected.open(pe)
                lin.shift(pe)
                lin.await_ready(pe)

                def project(n, u):
                    norm.kept.ready(pe, n)
                    gated.free(pe, n)
                    for h in range(2):
                        pe.matmul(halves(u)[:, h, :].rearrange("p (k n) -> p k n", k=2), chip.ones3[:, :],
                                  lin.bias3.unsqueeze(1).to_broadcast([3, 2, E]), start=True, stop=False)
                    for k in range(2):
                        for h in range(2):
                            c = slice(h * C, (h + 1) * C)
                            last = pe.matmul(halves(u)[:, h, k * P:(k + 1) * P], norm.zt[c, u % 2, k * P:(k + 1) * P],
                                             lin.w[c, :], start=False, stop=k == 1)
                    projected.done(last)
                engine_loop(pe, GROUPS, 2, [(lambda n, u: norm.turn(pe, n, u), 0), (project, 1)])


SLOT = G * P
SLOTS = 2 * NP_ * NC_ // SLOT + EXPERTS
TAIL = 2
ROW = E + TAIL
PACK = HID + HC * E + HC + E // 2
NOWHERE = 1 << 20


class Mixture:

    def __init__(self, nc, chip, p):
        self.nc, self.chip, self.p = nc, chip, p
        self.sorted = nc.dram_tensor("sorted_tokens", (SLOTS * SLOT, ROW), F32).ap()
        self.out = nc.dram_tensor("choices", (NP_ * NC_ * 2, E), F32).ap()
        ab = Carve(chip.ab[:, :, :, :].rearrange("p t s c -> p (t s c)"))
        self.pack = ab(EXPERTS, PACK)
        self.ab_rest = chip.ab[:, :, :, :].rearrange("p t s c -> p (t s c)")[:, ab.at:]
        work = Carve(chip.work)
        self.mean, self.scale = work(TILES), work(TILES)
        self.tail = work(TILES, 2, TAIL)
        self.place = work(TILES, 2, dt=U32)
        self.expert = work(SLOTS, dt=I32)
        self.work_rest = chip.work[:, work.at:]
        self.logits = self.work_rest[:, 0:TILES * EXPERTS].rearrange("p (t e) -> p t e", e=EXPERTS)

    def w1(self, e):
        return self.pack[:, e, 0:HID]

    def w2(self, e):
        return self.pack[:, e, HID:HID + HC * E]

    def b1(self, e):
        return self.pack[:, e, HID + HC * E:HID + HC * E + HC]

    def b2(self, e):
        return self.pack[0:3, e, HID + HC * E + HC:PACK].bitcast(BF16)

    def group(self, n):
        return self.chip.x[:, bass.ds(n * G, G), :]

    def route(self):
        nc, chip, p = self.nc, self.chip, self.p
        with chip.phase("route"):
            work = Carve(self.work_rest[:, TILES * EXPERTS:])
            norm = Norm(chip, work, (EPS_LN,), banks=(5, 6), depth=4, by_act=2)
            wr, br = work(EXPERTS), work(EXPERTS)
            total, rest = work(EXPERTS * E, parts=1), work(EXPERTS * E, parts=1)
            pieces = [work(EXPERTS * E, parts=1, dt=BF16) for _ in range(3)]
            empty = work(SLOTS // 6, ROW)
            r_in, w_in, b_in = chip.sem("r_in"), chip.sem("w_in"), chip.sem("b_in")
            shifted, folded, cut, spread = (chip.sem(s) for s in ("shifted", "folded", "cut", "spread"))
            emptied, cleared = chip.sem("emptied"), chip.sem("cleared")
            prep = Chain(chip, "prep")
            routed = Flow(chip, "routed", 2)
            scored = Flow(chip, "scored", 2)
            kept_scales = Flow(chip, "kept_scales")
            scales = Flow(chip, "scales")
            mhalf, mhalf_made = work(G), chip.sem("mhalf")
            rows = SLOTS * SLOT // P // 24

            with nc.Block() as block:
                @block.sync
                def _(sp):
                    sp.dma_start(wr, p["Wr"]).then_inc(r_in, 16)
                    sp.dma_start(br, row(p["br"]).to_broadcast([P, EXPERTS])).then_inc(r_in, 16)
                    for e in range(EXPERTS):
                        sp.dma_start(self.w1(e), p["W1"][e]).then_inc(w_in, 16)
                        sp.dma_start(self.w2(e).rearrange("p (h d) -> p h d", d=E),
                                     p["W2"][e].rearrange("(h p) d -> p h d", p=P)).then_inc(w_in, 16)
                    sp.dma_start(total, p["b2"].rearrange("(a e) d -> a (e d)", a=1)).then_inc(b_in, 16)
                    sp.wait_ge(emptied, 2)
                    for k in range(24):
                        sp.dma_start(self.sorted.rearrange("(k p n) w -> k p n w", p=P, k=24)[k],
                                     empty[:, 0:rows, :]).then_inc(cleared, 16)
                    sp.wait_ge(cut, 1)
                    for e in range(EXPERTS):
                        for k in range(3):
                            sp.dma_start(self.b2(e)[k:k + 1, :], pieces[k][:, e * E:(e + 1) * E]).then_inc(spread, 16)
                    sp.wait_ge(cleared, 16 * 24)
                    sp.wait_ge(spread, 16 * 3 * EXPERTS)

                @block.gpsimd
                def _(pool):
                    norm.open_pool(pool)
                    pool.wait_ge(r_in, 32)

                    pool.memset(mhalf, -0.5).then_inc(mhalf_made, 1)
                    pool.wait_ge(mhalf_made, 1)

                    def both(n, u):
                        kept_scales.ready(pool, n)
                        scales.done(pool.tensor_tensor(self.scale[:, bass.ds(n * G, G)],
                                                       self.scale[:, bass.ds(n * G, G)], mhalf, ALU.pow))
                    engine_loop(pool, GROUPS, 4, [(lambda n, u: norm.rstd(pool, n, u), 0), (both, 2)])

                @block.vector
                def _(dve):
                    dve.memset(empty, 0.0).then_inc(emptied, 1)
                    dve.memset(self.pack[:, :, HID + HC * E + HC:PACK], 0.0)
                    dve.wait_ge(emptied, 1)
                    dve.memset(empty[:, :, E + 1:ROW].bitcast(U32), NOWHERE).then_inc(emptied, 1)
                    scored.open(dve)
                    dve.wait_ge(r_in, 32)

                    def keep_scales(n, u):
                        dve.tensor_copy(self.mean[:, bass.ds(n * G, G)], norm.mv[:, u, :, 0])
                        kept_scales.done(dve.tensor_scalar(self.scale[:, bass.ds(n * G, G)], norm.mv[:, u, :, 1],
                                                           1.0 + EPS_LN, EPS_LN * EPS_LN, ALU.mult, ALU.add))

                    def score(n, u):
                        routed.ready(dve, n)
                        scored.done(dve.tensor_tensor(
                            self.logits[:, bass.ds(n * G, G), :],
                            chip.banks[:, 3 + u % 2, 0:G * EXPERTS].rearrange("p (g e) -> p g e", g=G),
                            br.unsqueeze(1).to_broadcast([P, G, EXPERTS]), ALU.add))

                    engine_loop(dve, GROUPS, 4, [(lambda n, u: norm.stats(dve, self.group(n), n, u), 0),
                                                 (lambda n, u: norm.apply(dve, self.group(n), n, u), 1),
                                                 (keep_scales, 1), (score, 3)])
                    chain = prep.on(dve)
                    dve.wait_ge(w_in, 32 * EXPERTS)
                    dve.wait_ge(shifted, 1)
                    dve.tensor_tensor(self.pack[:, :, HID + HC * E:HID + HC * E + HC],
                                      chip.banks[:, 0, 0:EXPERTS * HC].rearrange("p (e h) -> p e h", e=EXPERTS),
                                      chip.cols[:, COL["moe_b1"]:COL["moe_b1"] + EXPERTS * HC]
                                      .rearrange("p (e h) -> p e h", e=EXPERTS), ALU.add)
                    for e in range(EXPERTS):
                        dve.tensor_scalar(self.w1(e), self.w1(e), col(chip, "moe_g", e), None, ALU.mult)
                    dve.wait_ge(b_in, 16)
                    for k in range(3):
                        piece = dve.tensor_copy(pieces[k], total)
                        if k == 2:
                            piece.then_inc(cut, 1)
                        else:
                            chain(piece)
                            chain(dve.tensor_tensor(rest, total, pieces[k], ALU.subtract))
                            chain(dve.tensor_copy(total, rest))

                @block.scalar
                def _(act):
                    norm.open_act(act)

                    def keep(n, u):
                        routed.free(act, n)
                        norm.keep(act, n, u)
                    engine_loop(act, GROUPS, 4, [(lambda n, u: norm.apply_act(act, self.group(n), n, u), 0), (keep, 1)])

                @block.tensor
                def _(pe):
                    norm.open_pe(pe)
                    pe.wait_ge(r_in, 32)

                    def logit(n, u):
                        norm.kept.ready(pe, n)
                        scored.free(pe, n)
                        for t in range(G):
                            last = pe.matmul(chip.banks[:, 3 + u % 2, t * EXPERTS:(t + 1) * EXPERTS],
                                             norm.zt[:, u % 2, t * P:(t + 1) * P], wr, start=True, stop=True)
                        routed.done(last)
                    routed.open(pe)
                    engine_loop(pe, GROUPS, 4, [(lambda n, u: norm.turn(pe, n, u), 0), (logit, 1)])
                    pe.wait_ge(w_in, 32 * EXPERTS)
                    for e in range(EXPERTS):
                        for h in range(HC):
                            last = pe.matmul(chip.banks[:, 0, e * HC + h:e * HC + h + 1],
                                             self.w1(e)[:, h * P:(h + 1) * P],
                                             col(chip, "moe_b", e), start=True, stop=True)
                    last.then_inc(shifted, 1)

    def choose(self):
        nc, chip = self.nc, self.chip
        T = TILES
        with chip.phase("choose"):
            work = Carve(self.work_rest)
            logits = work(T, EXPERTS)
            same, rest, at = work(T, EXPERTS), work(T, EXPERTS), work(T, EXPERTS)
            pick = [work(T, EXPERTS) for _ in range(2)]
            best = [work(T) for _ in range(2)]
            which, lead, share = work(T), work(T), work(T)
            chosen = work(T, EXPERTS, dt=BF16)
            before_f, before, ones = work(P), work(P, dt=BF16), work(P, dt=BF16)
            lane8 = work(EXPERTS)
            steps = work(NP_ * NC_ // SLOT)
            slot_no = work(SLOTS)
            place_out = work(T, 2)
            sofar = work(EXPERTS, T)
            fills = work(EXPERTS, NP_ * NC_ // SLOT)
            slots, ends, base = work(EXPERTS), work(EXPERTS), work(EXPERTS)
            done = work(SLOTS, EXPERTS)
            zeros = work(T)
            expert = work(SLOTS)
            made, led, bounded, counted, picked = (chip.sem(s) for s in ("made", "led", "bounded", "counted", "picked"))
            chain = Chain(chip, "chain")

            def by_token(v):
                return v.unsqueeze(2).to_broadcast([P, T, EXPERTS])

            def by_expert(v):
                return v.unsqueeze(1).to_broadcast([P, T, EXPERTS])

            with nc.Block() as block:
                @block.gpsimd
                def _(pool):
                    def iota(out, pattern, base, step):
                        pool.iota(out, pattern=pattern, base=base, channel_multiplier=step,
                                  allow_small_or_imprecise_dtypes=True)
                    iota(lane8, [[1, EXPERTS]], -EXPERTS, 0)
                    iota(steps, [[SLOT, NP_ * NC_ // SLOT]], 0, 0)
                    iota(slot_no, [[1, SLOTS]], 0, 0)
                    iota(place_out, [[2, T], [1, 2]], 0, 2 * T)
                    pool.memset(before_f, 1.0).then_inc(made, 1)
                    pool.wait_ge(made, 1)
                    pool.affine_select(out=before_f, in_=before_f, compare_op=ALU.is_gt, fill=0.0, base=0,
                                       pattern=[[1, P]], channel_multiplier=-1).then_inc(made, 1)

                @block.vector
                def _(dve):
                    c = chain.on(dve)
                    dve.memset(ones, 1.0)
                    dve.memset(zeros, 0.0)
                    dve.wait_ge(made, 2)
                    c(dve.tensor_copy(before, before_f))
                    src = logits
                    for k in range(2):
                        c(dve.tensor_reduce(best[k], src, AX.X, ALU.max))
                        c(dve.tensor_tensor(same, src, by_token(best[k]), ALU.is_equal))
                        c(dve.tensor_tensor(same, same, by_expert(lane8), ALU.mult))
                        c(dve.tensor_reduce(which, same, AX.X, ALU.min))
                        c(dve.tensor_tensor(pick[k], by_expert(lane8), by_token(which), ALU.is_equal))
                        if k == 0:
                            c(dve.scalar_tensor_tensor(rest, pick[k], -1e30, logits, ALU.mult, ALU.add))
                            src = rest
                    dve.tensor_tensor(chosen, pick[0], pick[1], ALU.add).then_inc(picked, 1)
                    dve.tensor_tensor(lead, best[0], best[1], ALU.subtract).then_inc(led, 1)
                    dve.wait_ge(counted, 1)
                    for h in range(2):
                        part = slice(h * T // 2, (h + 1) * T // 2)
                        counts = chip.banks[:, 2 + h, :].rearrange("p (t e) -> p t e", e=EXPERTS)
                        c(dve.tensor_copy(same[:, part, :], counts))
                        c(dve.tensor_tensor(at[:, part, :], chip.banks[:, h, :].rearrange("p (t e) -> p t e", e=EXPERTS),
                                            same[:, part, :], ALU.subtract))
                    for e in range(EXPERTS):
                        last = dve.tensor_tensor_scan(sofar[:, e, :], same[:, :, e], zeros, 0.0, ALU.add, ALU.add)
                    c(last)
                    c(dve.tensor_tensor(fills, sofar[:, :, T - 1:T].to_broadcast([P, EXPERTS, NP_ * NC_ // SLOT]),
                                        steps.unsqueeze(1).to_broadcast([P, EXPERTS, NP_ * NC_ // SLOT]), ALU.is_gt))
                    c(dve.tensor_reduce(slots, fills, AX.X, ALU.add))
                    c(dve.tensor_tensor_scan(ends, slots, zeros[:, 0:EXPERTS], 0.0, ALU.add, ALU.add))
                    c(dve.tensor_tensor(base, ends, slots, ALU.subtract))
                    c(dve.tensor_scalar(base, base, float(SLOT), None, ALU.mult))
                    c(dve.tensor_tensor(done, slot_no.unsqueeze(2).to_broadcast([P, SLOTS, EXPERTS]),
                                        ends.unsqueeze(1).to_broadcast([P, SLOTS, EXPERTS]), ALU.is_ge))
                    c(dve.tensor_reduce(expert, done, AX.X, ALU.add))
                    c(dve.tensor_scalar(expert, expert, float(EXPERTS - 1), None, ALU.min))
                    dve.tensor_copy(self.expert, expert)
                    c(dve.tensor_tensor(at, at, sofar.rearrange("p e t -> p t e"), ALU.add))
                    c(dve.tensor_tensor(at, at, by_expert(base), ALU.add))
                    for k in range(2):
                        c(dve.tensor_tensor(same, at, pick[k], ALU.mult))
                        c(dve.tensor_reduce(which, same, AX.X, ALU.add))
                        dve.tensor_copy(self.place[:, :, k], which)
                        dve.tensor_copy(self.tail[:, :, k, 1].bitcast(U32), place_out[:, :, k])
                    dve.wait_ge(bounded, 1)
                    for k, sign in enumerate((0.5, -0.5)):
                        dve.tensor_scalar(self.tail[:, :, k, 0], share, sign, 0.5, ALU.mult, ALU.add)

                @block.scalar
                def _(act):
                    act.wait_ge(led, 1)
                    act.activation(share, lead, ACT.Tanh, scale=0.5).then_inc(bounded, 1)

                @block.tensor
                def _(pe):
                    pe.wait_ge(picked, 1)
                    flat = chosen.rearrange("p t e -> p (t e)")
                    for m, w in enumerate((before, ones)):
                        for h in range(2):
                            last = pe.matmul(chip.bank(2 * m + h), w, flat[:, h * 512:(h + 1) * 512], start=True, stop=True)
                    last.then_inc(counted, 1)

    def dispatch(self):
        nc, chip = self.nc, self.chip
        with chip.phase("dispatch"):
            work = Carve(self.work_rest)
            rows = work(2, G, 2, ROW)
            where = work(2, G, 2, dt=U32)
            built = Flow(chip, "built")
            paced, paced_pool = chip.sem("paced"), chip.sem("paced_pool")
            sent = [chip.sem(f"sent{u}") for u in range(2)]

            with nc.Block() as block:
                @block.vector
                def _(dve):
                    def build(n, u):
                        if not isinstance(n, int) or n >= 2:
                            dve.wait_ge(sent[u], (n - u) * (2 * G * 16 // 2))
                            dve.sem_inc(paced, 1)
                        dve.tensor_copy(where[:, u, :, :], self.place[:, bass.ds(n * G, G), :])
                        dve.tensor_copy(rows[:, u, :, :, E:ROW], self.tail[:, bass.ds(n * G, G), :, :])
                        for t in range(G):
                            tile = n * G + t
                            last = dve.tensor_scalar(rows[:, u, t, :, 0:E],
                                                     chip.x[:, bass.ds(tile, 1), :].to_broadcast([P, 2, E]),
                                                     self.mean[:, bass.ds(tile, 1)], self.scale[:, bass.ds(tile, 1)],
                                                     ALU.subtract, ALU.mult)
                        built.done(last)
                    engine_loop(dve, GROUPS, 2, [(build, 0)], peel=2)

                @block.gpsimd
                def _(pool):
                    def send(n, u):
                        built.ready(pool, n)
                        pool.sem_inc(paced_pool, 1)
                        for t in range(G):
                            for k in range(2):
                                pool.indirect_dma_start(
                                    out=self.sorted,
                                    out_offset=bass.IndirectOffsetOnAxis(ap=where[:, u, t, k:k + 1], axis=0),
                                    in_=rows[:, u, t, k, :], in_offset=None).then_inc(sent[u], 16)
                    engine_loop(pool, GROUPS, 2, [(send, 0)])
                    for u in range(2):
                        pool.wait_ge(sent[u], 16 * 8 * GROUPS // 2)

    def experts(self):
        nc, chip = self.nc, self.chip
        with chip.phase("experts"):
            ab, work = Carve(self.ab_rest), Carve(self.work_rest)
            rows = ab(8, G, ROW)
            hidden = work(2, HC, G * P)
            w = work(4, PACK)
            zt = work(2, G * P)
            y = work(4, G, P)
            now = work(2, dt=I32)
            rows_in = [chip.sem(f"rows_in{u}") for u in range(8)]
            sent = [chip.sem(f"sent{u}") for u in range(4)]
            named = Flow(chip, "named")
            paced, paced_act, paced_pool = (chip.sem(f"paced_{k}") for k in ("vector", "scalar", "gpsimd"))
            weighed = Flow(chip, "weighed")
            turned = Flow(chip, "turned")
            kept = Flow(chip, "kept", 2)
            lifted = Flow(chip, "lifted", 2 * HC)
            bent = Flow(chip, "bent", HC)
            lowered = Flow(chip, "lowered", 4)
            mixed = Flow(chip, "mixed", 2)

            with nc.Block() as block:
                @block.sync
                def _(sp):
                    def load(s, u):
                        if not isinstance(s, int) or s >= 8:
                            sp.wait_ge(sent[u % 4], (s - (4 + u % 4)) * (G * 16 // 4))
                        sp.dma_start(rows[:, u, :, :], self.sorted[bass.ds(s * SLOT, SLOT), :]
                                     .rearrange("(g p) w -> p g w", p=P)).then_inc(rows_in[u], 16)
                    engine_loop(sp, SLOTS, 8, [(load, 0)], peel=8)

                @block.vector
                def _(dve):
                    mixed.open(dve)

                    def weights(s, u):
                        named.done(dve.tensor_copy(now[0:1, u % 2:u % 2 + 1], self.expert[0:1, bass.ds(s, 1)]))
                        named.ready(dve, s)
                        dve.sem_inc(paced, 1)
                        e = dve.value_load(now[0:1, u % 2:u % 2 + 1], min_val=0, max_val=EXPERTS - 1)
                        lowered.free(dve, s)
                        weighed.done(dve.tensor_copy(w[:, u % 4, :],
                                                     self.pack[:, bass.ds(e, 1), :].rearrange("p a n -> p (a n)")))

                    def mix(s, u):
                        if not isinstance(s, int) or s >= 4:
                            dve.wait_ge(sent[u % 4], (s - u % 4) * (G * 16 // 4))
                            dve.sem_inc(paced, 1)
                        lowered.ready(dve, s)
                        for t in range(G):
                            last = dve.tensor_scalar(y[:, u % 4, t, :], chip.banks[:, 4 + u % 2, t * P:(t + 1) * P],
                                                     rows[:, u, t, E:E + 1], None, ALU.mult)
                        mixed.done(last)
                    engine_loop(dve, SLOTS, 8, [(weights, 0), (mix, 2)])

                @block.gpsimd
                def _(pool):
                    def send(s, u):
                        mixed.ready(pool, s)
                        pool.sem_inc(paced_pool, 1)
                        for t in range(G):
                            pool.indirect_dma_start(
                                out=self.out,
                                out_offset=bass.IndirectOffsetOnAxis(ap=rows[:, u, t, E + 1:ROW].bitcast(U32), axis=0),
                                in_=y[:, u % 4, t, :], in_offset=None, bounds_check=2 * NP_ * NC_ - 1,
                                oob_is_err=False).then_inc(sent[u % 4], 16)
                    engine_loop(pool, SLOTS, 8, [(send, 0)])
                    for u in range(4):
                        pool.wait_ge(sent[u], G * 16 * SLOTS // 4)

                @block.scalar
                def _(act):
                    kept.open(act)
                    bent.open(act)

                    def keep(s, u):
                        lifted.free(act, s * HC + (HC - 1))
                        turned.ready(act, s)
                        kept.done(act.copy(zt[:, u % 2, :], chip.bank(6 + u % 2)))

                    def bend(s, u):
                        b1 = w[:, u % 4, HID + HC * E:HID + HC * E + HC]
                        act.wait_ge(lowered.sem, s + 3)
                        act.sem_inc(paced_act, 1)
                        for h in range(HC):
                            lifted.ready(act, s * HC + h)
                            bent.done(act.activation(hidden[:, u % 2, h, :], chip.bank(h), ACT.Gelu,
                                                     bias=b1[:, h:h + 1]))
                    engine_loop(act, SLOTS, 8, [(keep, 0), (bend, 1)])

                @block.tensor
                def _(pe):
                    lowered.open(pe)
                    lifted.open(pe)

                    def turn(s, u):
                        pe.wait_ge(rows_in[u], s * 2 + (16 - 2 * u))
                        kept.free(pe, s)
                        for t in range(G):
                            last = pe.transpose(chip.banks[:, 6 + u % 2, t * P:(t + 1) * P], rows[:, u, t, 0:E], chip.ident[:, :])
                        turned.done(last)

                    def lift(s, u):
                        kept.ready(pe, s)
                        weighed.ready(pe, s)
                        for h in range(HC):
                            bent.free(pe, s * HC + h)
                            lifted.done(pe.matmul(chip.bank(h), w[:, u % 4, h * P:(h + 1) * P], zt[:, u % 2, :],
                                                  start=True, stop=True))

                    def lower(s, u):
                        mixed.free(pe, s)
                        out = chip.bank(4 + u % 2)
                        b2 = w[0:3, u % 4, HID + HC * E + HC:PACK].bitcast(BF16)
                        pe.matmul(out.rearrange("p (g n) -> p g n", g=G), chip.ones3[:, :],
                                  b2.unsqueeze(1).to_broadcast([3, G, E]), start=True, stop=False)
                        for h in range(HC):
                            bent.ready(pe, s * HC + h)
                            for t in range(G):
                                last = pe.matmul(out[:, t * P:(t + 1) * P], hidden[:, u % 2, h, t * P:(t + 1) * P],
                                                 w[:, u % 4, HID + h * P:HID + (h + 1) * P], start=False,
                                                 stop=h == HC - 1 and t == G - 1)
                        lowered.done(last)
                    engine_loop(pe, SLOTS, 8, [(turn, 0), (lift, 1), (lower, 2)])

    def run(self):
        self.route()
        self.choose()
        self.dispatch()
        self.experts()


def turn_tokens(nc, chip):
    xt = chip.ab[:, :, :, :].rearrange("p t s c -> p t (s c)")
    with chip.phase("turn"):
        norm = Norm(chip, Carve(chip.small), (EPS_LN,), banks=(0, 1), by_act=2)

        def group(n):
            return chip.x[:, bass.ds(n * G, G), :]

        with nc.Block() as block:
            @block.gpsimd
            def _(pool):
                norm.open_pool(pool)
                engine_loop(pool, GROUPS, 2, [(lambda n, u: norm.rstd(pool, n, u), 0)])

            @block.vector
            def _(dve):
                engine_loop(dve, GROUPS, 2, [(lambda n, u: norm.stats(dve, group(n), n, u), 0),
                                             (lambda n, u: norm.apply(dve, group(n), n, u), 1)])

            @block.scalar
            def _(act):
                norm.open_act(act)

                def keep(n, u):
                    norm.keep(act, n, u, out=xt[:, bass.ds(n * G, G), :].rearrange("p g n -> p (g n)"))
                engine_loop(act, GROUPS, 2, [(lambda n, u: norm.apply_act(act, group(n), n, u), 0), (keep, 1)])

            @block.tensor
            def _(pe):
                norm.open_pe(pe)
                engine_loop(pe, GROUPS, 2, [(lambda n, u: norm.turn(pe, n, u), 0)])


GATES = ("c", "i", "o")
UNROLL = 8
HALVES = 2
CHUNKS, STEPS = NP_, NC_


class Pass:

    def __init__(self, cell, tag, first, stores):
        self.cell, self.first, self.stores = cell, first, stores
        self.steps = STEPS - first
        chip = cell.chip
        self.summed = Flow(chip, f"{tag}_summed")
        self.read = Flow(chip, f"{tag}_read", 4)
        self.carried = Flow(chip, f"{tag}_carried")
        self.bounded = Flow(chip, f"{tag}_bounded")
        self.stepped = Flow(chip, f"{tag}_stepped")
        self.links = chip.sem(f"{tag}_links")
        self.saved = Flow(chip, f"{tag}_saved", 4)

    def each_step(self, eng, stage):
        with eng.Fori(self.first // UNROLL, STEPS // UNROLL) as i:
            for u in range(UNROLL):
                step = i * UNROLL + u
                stage(step - self.first if self.first else step, step, u % 2)

    def tensor(self, pe, base, base_h):
        cell, banks = self.cell, self.cell.chip.banks

        def bank(s, par, g):
            return banks[:, 4 + 2 * s + par, 0:P] if g == 0 else banks[:, 2 * s + par, (g - 1) * P:g * P]

        def prime(k, step, par, s):
            self.read.free(pe, base + (k * HALVES + s))
            for g, gate in enumerate(GATES):
                pe.matmul(bank(s, par, g), cell.bias3[:, g, :], cell.chip.ones3[:, :], start=g < 2, stop=False)
            for g, gate in enumerate(GATES):
                pe.matmul(bank(s, par, g), cell.u_w[gate], cell.xt[:, bass.ds(step + s * STEPS, 1), :]
                          .rearrange("p a n -> p (a n)"), start=False, stop=False)

        def finish(k, par, s):
            self.stepped.ready(pe, base_h + (k * HALVES + s))
            for g, gate in enumerate(GATES):
                last = pe.matmul(bank(s, par, g), cell.v_w[gate], cell.h[:, 1 - par, s, :], start=False, stop=g != 1)
                if g != 1:
                    self.summed.done(last)

        def body(i, last):
            for u in range(UNROLL):
                step = i * UNROLL + u
                k = step - self.first
                for s in range(HALVES):
                    finish(k, u % 2, s)
                    if not (last and u == UNROLL - 1):
                        prime(k + 1, step + 1, (u + 1) % 2, s)

        for s in range(HALVES):
            prime(0, self.first, 0, s)
        with pe.Fori(self.first // UNROLL, STEPS // UNROLL - 1) as i:
            body(i, False)
        body(STEPS // UNROLL - 1, True)

    def scalar(self, act, base):
        cell, banks = self.cell, self.cell.chip.banks

        def stage(k, step, par):
            for s in range(HALVES):
                n = base + (k * HALVES + s)
                self.summed.ready(act, n * 2)
                act.activation(cell.g[:, s, :], banks[:, 4 + 2 * s + par, 0:P], ACT.Tanh)
                self.summed.ready(act, n * 2 + 1)
                self.read.done(act.activation(cell.io[:, s, :, :].rearrange("p a n -> p (a n)"), banks[:, 2 * s + par, 0:2 * P],
                                              ACT.Sigmoid))
                self.carried.ready(act, n)
                self.bounded.done(act.activation(cell.g[:, s, :], cell.c[:, s, :], ACT.Tanh))
        self.each_step(act, stage)

    def vector(self, dve, base, base_h):
        cell = self.cell

        def stage(k, step, par):
            for s in range(HALVES):
                n, nh = base + (k * HALVES + s), base_h + (k * HALVES + s)
                i, o = cell.io[:, s, 0, :], cell.io[:, s, 1, :]
                self.stepped.ready(dve, nh)
                dve.tensor_tensor(cell.hc[:, s, :], cell.h[:, 1 - par, s, :], cell.c[:, s, :], ALU.mult
                                  ).then_inc(self.links, 1)
                dve.wait_ge(self.read.sem, n + 5)
                dve.tensor_tensor(cell.ig[:, s, :], i, cell.g[:, s, :], ALU.mult).then_inc(self.links, 1)
                dve.wait_ge(self.links, n * 2 + 2)
                self.carried.done(dve.tensor_tensor(cell.c[:, s, :], cell.hc[:, s, :], cell.ig[:, s, :], ALU.add))
                self.bounded.ready(dve, n)
                if self.stores:
                    self.saved.free(dve, n)
                    dve.sem_inc(cell.paced, 1)
                self.stepped.done(dve.tensor_tensor(cell.h[:, par, s, :], o, cell.g[:, s, :], ALU.mult))
        self.each_step(dve, stage)

    def gpsimd(self, pool, base, base_h):
        cell = self.cell
        if not self.stores:
            return

        def stage(k, step, par):
            for s in range(HALVES):
                self.stepped.ready(pool, base_h + (k * HALVES + (s + HALVES)))
                self.saved.done(pool.tensor_copy(cell.hs[:, bass.ds(step + s * STEPS, 1), :].rearrange("p a n -> p (a n)"),
                                                 cell.h[:, par, s, :]))
        self.each_step(pool, stage)

    def begin(self, dve, fresh, base_h):
        cell = self.cell
        if fresh:
            dve.memset(cell.start, 0.0).then_inc(cell.begun, 1)
            dve.wait_ge(cell.begun, 1)
        else:
            ends = self.ends()
            cell.chain(dve.tensor_copy(cell.start[:, 0, 1:CHUNKS], ends[0][:, 0:CHUNKS - 1]))
            cell.chain(dve.tensor_copy(cell.start[:, 1, 1:CHUNKS], ends[1][:, 0:CHUNKS - 1]))
        dve.tensor_copy(self.ends()[1], cell.start[:, 1, :])
        for s in range(HALVES):
            self.stepped.done(dve.tensor_copy(cell.h[:, 1, s, :], cell.start[:, 0, s * P:(s + 1) * P]))

    def ends(self):
        cell = self.cell
        return (cell.h[:, 1, :, :].rearrange("p s n -> p (s n)"), cell.c.rearrange("p s n -> p (s n)"))


class Links:

    def __init__(self, sem):
        self.sem, self.eng, self.base, self.n = sem, None, 0, 0

    def at(self, eng, base):
        self.eng, self.base, self.n = eng, base, 0

    def __call__(self, ins):
        self.n += 1
        ins.then_inc(self.sem, 1)
        self.eng.wait_ge(self.sem, self.base + self.n)


class Cell:

    def __init__(self, chip):
        self.chip = chip
        carve, scratch = Carve(chip.small), Carve(chip.work)
        self.u_w = {g: carve(P) for g in GATES}
        self.v_w = {g: carve(P) for g in GATES}
        self.bias3 = carve(3, P, parts=3, dt=BF16)
        self.start = carve(2, CHUNKS)
        self.h = carve(2, HALVES, P)
        self.c = carve(HALVES, P)
        self.io = carve(HALVES, 2, P)
        self.g = carve(HALVES, P)
        products = carve(2, HALVES, P)
        self.ig, self.hc = products[:, 0, :, :], products[:, 1, :, :]
        self.flag = carve(1, dt=I32)
        self.met, self.ones = carve(1), carve(1)
        self.total, self.rest = scratch(3 * P, parts=1), scratch(3 * P, parts=1)
        self.pieces = [scratch(3 * P, parts=1, dt=BF16) for _ in range(3)]
        self.xt = chip.ab[:, :, :, :].rearrange("p t s c -> p t (s c)")
        self.hs = chip.work[:, :].rearrange("p (t n) -> p t n", n=P)
        self.moved = self.io.rearrange("p s a n -> p (s a n)").rearrange("p (q n) -> p q n", q=2)[:, :, 0:CHUNKS - 1]
        self.size = products.rearrange("p a s n -> p a (s n)")[:, :, 0:CHUNKS - 1]
        self.paced, self.begun = chip.sem("paced"), chip.sem("begun")
        self.chain = Links(chip.sem("chain"))
        self.tested = chip.sem("tested")
        self.counted = chip.sem("counted")
        self.flagged = chip.sem("flagged")

    def compare(self, dve, run, turn):
        chain = self.chain
        ends = run.ends()
        for q in range(2):
            last = dve.tensor_tensor(self.moved[:, q, :], ends[q][:, 0:CHUNKS - 1], self.start[:, q, 1:CHUNKS],
                                     ALU.subtract)
        chain(last)
        for q in range(2):
            last = dve.tensor_tensor(self.size[:, q, :], ends[q][:, 0:CHUNKS - 1], ends[q][:, 0:CHUNKS - 1], ALU.mult)
        chain(last)
        chain(dve.tensor_tensor(self.moved, self.moved, self.moved, ALU.mult))
        chain(dve.tensor_scalar(self.size, self.size, 1.0, CHUNK_TOL ** 2, ALU.add, ALU.mult))
        chain(dve.tensor_tensor(self.moved, self.moved, self.size, ALU.is_le))
        dve.tensor_reduce(self.met, self.moved, AX.XY, ALU.min).then_inc(self.tested, 1)
        dve.wait_ge(self.counted, turn + 1)
        dve.tensor_copy(self.flag[0:1, :], self.chip.banks[0:1, 0, 0:1]).then_inc(self.flagged, 1)

    TEST_LINKS = 5

    def count(self, pe, turn):
        pe.wait_ge(self.tested, turn + 1)
        pe.matmul(self.chip.banks[0:1, 0, 0:1], self.met, self.ones, start=True, stop=True).then_inc(self.counted, 1)

    def flag_value(self, eng, turn):
        eng.wait_ge(self.flagged, turn + 1)
        eng.sem_inc(self.paced, 1)
        return eng.value_load(self.flag[0:1, 0:1], min_val=0, max_val=P)


def recur(nc, chip, p):
    with chip.phase("cell"):
        cell = Cell(chip)
        w_in, b_in, zeroed, cut, spread = (chip.sem(s) for s in ("w_in", "b_in", "zeroed", "cut", "spread"))
        prep = Chain(chip, "prep")
        warm = Pass(cell, "warm", STEPS - WARM, False)
        main = Pass(cell, "main", 0, True)
        more = Pass(cell, "more", 0, True)
        per, per_h = STEPS * HALVES, (STEPS + 1) * HALVES

        def rounds(eng, run, skipped=None):
            with eng.If(cell.flag_value(eng, 0) < P):
                with eng.Fori(0, CHUNKS - 2) as t:
                    with eng.If(cell.flag_value(eng, t) < P):
                        run(t)
                    with eng.Else():
                        if skipped is not None:
                            skipped()
                        else:
                            eng.sem_inc(cell.paced, 1)
                    eng.sem_inc(cell.paced, 1)
                eng.sem_inc(cell.paced, 1)

        with nc.Block() as block:
            @block.sync
            def _(sp):
                for gate in GATES:
                    sp.dma_start(cell.u_w[gate], p[f"U_{gate}"]).then_inc(w_in, 16)
                    sp.dma_start(cell.v_w[gate], p[f"V_{gate}"]).then_inc(w_in, 16)
                for g, gate in enumerate(GATES):
                    sp.dma_start(cell.total[:, g * P:(g + 1) * P], row(p[f"b_{gate}"])).then_inc(b_in, 16)
                sp.wait_ge(cut, 1)
                for k in range(3):
                    sp.dma_start(cell.bias3[k:k + 1, :, :].rearrange("a g n -> a (g n)"), cell.pieces[k]).then_inc(spread, 16)

            @block.gpsimd
            def _(pool):
                main.saved.open(pool)
                more.saved.open(pool)
                pool.wait_ge(spread, 48)
                main.gpsimd(pool, 0, 0)
                rounds(pool, lambda t: more.gpsimd(pool, t * per, t * per_h))

            @block.vector
            def _(dve):
                dve.memset(cell.ones, 1.0).then_inc(zeroed, 1)
                chain = prep.on(dve)
                dve.wait_ge(b_in, 48)
                for k in range(3):
                    piece = dve.tensor_copy(cell.pieces[k], cell.total)
                    if k == 2:
                        piece.then_inc(cut, 1)
                    else:
                        chain(piece)
                        chain(dve.tensor_tensor(cell.rest, cell.total, cell.pieces[k], ALU.subtract))
                        chain(dve.tensor_copy(cell.total, cell.rest))
                warm.begin(dve, True, 0)
                warm.vector(dve, 0, 0)
                cell.chain.at(dve, 0)
                warm.stepped.ready(dve, (WARM + 1) * HALVES - 1)
                main.begin(dve, False, 0)
                main.vector(dve, 0, 0)
                main.stepped.ready(dve, per_h - 1)
                cell.compare(dve, main, 0)
                main.saved.ready(dve, per - 1)

                def again(t):
                    cell.chain.at(dve, t * (2 + cell.TEST_LINKS) + (2 + cell.TEST_LINKS))
                    more.begin(dve, False, t * per_h)
                    more.vector(dve, t * per, t * per_h)
                    more.stepped.ready(dve, t * per_h + (per_h - 1))
                    cell.compare(dve, more, t + 1)
                    more.saved.ready(dve, t * per + (per - 1))
                    dve.sem_inc(cell.paced, 1)
                rounds(dve, again, skipped=lambda: dve.sem_inc(cell.flagged, 1))

            @block.scalar
            def _(act):
                for run in (warm, main, more):
                    run.read.open(act)
                warm.scalar(act, 0)
                main.scalar(act, 0)
                rounds(act, lambda t: more.scalar(act, t * per))

            @block.tensor
            def _(pe):
                pe.wait_ge(w_in, 96)
                pe.wait_ge(spread, 48)
                pe.wait_ge(zeroed, 1)
                warm.tensor(pe, 0, 0)
                main.tensor(pe, 0, 0)
                cell.count(pe, 0)

                def again(t):
                    more.tensor(pe, t * per, t * per_h)
                    cell.count(pe, t + 1)
                rounds(pe, again)


def finish(nc, chip, out):
    hs = chip.work[:, :].rearrange("p (t n) -> p t n", n=P)
    carve = Carve(chip.small)
    with chip.phase("finish"):
        flat = carve(2, G, P)
        copied = Flow(chip, "copied")
        turned = Flow(chip, "turned", 2)
        added = Flow(chip, "added", 2)
        stored = [chip.sem(f"stored{u}") for u in range(2)]

        def group(n):
            return chip.x[:, bass.ds(n * G, G), :]

        with nc.Block() as block:
            @block.sync
            def _(sp):
                for ic in range(ICS):
                    with sp.Fori(0, GROUPS // ICS // 2) as i:
                        for u in range(2):
                            n = i * 2 + (u + ic * (GROUPS // ICS))
                            added.ready(sp, n)
                            sp.dma_start(out[:, ic, bass.ds((i * 2 + u) * G, G), :], group(n)).then_inc(stored[u], 16)
                for u in range(2):
                    sp.wait_ge(stored[u], 16 * GROUPS // 2)

            @block.scalar
            def _(act):
                def copy(n, u):
                    turned.free(act, n)
                    copied.done(act.copy(flat[:, u, :, :], hs[:, bass.ds(n * G, G), :]))
                engine_loop(act, GROUPS, 2, [(copy, 0)])

            @block.tensor
            def _(pe):
                turned.open(pe)

                def turn(n, u):
                    copied.ready(pe, n)
                    added.free(pe, n)
                    for t in range(G):
                        last = pe.transpose(chip.banks[:, u, t * P:(t + 1) * P], flat[:, u, t, :], chip.ident[:, :])
                    turned.done(last)
                engine_loop(pe, GROUPS, 2, [(turn, 0)])

            @block.vector
            def _(dve):
                added.open(dve)

                def add(n, u):
                    turned.ready(dve, n)
                    added.done(dve.tensor_tensor(group(n), group(n), chip.bank(u).rearrange("p (g e) -> p g e", g=G), ALU.add))
                engine_loop(dve, GROUPS, 2, [(add, 0)])


def metaformer(nc, D, out):
    tokens = "(i p) j e -> p i j e"
    x0 = D["x"][0].rearrange(tokens, p=P)
    x1 = nc.dram_tensor("after_mixture", (P, TILES, E), F32).ap()
    with ExitStack() as ctx:
        chip = Chip(nc, ctx)
        setup(nc, chip, setup_par(D))
        par = conv_par(chip, D, "l0")
        project_tokens(nc, chip, "l0", par, x0)
        compound_sums(nc, chip, "l0", par, False)
        protein_sums(nc, chip, "l0", par, False)
        combine(nc, chip, "l0", par, x0)
        chip.recycle()
        mixture = Mixture(nc, chip, {k.removeprefix("L0_ffn_"): v for k, v in D.items() if k.startswith("L0_ffn_")})
        mixture.run()
        chip.recycle()
        par = conv_par(chip, D, "l1")
        project_tokens(nc, chip, "l1", par, None, mixture.out.rearrange("(p t k) e -> p t k e", p=P, k=2), x1)
        compound_sums(nc, chip, "l1", par, True)
        protein_sums(nc, chip, "l1", par, True)
        combine(nc, chip, "l1", par, x1.rearrange("p (i j) e -> p i j e", i=ICS))
        turn_tokens(nc, chip)
        recur(nc, chip, {k.removeprefix("L1_ffn_"): v for k, v in D.items() if k.startswith("L1_ffn_")})
        finish(nc, chip, out[0].rearrange(tokens, p=P))


def setup_par(D):
    return {"l0_ln_w": D["L0_conv_ln_w"], "l1_ln_w": D["L1_conv_ln_w"], "l1_ln_b": D["L1_conv_ln_b"],
            "l0_lnc_w": D["L0_conv_lnc_w"], "l1_lnc_w": D["L1_conv_lnc_w"], "l1_lnc_b": D["L1_conv_lnc_b"],
            "moe_ln_g": D["L0_ffn_ln_g"], "moe_ln_b": D["L0_ffn_ln_b"], "moe_b1": D["L0_ffn_b1"]}


def conv_par(chip, D, layer):
    if layer == "l0":
        q = {k.removeprefix("L0_conv_"): v for k, v in D.items() if k.startswith("L0_conv_")}
        return {"gates": [(q["gw1"], None), (q["gw2"], None)], "lins": [(q["w1"], q["b1"]), (q["w2"], q["b2"])],
                "edge": (q["we"], q["be"]), "out": (q["ws"], q["bs"]), "mask": q["z_mask"].rearrange("b i j c -> (b i) (j c)"),
                "ln_w": col(chip, "l0_ln_w"), "ln_b": None, "lnc_w": col(chip, "l0_lnc_w"), "lnc_b": None,
                "protein": q["protein_pair"], "compound": q["compound_pair"]}
    q = {k.removeprefix("L1_conv_"): v for k, v in D.items() if k.startswith("L1_conv_")}
    return {"gates": [(q["gate_w"], q["gate_b"])], "lins": [(q["lin_w"], q["lin_b"])],
            "edge": (q["eg_w"], q["eg_b"]), "out": (q["as_w"], q["as_b"]), "mask": q["z_mask"].rearrange("b i j c -> (b i) (j c)"),
            "ln_w": col(chip, "l1_ln_w"), "ln_b": col(chip, "l1_ln_b"),
            "lnc_w": col(chip, "l1_lnc_w"), "lnc_b": col(chip, "l1_lnc_b", hi=C),
            "protein": q["protein_pair"], "compound": q["compound_pair"]}


def kernel(**inputs):
    import numpy as np
    import concourse.bacc as bacc
    from concourse.bass_utils import run_bass_kernel_spmd

    nc = bacc.Bacc("TRN2", target_bir_lowering=False, num_devices=1)
    arrays, D = {}, {}
    for name, a in inputs.items():
        if name in ("L1_ffn_U_f", "L1_ffn_V_f", "L1_ffn_b_f"):
            continue
        arrays[name] = np.ascontiguousarray(a)
        D[name] = nc.dram_tensor(name, arrays[name].shape, F32, kind="ExternalInput").ap()
    out = nc.dram_tensor("out", (1, NP_, NC_, E), F32, kind="ExternalOutput").ap()
    metaformer(nc, D, out)
    return run_bass_kernel_spmd(nc, [arrays], core_ids=[0]).results[0]["out"]
```

```python
from contextlib import ExitStack

import concourse.bass as bass
from concourse import mybir

F32 = mybir.dt.float32
BF16 = mybir.dt.bfloat16
F32R = mybir.dt.float32r
I32 = mybir.dt.int32
U32 = mybir.dt.uint32
ALU = mybir.AluOpType
ACT = mybir.ActivationFunctionType
AX = mybir.AxisListType

P = 128
NP_, NC_, E, C = 256, 64, 128, 64
TILES = NP_ * NC_ // P
G = 4
GROUPS = TILES // G
EXPERTS, HID = 8, 512
HC = HID // P
ICS = NP_ // P
EPS_LN = 1e-5
EPS_LNC = 1e-6
CHUNK_TOL = 2.0 ** -18
WARM = 64



def engine_loop(eng, total, unroll, stages, peel=0):
    lag = max(l for _, l in stages)
    head = min(total, -(-max(lag, peel) // unroll) * unroll)

    for t in range(head):
        for stage, l in stages:
            if t >= l:
                stage(t - l, (t - l) % unroll)
    if total > head:
        with eng.Fori(head // unroll, total // unroll) as i:
            for u in range(unroll):
                for stage, l in stages:
                    stage(i * unroll + (u - l), (u - l) % unroll)
    for t in range(total, total + lag):
        for stage, l in stages:
            if 0 <= t - l < total:
                stage(t - l, (t - l) % unroll)


class Flow:

    def __init__(self, chip, name, depth=0):
        self.sem, self.depth = chip.sem(name), depth

    def open(self, eng):
        eng.sem_inc(self.sem, self.depth)

    def done(self, ins):
        ins.then_inc(self.sem, 1)

    def ready(self, eng, n):
        eng.wait_ge(self.sem, n + (1 + self.depth))

    def free(self, eng, n):
        eng.wait_ge(self.sem, n + 1)


class Chain:

    def __init__(self, chip, name, eng=None):
        self.sem, self.n = chip.sem(name), 0

    def on(self, eng):
        self.eng = eng
        return self

    def __call__(self, ins):
        self.n += 1
        ins.then_inc(self.sem, 1)
        self.eng.wait_ge(self.sem, self.n)


class Chip:

    def __init__(self, nc, ctx):
        self.nc, self.ctx, self.sems = nc, ctx, []
        sb = self.sb
        self.x = sb("x_tiles", [P, TILES, E])
        self.ab = sb("ab_tiles", [P, TILES, 2, C])
        self.ident = sb("ident", [P, P])
        self.cols = sb("cols", [P, 64])
        self.ones3 = sb("ones3", [3, P], BF16)
        self.small = sb("small", [P, 3740])
        self.banks = ctx.enter_context(nc.psum_tensor("banks", [P, 8, 512], F32))
        self.take_work("work")
        ctx.callback(self.give_work)

    def sb(self, name, shape, dt=F32):
        return self.ctx.enter_context(self.nc.sbuf_tensor(name, shape, dt))

    def take_work(self, name):
        self.work_ctx = ExitStack()
        self.work = self.work_ctx.enter_context(self.nc.sbuf_tensor(name, [P, 2 * NC_ * P], F32))

    def give_work(self):
        self.work_ctx.close()

    def sem(self, name):
        self.sems.append(self.nc.alloc_semaphore(name=f"{self.tag}_{name}"))
        return self.sems[-1]

    def bank(self, b):
        return self.banks[:, b, :]

    def phase(self, tag):
        self.tag = tag
        return ExitStack()

    def recycle(self):
        self.nc.clear_and_free_semaphores(self.sems)
        self.nc.all_engine_barrier()
        self.sems = []


class Carve:

    def __init__(self, base):
        self.base, self.at = base, 0

    def __call__(self, *dims, parts=P, dt=F32):
        n = 1
        for d in dims:
            n *= d
        words = n if dt in (F32, I32, U32) else (n + 1) // 2
        ap = self.base[0:parts, self.at:self.at + words]
        self.at += words
        assert self.at <= self.base.shape[1], "region too small"
        if dt != F32:
            ap = ap.bitcast(dt)
        names = "abcd"[:len(dims)]
        if len(dims) > 1:
            ap = ap.rearrange(f"p ({' '.join(names)}) -> p {' '.join(names)}", **dict(zip(names, dims)))
        return ap


def row(v):
    return v.rearrange("(a n) -> a n", a=1)


COL = {"l0_ln_w": 0, "l1_ln_w": 1, "l1_ln_b": 2, "l0_lnc_w": 3, "l1_lnc_w": 4, "l1_lnc_b": 5,
       "moe_g": 8, "moe_b": 16, "moe_b1": 24, "cell_c": 56, "cell_i": 57, "cell_o": 58}
N_COLS = 59


def setup(nc, chip, par):
    rows = chip.small[0:N_COLS, 0:P]
    one_row = {name: par[name] for name in ("l0_ln_w", "l1_ln_w", "l1_ln_b", "cell_c", "cell_i", "cell_o")}
    half_row = {"l0_lnc_w": par["l0_lnc_w"], "l1_lnc_w": par["l1_lnc_w"], "l1_lnc_b": par["l1_lnc_b"]}
    n_dma = len(one_row) + 2 * len(half_row) + 3
    with chip.phase("setup"):
        rows_in, zeroed, ident_made, turned, ones_made = (
            chip.sem(n) for n in ("rows_in", "zeroed", "ident", "turned", "ones"))
        with nc.Block() as block:
            @block.sync
            def _(sp):
                sp.wait_ge(zeroed, 1)
                for k, v in one_row.items():
                    sp.dma_start(rows[COL[k]:COL[k] + 1, :], row(v)).then_inc(rows_in, 16)
                for k, v in half_row.items():
                    for h in range(2):
                        sp.dma_start(rows[COL[k]:COL[k] + 1, h * C:(h + 1) * C], row(v)).then_inc(rows_in, 16)
                for k, v in (("moe_g", par["moe_ln_g"]), ("moe_b", par["moe_ln_b"])):
                    sp.dma_start(rows[COL[k]:COL[k] + EXPERTS, :], v).then_inc(rows_in, 16)
                sp.dma_start(rows[COL["moe_b1"]:COL["moe_b1"] + EXPERTS * HC, :],
                             par["moe_b1"].rearrange("e (h p) -> (e h) p", p=P)).then_inc(rows_in, 16)

            @block.gpsimd
            def _(pool):
                pool.memset(chip.ident[:, :], 0.0).then_inc(ident_made, 1)
                pool.wait_ge(ident_made, 1)
                pool.affine_select(out=chip.ident[:, :], in_=chip.ident[:, :], compare_op=ALU.not_equal,
                                   fill=1.0, base=0, pattern=[[-1, P]], channel_multiplier=1
                                   ).then_inc(ident_made, 1)

            @block.vector
            def _(dve):
                dve.memset(rows, 0.0).then_inc(zeroed, 1)
                dve.memset(chip.ones3[:, :], 1.0).then_inc(ones_made, 1)
                dve.wait_ge(turned, 1)
                dve.tensor_copy(chip.cols[:, 0:N_COLS], chip.banks[:, 0, 0:N_COLS]).then_inc(ones_made, 1)

            @block.tensor
            def _(pe):
                pe.wait_ge(rows_in, 16 * n_dma)
                pe.wait_ge(ident_made, 2)
                pe.transpose(chip.banks[:, 0, 0:N_COLS], rows, chip.ident[0:N_COLS, 0:N_COLS]).then_inc(turned, 1)


def col(chip, name, k=0, lo=0, hi=P):
    c = COL[name] + k
    return chip.cols[lo:hi, c:c + 1]


class Linear:

    def __init__(self, chip, carve, tag, weights, biases, g, b, bank, copies=1, scratch=None):
        self.chip, self.weights, self.biases, self.g, self.b = chip, weights, biases, g, b
        self.n = n = sum(w.shape[1] for w in weights)
        self.k = weights[0].shape[0]
        self.copies = copies
        self.w = carve(n)
        self.bias3 = carve(n, parts=3, dt=BF16)
        scratch = carve if scratch is None else scratch
        self.raw = scratch(n)
        self.total, self.rest = scratch(n, parts=1), scratch(n, parts=1)
        self.pieces = [scratch(n, parts=1, dt=BF16) for _ in range(3)]
        self.product = chip.banks[0:1, bank, 0:n]
        self.zeroed, self.loaded, self.folded, self.shifted, self.cut, self.spread = (
            chip.sem(f"{tag}_{s}") for s in ("zeroed", "loaded", "folded", "shifted", "cut", "spread"))
        self.n_loads = len(weights) * copies + sum(x is not None for x, _ in biases)
        self.chain = Chain(chip, f"{tag}_chain")

    def load(self, sp):
        sp.wait_ge(self.zeroed, 1)
        at = 0
        for w in self.weights:
            for h in range(self.copies):
                sp.dma_start(self.raw[h * self.k:(h + 1) * self.k, at:at + w.shape[1]], w).then_inc(self.loaded, 16)
            at += w.shape[1]
        at = 0
        for v, n in self.biases:
            if v is not None:
                sp.dma_start(self.total[0:1, at:at + n], row(v)).then_inc(self.loaded, 16)
            at += n
        sp.wait_ge(self.cut, 1)
        for k in range(3):
            sp.dma_start(self.bias3[k:k + 1, :], self.pieces[k]).then_inc(self.spread, 16)

    def fold(self, dve):
        chain = self.chain.on(dve)
        dve.memset(self.total, 0.0).then_inc(self.zeroed, 1)
        dve.wait_ge(self.loaded, 16 * self.n_loads)
        rows = self.k * self.copies
        dve.tensor_scalar(self.w[0:rows, :], self.raw[0:rows, :], self.g, None, ALU.mult).then_inc(self.folded, 1)
        if self.b is not None:
            dve.wait_ge(self.shifted, 1)
            chain(dve.tensor_tensor(self.total, self.total, self.product, ALU.add))
        for k in range(3):
            piece = dve.tensor_copy(self.pieces[k], self.total)
            if k == 2:
                piece.then_inc(self.cut, 1)
            else:
                chain(piece)
                chain(dve.tensor_tensor(self.rest, self.total, self.pieces[k], ALU.subtract))
                chain(dve.tensor_copy(self.total, self.rest))

    def shift(self, pe):
        if self.b is not None:
            pe.wait_ge(self.loaded, 16 * self.n_loads)
            pe.matmul(self.product, self.b, self.raw[0:self.k, :], start=True, stop=True).then_inc(self.shifted, 1)

    def await_ready(self, pe):
        pe.wait_ge(self.folded, 1)
        pe.wait_ge(self.spread, 48)


class Norm:

    def __init__(self, chip, carve, eps, banks, depth=2, zn=None, width=E, by_act=0):
        self.by_act = by_act
        self.chip, self.banks, self.depth = chip, banks, depth
        self.affine = (1.0, eps[0]) if len(eps) == 1 else (1.0 + eps[1], eps[0] * eps[1])
        self.width = width
        self.st = carve(depth, G, 6)
        self.mv = carve(depth, G, 2)
        self.r = carve(depth, G)
        self.var, self.shift = carve(depth, G), carve(depth, G)
        self.shifted, self.applied_act = Flow(chip, "norm_shifted"), Flow(chip, "applied_act", depth)
        self.mhalf = carve(G)
        self.zn = carve(depth, G, width) if zn is None else zn
        self.zt = carve(2, G * P)
        self.stat, self.scaled = Flow(chip, "stat"), Flow(chip, "scaled")
        self.agg = Flow(chip, "agg")
        self.half, self.links, self.paced = chip.sem("half"), chip.sem("links"), chip.sem("paced")
        self.applied = Flow(chip, "applied")
        self.turned = Flow(chip, "turned", depth)
        self.kept = Flow(chip, "kept", len(set(banks)))

    def open_pool(self, pool):
        pool.memset(self.mhalf, -0.5).then_inc(self.half, 1)
        pool.wait_ge(self.half, 1)

    def open_pe(self, pe):
        self.turned.open(pe)

    def open_act(self, act):
        self.kept.open(act)
        if self.by_act:
            self.applied_act.open(act)

    def stats(self, dve, src, n, u):
        for t in range(G):
            last = dve.bn_stats(self.st[:, u, t, :], src[:, t, :])
        self.stat.done(last)
        self.stat.ready(dve, n)
        dve.sem_inc(self.paced, 1)
        for t in range(G):
            last = dve.bn_aggr(self.mv[:, u, t, :], self.st[:, u, t, :])
        last.then_inc(self.links, 1)
        dve.wait_ge(self.links, n + 1)
        self.agg.done(dve.tensor_scalar(self.var[:, u, :], self.mv[:, u, :, 1], self.affine[0], self.affine[1],
                                        ALU.mult, ALU.add))

    def rstd(self, pool, n, u):
        if self.by_act:
            self.applied_act.free(pool, n)
        self.agg.ready(pool, n)
        self.scaled.done(pool.tensor_tensor(self.r[:, u, :], self.var[:, u, :], self.mhalf, ALU.pow))

    def apply(self, dve, src, n, u):
        self.scaled.ready(dve, n)
        if self.by_act:
            self.shifted.done(dve.scalar_tensor_tensor(self.shift[:, u, :], self.mv[:, u, :, 0], -1.0,
                                                       self.r[:, u, :], ALU.mult, ALU.mult))
        self.turned.free(dve, n)
        for t in range(G - self.by_act):
            last = dve.tensor_scalar(self.zn[:, u, t, :], src[:, t, :], self.mv[:, u, t, 0:1],
                                     self.r[:, u, t:t + 1], ALU.subtract, ALU.mult)
        self.applied.done(last)

    def apply_act(self, act, src, n, u):
        self.shifted.ready(act, n)
        self.turned.free(act, n)
        for t in range(G - self.by_act, G):
            last = act.activation(self.zn[:, u, t, :], src[:, t, :], ACT.Identity, bias=self.shift[:, u, t:t + 1],
                                  scale=self.r[:, u, t:t + 1])
        self.applied_act.done(last)

    def turn(self, pe, n, u):
        self.applied.ready(pe, n)
        if self.by_act:
            self.applied_act.ready(pe, n)
        self.kept.free(pe, n)
        w = self.width
        for k in range(G * w // P):
            src = self.zn[:, u, :, :].rearrange("p g e -> p (g e)")[:, k * P:(k + 1) * P]
            last = pe.transpose(self.chip.banks[:, self.banks[u % 2], k * P:(k + 1) * P], src, self.chip.ident[:, :])
        self.turned.done(last)

    def keep(self, act, n, u, out=None):
        self.turned.ready(act, n)
        cols = G * self.width
        if out is None:
            out = self.zt[:, u % 2, 0:cols]
        self.kept.done(act.copy(out, self.chip.banks[:, self.banks[u % 2], 0:cols]))


def load_tiles(sp, dst, src, arrived):
    for ic in range(ICS):
        for n in range(4):
            if ic:
                sp.wait_ge(arrived[n], 64)
            sp.dma_start(dst[:, (ic * 16 + n) * G:(ic * 16 + n + 1) * G, :],
                         src[:, ic, n * G:(n + 1) * G, :]).then_inc(arrived[n], 16)
        with sp.Fori(1, 4) as i:
            for u in range(4):
                sp.wait_ge(arrived[u], 16 * i + 64 * ic)
                sp.dma_start(dst[:, bass.ds((i * 4 + (u + ic * 16)) * G, G), :],
                             src[:, ic, bass.ds((i * 4 + u) * G, G), :]).then_inc(arrived[u], 16)


def await_tiles(eng, arrived, n, u):
    eng.wait_ge(arrived[u], 4 * n + (16 - 4 * u))


def project_tokens(nc, chip, tag, par, src, choices=None, keep_in=None):
    gates, lins, (edge, edge_b) = par["gates"], par["lins"], par["edge"]
    NG, NL = C * len(gates), C * len(lins)
    NS = NG + E
    carve = Carve(chip.work)
    xf = chip.x
    with chip.phase(f"{tag}_project"):
        lin = Linear(chip, carve, "w", [w for w, _ in gates] + [edge] + [w for w, _ in lins],
                     [(b, C) for _, b in gates] + [(edge_b, E)] + [(b, C) for _, b in lins],
                     par["ln_w"], par["ln_b"], bank=2)
        shared = 2 * lin.n <= 512
        DEPTH = 4 if shared else 2
        norm = Norm(chip, carve, (EPS_LNC, EPS_LN), banks=(0, 1), depth=DEPTH, by_act=2 if shared else 0)
        PAIRS = 4 if shared else 2
        sg = carve(PAIRS, 2, NS)
        mask = carve(TILES)
        mask_in = chip.sem("mask_in")
        if choices is not None:
            pair = carve(4, G, 2, E)
            pair_in = [chip.sem(f"pair_in{k}") for k in range(4)]
            stored = [chip.sem(f"stored{k}") for k in range(4)]
            merged = Flow(chip, "merged", 4)
            summed = Flow(chip, "summed")
        x_in = [chip.sem(f"x_in{k}") for k in range(4)]
        projected = Flow(chip, "projected", 4)
        squashed = Flow(chip, "squashed")
        gated = Flow(chip, "gated", PAIRS)
        masked = Flow(chip, "masked", PAIRS)

        def slot(u, h):
            return (2 * (u % 2) + h) % PAIRS

        def products(u, h):
            if shared:
                return chip.bank(4 + slot(u, h)).rearrange("p (t n) -> p t n", t=2)
            return chip.banks[:, 4 + 2 * h:6 + 2 * h, 0:lin.n]

        def tiles(n, k=0, m=G):
            return xf[:, bass.ds(n * G + k, m), :]

        with nc.Block() as block:
            @block.sync
            def _(sp):
                sp.dma_start(mask.rearrange("p (i j) -> p i j", i=ICS),
                             par["mask"].rearrange("(i p) j -> p i j", p=P)).then_inc(mask_in, 16)
                lin.load(sp)
                if src is not None:
                    load_tiles(sp, xf, src, x_in)
                    return

                def load(n, u):
                    merged.free(sp, n)
                    sp.dma_start(pair[:, u, :, :, :], choices[:, bass.ds(n * G, G), :, :]).then_inc(pair_in[u], 16)

                def store(n, u):
                    merged.ready(sp, n)
                    sp.dma_start(keep_in[:, bass.ds(n * G, G), :], tiles(n)).then_inc(stored[u], 16)
                engine_loop(sp, GROUPS, 4, [(load, 0), (store, 3)])
                for u in range(4):
                    sp.wait_ge(stored[u], 16 * GROUPS // 4)

            @block.vector
            def _(dve):
                gated.open(dve)
                if choices is not None:
                    merged.open(dve)
                lin.fold(dve)
                dve.wait_ge(mask_in, 16)

                def stats(n, u):
                    if src is not None:
                        await_tiles(dve, x_in, n, u)
                    else:
                        summed.ready(dve, n)
                        merged.done(dve.tensor_tensor(tiles(n), tiles(n), pair[:, u, :, 0, :], ALU.add))
                        merged.ready(dve, n)
                        dve.sem_inc(norm.paced, 1)
                    norm.stats(dve, tiles(n), n, u % DEPTH)

                def apply(n, u):
                    norm.apply(dve, tiles(n), n, u % DEPTH)

                def gate(n, u):
                    for h in range(2):
                        pair = n * 2 + h
                        projected.ready(dve, pair)
                        squashed.ready(dve, pair)
                        for t in range(2):
                            tile = n * G + (2 * h + t)
                            last = dve.scalar_tensor_tensor(
                                chip.ab[:, bass.ds(tile, 1), 0:NL // C, :].rearrange("p a b c -> p (a b c)"),
                                sg[:, slot(u, h), t, 0:NG], mask[:, bass.ds(tile, 1)],
                                products(u, h)[:, t, NS:NS + NL], ALU.mult, ALU.mult)
                        gated.done(last)

                engine_loop(dve, GROUPS, 4, [(stats, 0), (apply, 1), (gate, 4 if shared else 3)])

            @block.gpsimd
            def _(pool):
                norm.open_pool(pool)
                masked.open(pool)
                pool.wait_ge(mask_in, 16)

                def edge_mask(n, u):
                    if choices is not None:
                        await_tiles(pool, stored, n, u)
                        pool.sem_inc(norm.paced, 1)
                    for h in range(2):
                        pair = n * 2 + h
                        squashed.ready(pool, pair)
                        masked.done(pool.tensor_tensor(
                            tiles(n, 2 * h, 2), sg[:, slot(u, h), :, NG:NS],
                            mask[:, bass.ds(n * G + 2 * h, 2)].unsqueeze(2).to_broadcast([P, 2, E]), ALU.mult))

                def add_choices(n, u):
                    await_tiles(pool, pair_in, n, u)
                    pool.sem_inc(norm.paced, 1)
                    summed.done(pool.tensor_tensor(pair[:, u, :, 0, :], pair[:, u, :, 0, :], pair[:, u, :, 1, :], ALU.add))

                stages = [(lambda n, u: norm.rstd(pool, n, u % DEPTH), 1), (edge_mask, 4 if shared else 3)]
                engine_loop(pool, GROUPS, 4, stages if choices is None else [(add_choices, 0)] + stages)

            @block.scalar
            def _(act):
                norm.open_act(act)

                def squash(n, u):
                    for h in range(2):
                        pair = n * 2 + h
                        projected.ready(act, pair)
                        masked.free(act, pair)
                        gated.free(act, pair)
                        squashed.done(act.activation(sg[:, slot(u, h), :, :], products(u, h)[:, :, 0:NS], ACT.Sigmoid))

                def keep(n, u):
                    projected.free(act, n * 2 + 1)
                    norm.keep(act, n, u)

                stages = [(keep, 0), (squash, 1)]
                if norm.by_act:
                    stages = [(lambda n, u: norm.apply_act(act, tiles(n), n, u % DEPTH), 0), (keep, 1), (squash, 2)]
                engine_loop(act, GROUPS, 4, stages)

            @block.tensor
            def _(pe):
                norm.open_pe(pe)
                projected.open(pe)
                lin.shift(pe)
                lin.await_ready(pe)

                def project(n, u):
                    norm.kept.ready(pe, n)
                    for h in range(2):
                        pair = n * 2 + h
                        gated.free(pe, pair)
                        out = products(u, h)
                        if shared:
                            pe.matmul(out, chip.ones3[:, :], lin.bias3.unsqueeze(1).to_broadcast([3, 2, lin.n]),
                                      start=True, stop=False)
                        for t in range(2):
                            k = (2 * h + t) * P
                            if not shared:
                                pe.matmul(out[:, t, :], chip.ones3[:, :], lin.bias3, start=True, stop=False)
                            last = pe.matmul(out[:, t, :], norm.zt[:, u % 2, k:k + P], lin.w, start=False,
                                             stop=not shared or t == 1)
                        projected.done(last)

                engine_loop(pe, GROUPS, 4, [(lambda n, u: norm.turn(pe, n, u % DEPTH), 0), (project, 1)])


class PairStream:

    def __init__(self, chip, carve, carve_lin, gate_w, lin_w, lin_b, g, b=None, scratch=None):
        self.chip = chip
        self.stage = carve(4, G, E)
        self.norm = Norm(chip, carve, (EPS_LN,), banks=(0, 1), depth=4, zn=self.stage, by_act=3)
        self.lin = Linear(chip, carve_lin, "w", [gate_w, lin_w], [(None, C), (lin_b, C)], g, b, bank=2,
                          scratch=scratch)
        self.arrived = [chip.sem(f"arrived{u}") for u in range(4)]
        self.projected = Flow(chip, "projected", 2)
        self.squashed = Flow(chip, "squashed")
        self.gated = Flow(chip, "gated", 2)

    def out_bank(self, u):
        return self.chip.bank(2 + u % 2).rearrange("p (g s c) -> p g s c", g=G, s=2)

    def load(self, sp, srcs, n, u):
        self.norm.turned.free(sp, n)
        for lo, src in srcs:
            sp.dma_start(self.stage[lo:lo + src.shape[0], u, :, :], src).then_inc(self.arrived[u], 16 * (2 // len(srcs)))

    def stats(self, dve, n, u):
        dve.wait_ge(self.arrived[u], 8 * n + (32 - 8 * u))
        self.norm.stats(dve, self.stage[:, u, :, :], n, u)

    def apply(self, dve, n, u):
        self.norm.apply(dve, self.stage[:, u, :, :], n, u)

    def apply_act(self, act, n, u):
        self.norm.apply_act(act, self.stage[:, u, :, :], n, u)

    def keep(self, act, n, u):
        self.projected.free(act, n)
        self.norm.keep(act, n, u)

    def project(self, pe, n, u):
        self.norm.kept.ready(pe, n)
        self.gated.free(pe, n)
        out = self.chip.bank(2 + u % 2)
        pe.matmul(out.rearrange("p (g n) -> p g n", g=G), self.chip.ones3[:, :],
                  self.lin.bias3.unsqueeze(1).to_broadcast([3, G, 2 * C]), start=True, stop=False)
        for t in range(G):
            last = pe.matmul(out[:, t * P:(t + 1) * P], self.norm.zt[:, u % 2, t * P:(t + 1) * P], self.lin.w,
                             start=False, stop=t == G - 1)
        self.projected.done(last)

    def squash(self, act, dest, n, u):
        self.projected.ready(act, n)
        self.squashed.done(act.activation(dest, self.out_bank(u)[:, :, 0, :], ACT.Sigmoid))

    def gate(self, dve, dest, n, u):
        self.squashed.ready(dve, n)
        self.gated.done(dve.tensor_tensor(dest, dest, self.out_bank(u)[:, :, 1, :], ALU.mult))


ROWS = 16


def chunk_buffers(chip):
    return Carve(chip.work)(2, ICS, C, C)


def load_chunk(sp, pp, ppv, ic, h, arrived):
    for kc in range(ICS):
        for i in range(0, C, ROWS):
            sp.dma_start(pp[:, 1 - h, kc, i:i + ROWS, :],
                         ppv[ic * P + h * C + i:ic * P + h * C + i + ROWS, kc * P:(kc + 1) * P, :]
                         .rearrange("i k c -> k i c")).then_inc(arrived, 16)


def compound_sums(nc, chip, tag, par, raw_pairs):
    half = 0 if raw_pairs else 1
    carve = Carve(chip.work)
    cp = carve(NC_, C)
    ab2t = carve(2, 8, P)
    pairs = carve(2, 8, ICS * NC_)
    with chip.phase(f"{tag}_compound"):
        if raw_pairs:
            cp_in, chunk_in = chip.sem("cp_in"), chip.sem("chunk_in")
        else:
            (gate_w, _), (lin_w, lin_b) = par["gates"][0], par["lins"][0]
            stream = PairStream(chip, carve, Carve(chip.small), gate_w, lin_w, lin_b, par["ln_w"])
        groups = NC_ // G
        ab_turned = Flow(chip, "ab_turned")
        ab_kept = Flow(chip, "ab_kept", 2)
        zeroed, spread = chip.sem("zeroed"), Flow(chip, "spread")
        summed = Flow(chip, "summed")
        stored = Flow(chip, "stored", 2)
        cpv = par["compound"][0]

        with nc.Block() as block:
            @block.sync
            def _(sp):
                if raw_pairs:
                    for h in range(2):
                        sp.dma_start(cp[h * NC_:(h + 1) * NC_, :, :], cpv.rearrange("j k c -> k j c")).then_inc(cp_in, 16)
                    load_chunk(sp, chunk_buffers(chip), par["protein"][0], 0, 0, chunk_in)
                    return
                stream.lin.load(sp)

                def load(n, u):
                    src = cpv[bass.ds(n * G, G), :, :].rearrange("j k e -> k j e")
                    stream.load(sp, [(0, src), (NC_, src)], n, u)
                engine_loop(sp, groups, 4, [(load, 0)])

            @block.gpsimd
            def _(pool):
                pool.memset(pairs, 0.0).then_inc(zeroed, 1)
                if raw_pairs:
                    pool.wait_ge(cp_in, 32)
                else:
                    stream.norm.open_pool(pool)
                    engine_loop(pool, groups, 4, [(lambda n, u: stream.norm.rstd(pool, n, u), 0)])
                    stream.gated.ready(pool, groups - 1)
                pool.wait_ge(zeroed, 1)
                for c8 in range(C // 8):
                    if c8 >= 2:
                        summed.ready(pool, (c8 - 2) * 2 + 1)
                    for ic in range(ICS):
                        k = slice(ic * NC_, (ic + 1) * NC_)
                        last = pool.tensor_copy(pairs[k, c8 % 2, :, k], cp[k, :, c8 * 8:c8 * 8 + 8].rearrange("p j c -> p c j"))
                    spread.done(last)

            @block.vector
            def _(dve):
                if not raw_pairs:
                    stream.gated.open(dve)
                    stream.lin.fold(dve)
                ab_kept.open(dve)

                if not raw_pairs:
                    def gate(n, u):
                        stream.gate(dve, cp[:, bass.ds(n * G, G), :], n, u)
                    engine_loop(dve, groups, 4, [(lambda n, u: stream.stats(dve, n, u), 0),
                                                 (lambda n, u: stream.apply(dve, n, u), 1), (gate, 4)])
                for c8 in range(C // 8):
                    for q in range(2):
                        ab_turned.ready(dve, 2 * c8 + q)
                        if c8 >= 2 and q == 0:
                            summed.ready(dve, (c8 - 2) * 2 + 1)
                        ab_kept.done(dve.tensor_copy(ab2t[:, c8 % 2, 4 * q:4 * q + 4, :].rearrange("p c i -> p (c i)"),
                                                     chip.bank(4 + q)))

            @block.scalar
            def _(act):
                stored.open(act)
                if not raw_pairs:
                    stream.norm.open_act(act)

                    def squash(n, u):
                        stream.squash(act, cp[:, bass.ds(n * G, G), :], n, u)
                    engine_loop(act, groups, 4, [(lambda n, u: stream.apply_act(act, n, u), 0),
                                                 (lambda n, u: stream.keep(act, n, u), 1), (squash, 2)])
                for n in range(C // 4):
                    summed.ready(act, n)
                    stored.done(act.copy(chip.ab[:, :, 1, 4 * n:4 * n + 4],
                                         chip.bank(6 + n % 2).rearrange("p (c t) -> p t c", c=4)))

            @block.tensor
            def _(pe):
                if not raw_pairs:
                    stream.norm.open_pe(pe)
                    stream.projected.open(pe)
                if not raw_pairs:
                    stream.lin.shift(pe)
                    stream.lin.await_ready(pe)
                    engine_loop(pe, groups, 4, [(lambda n, u: stream.norm.turn(pe, n, u), 0),
                                                (lambda n, u: stream.project(pe, n, u), 1)])

                def turn(c8):
                    for q in range(2):
                        ab_kept.free(pe, 2 * c8 + q)
                        for cc in range(4):
                            last = pe.transpose(chip.banks[:, 4 + q, cc * P:(cc + 1) * P],
                                                chip.ab[:, :, half, 8 * c8 + 4 * q + cc], chip.ident[:, :])
                        ab_turned.done(last)

                turn(0)
                for c8 in range(C // 8):
                    if c8 + 1 < C // 8:
                        turn(c8 + 1)
                    ab_kept.ready(pe, 2 * c8 + 1)
                    spread.ready(pe, c8)
                    for q in range(2):
                        stored.free(pe, 2 * c8 + q)
                        for cc in range(4):
                            last = pe.matmul(chip.banks[:, 6 + q, cc * P:(cc + 1) * P], ab2t[:, c8 % 2, 4 * q + cc, :],
                                             pairs[:, c8 % 2, 4 * q + cc, :], start=True, stop=True)
                        summed.done(last)
    return chunk_in if raw_pairs else None


def protein_sums(nc, chip, tag, par, raw_pairs, chunk_in=None):
    pp = chunk_buffers(chip)
    per_chunk = ICS * C // G
    ppv = par["protein"][0]
    with chip.phase(f"{tag}_protein"):
        if raw_pairs:
            pp_in = [chunk_in, chip.sem("pp_in1")]
        else:
            (gate_w, _), (lin_w, lin_b) = par["gates"][1], par["lins"][1]
            small = Carve(chip.small)
            scratch = Carve(chip.work[:, 0:ICS * C * C])
            stream = PairStream(chip, small, small, gate_w, lin_w, lin_b, par["ln_w"], scratch=scratch)
        blocked = Flow(chip, "blocked", 16)
        summed = Flow(chip, "summed", 4)

        def where(m, u, h):
            kc = u % 2
            return kc, (m - kc) * 2

        with nc.Block() as block:
            @block.sync
            def _(sp):
                if raw_pairs:
                    for q in range(1, 2 * ICS):
                        blocked.free(sp, q * 8 + 7)
                        load_chunk(sp, pp, ppv, q // 2, q % 2, pp_in[q % 2])
                    return
                stream.lin.load(sp)
                with sp.Fori(0, ICS) as ic:
                    for h in range(2):
                        def load(m, u):
                            kc, i = where(m, u, h)
                            src = ppv[bass.ds(ic * P + (i + h * C), G), kc * P:(kc + 1) * P, :]
                            stream.load(sp, [(0, src.rearrange("i k e -> k i e"))], (ic * 2 + h) * per_chunk + m, u)
                        engine_loop(sp, per_chunk, 4, [(load, 0)])

            @block.gpsimd
            def _(pool):
                if not raw_pairs:
                    stream.norm.open_pool(pool)
                    engine_loop(pool, 4 * per_chunk, 4, [(lambda n, u: stream.norm.rstd(pool, n, u), 0)])

            @block.vector
            def _(dve):
                summed.open(dve)
                if not raw_pairs:
                    stream.gated.open(dve)
                    stream.lin.fold(dve)
                with dve.Fori(0, ICS) as ic:
                    for h in range(2):
                        if not raw_pairs:
                            base = (ic * 2 + h) * per_chunk

                            def gate(m, u):
                                kc, i = where(m, u, h)
                                stream.gate(dve, pp[:, 1 - h, kc, bass.ds(i, G), :], base + m, u)
                            engine_loop(dve, per_chunk, 4, [(lambda m, u: stream.stats(dve, base + m, u), 0),
                                                            (lambda m, u: stream.apply(dve, base + m, u), 1), (gate, 4)])
                        rows = slice(h * C, (h + 1) * C)
                        for c8 in range(C // 8):
                            n = (ic * 2 + h) * 8 + c8
                            sums = chip.ab[rows, bass.ds(ic * NC_, NC_), 1, c8 * 8:(c8 + 1) * 8]
                            blocked.ready(dve, n)
                            summed.done(dve.tensor_tensor(
                                sums, chip.banks[rows, 4 + c8 % 4, :].rearrange("p (c j) -> p j c", c=8), sums, ALU.add))

            @block.scalar
            def _(act):
                if raw_pairs:
                    return
                stream.norm.open_act(act)
                with act.Fori(0, ICS) as ic:
                    for h in range(2):
                        base = (ic * 2 + h) * per_chunk
                        blocked.free(act, (ic * 2 + h) * 8 + 7)

                        def squash(m, u):
                            kc, i = where(m, u, h)
                            stream.squash(act, pp[:, 1 - h, kc, bass.ds(i, G), :], base + m, u)
                        engine_loop(act, per_chunk, 4, [(lambda m, u: stream.apply_act(act, base + m, u), 0),
                                                        (lambda m, u: stream.keep(act, base + m, u), 1), (squash, 2)])

            @block.tensor
            def _(pe):
                blocked.open(pe)
                if not raw_pairs:
                    stream.norm.open_pe(pe)
                    stream.projected.open(pe)
                    stream.lin.shift(pe)
                    stream.lin.await_ready(pe)
                with pe.Fori(0, ICS) as ic:
                    for h in range(2):
                        if raw_pairs:
                            pe.wait_ge(pp_in[h], (ic + 1) * (16 * ICS * C // ROWS))
                        else:
                            base = (ic * 2 + h) * per_chunk
                            engine_loop(pe, per_chunk, 4, [(lambda m, u: stream.norm.turn(pe, base + m, u), 0),
                                                           (lambda m, u: stream.project(pe, base + m, u), 1)])
                            stream.gated.ready(pe, base + (per_chunk - 1))
                        for c8 in range(C // 8):
                            n = (ic * 2 + h) * 8 + c8
                            summed.free(pe, n)
                            for cc in range(8):
                                c = c8 * 8 + cc
                                for kc in range(ICS):
                                    last = pe.matmul(chip.banks[h * C:(h + 1) * C, 4 + c8 % 4, cc * NC_:(cc + 1) * NC_],
                                                     pp[:, 1 - h, kc, :, c], chip.ab[:, kc * NC_:(kc + 1) * NC_, 0, c],
                                                     start=kc == 0, stop=kc == ICS - 1)
                            blocked.done(last)


RING = 8


def combine(nc, chip, tag, par, src, follow):
    small = Carve(chip.small)
    before = chip.work[:, 12288:].rearrange("p (s g e) -> p s g e", s=RING, g=G)
    with chip.phase(f"{tag}_combine"):
        norm = Norm(chip, small, (EPS_LN,), banks=(0, 1), width=C, by_act=3)
        lin = Linear(chip, small, "w", [par["out"][0]], [(par["out"][1], E)], par["lnc_w"], par["lnc_b"], bank=2, copies=2)
        before_in = [chip.sem(f"before_in{k}") for k in range(RING)]
        w_pair = small(2 * E)
        paired = chip.sem("paired")
        projected = Flow(chip, "projected", 2)
        gated = Flow(chip, "gated", 4)
        added = Flow(chip, "added", RING)
        chip.tag = f"{tag}_follow"
        follow.begin(Carve(chip.work[:, 0:12288]), added)

        def group(n):
            return chip.x[:, bass.ds(n * G, G), :]

        def sums(n):
            return chip.ab[:, bass.ds(n * G, G), 1, :]

        def update(u):
            return chip.bank(4 + u % 4)

        with nc.Block() as block:
            @block.sync
            def _(sp):
                lin.load(sp)
                follow.load(sp)
                for ic in range(ICS):
                    with sp.Fori(0, GROUPS // ICS // RING) as i:
                        for u in range(RING):
                            n = i * RING + (u + ic * (GROUPS // ICS))
                            added.free(sp, n)
                            sp.dma_start(before[:, u, :, :], src[:, ic, bass.ds((i * RING + u) * G, G), :]
                                         ).then_inc(before_in[u], 16)
                            follow.store(sp, n)
                follow.close(sp)

            @block.gpsimd
            def _(pool):
                norm.open_pool(pool)
                added.open(pool)
                follow.open_pool(pool)

                def add(n, u):
                    pool.wait_ge(before_in[u], 2 * n + (16 - 2 * u))
                    pool.sem_inc(norm.paced, 1)
                    gated.ready(pool, n)
                    added.done(pool.tensor_tensor(group(n), group(n), before[:, u, :, :], ALU.add))
                engine_loop(pool, GROUPS, RING, [(lambda n, u: norm.rstd(pool, n, u % 2), 0), (add, 4)]
                            + follow.gpsimd(pool))

            @block.vector
            def _(dve):
                gated.open(dve)
                dve.memset(w_pair, 0.0).then_inc(paired, 1)
                lin.fold(dve)
                dve.wait_ge(paired, 1)
                dve.wait_ge(lin.folded, 1)
                for h in range(2):
                    last = dve.tensor_copy(w_pair[h * C:(h + 1) * C, h * E:(h + 1) * E], lin.w[h * C:(h + 1) * C, :])
                last.then_inc(paired, 1)
                follow.open_vector(dve)

                def gate(n, u):
                    projected.ready(dve, n)
                    gated.done(dve.tensor_tensor(group(n), update(u).rearrange("p (g e) -> p g e", g=G), group(n),
                                                 ALU.mult))
                engine_loop(dve, GROUPS, 4, [(lambda n, u: norm.stats(dve, sums(n), n, u % 2), 0),
                                             (lambda n, u: norm.apply(dve, sums(n), n, u % 2), 1), (gate, 3)]
                            + follow.vector(dve))

            @block.scalar
            def _(act):
                norm.open_act(act)
                follow.open_scalar(act)

                def keep(n, u):
                    projected.free(act, n)
                    norm.keep(act, n, u % 2)
                engine_loop(act, GROUPS, 4, [(lambda n, u: norm.apply_act(act, sums(n), n, u % 2), 0), (keep, 1)]
                            + follow.scalar(act))

            @block.tensor
            def _(pe):
                norm.open_pe(pe)
                projected.open(pe)
                lin.shift(pe)
                lin.await_ready(pe)
                pe.wait_ge(paired, 2)
                follow.open_tensor(pe)

                def project(n, u):
                    norm.kept.ready(pe, n)
                    gated.free(pe, n)
                    pe.matmul(update(u).rearrange("p (g n) -> p g n", g=G), chip.ones3[:, :],
                              lin.bias3.unsqueeze(1).to_broadcast([3, G, E]), start=True, stop=False)
                    for k in range(2):
                        last = pe.matmul(update(u)[:, k * 2 * E:(k + 1) * 2 * E], norm.zt[:, u % 2, k * P:(k + 1) * P],
                                         w_pair, start=False, stop=k == 1)
                    projected.done(last)
                engine_loop(pe, GROUPS, 4, [(lambda n, u: norm.turn(pe, n, u % 2), 0), (project, 1)] + follow.tensor(pe))


class TurnTokens:

    def __init__(self, chip):
        self.chip = chip
        self.xt = chip.ab[:, :, :, :].rearrange("p t s c -> p t (s c)")

    def group(self, n):
        return self.chip.x[:, bass.ds(n * G, G), :]

    def begin(self, carve, complete):
        self.complete = complete
        self.norm = Norm(self.chip, carve, (EPS_LN,), banks=(2, 3), depth=4, by_act=2)

    def load(self, sp):
        pass

    def store(self, sp, n):
        pass

    def close(self, sp):
        pass

    def open_pool(self, pool):
        self.norm.open_pool(pool)

    def open_vector(self, dve):
        pass

    def open_scalar(self, act):
        self.norm.open_act(act)

    def open_tensor(self, pe):
        self.norm.open_pe(pe)

    def gpsimd(self, pool):
        return [(lambda n, u: self.norm.rstd(pool, n, u % 4), 7)]

    def vector(self, dve):
        def stats(n, u):
            self.complete.ready(dve, n)
            dve.sem_inc(self.norm.paced, 1)
            self.norm.stats(dve, self.group(n), n, u)
        return [(stats, 6), (lambda n, u: self.norm.apply(dve, self.group(n), n, u), 8)]

    def scalar(self, act):
        def keep(n, u):
            self.norm.keep(act, n, u, out=self.xt[:, bass.ds(n * G, G), :].rearrange("p g n -> p (g n)"))
        return [(lambda n, u: self.norm.apply_act(act, self.group(n), n, u), 8), (keep, 10)]

    def tensor(self, pe):
        return [(lambda n, u: self.norm.turn(pe, n, u), 9)]


SLOT = G * P
SLOTS = 2 * NP_ * NC_ // SLOT + EXPERTS
TAIL = 2
ROW = E + TAIL
PACK = HID + HC * E + HC + E // 2
NOWHERE = 1 << 20


class Router(TurnTokens):

    def __init__(self, chip, mixture, p):
        self.chip, self.mixture, self.p = chip, mixture, p

    def begin(self, carve, complete):
        chip, self.complete = self.chip, complete
        carve.at = self.mixture.tables
        self.norm = Norm(chip, carve, (EPS_LN,), banks=(2, 2), depth=4, by_act=2)
        self.logits = chip.banks[:, 3, 0:G * EXPERTS].rearrange("p (g e) -> p g e", g=G)
        self.wr = carve(EXPERTS)
        self.empty = carve(SLOTS * SLOT // P // GROUPS, ROW)
        self.mhalf, self.mhalf_made = carve(G), chip.sem("mhalf")
        self.w_in, self.emptied, self.cleared = chip.sem("w_in"), chip.sem("emptied"), chip.sem("cleared")
        self.routed = Flow(chip, "routed", 2)
        self.scored = Flow(chip, "scored", 1)
        self.kept_scales = Flow(chip, "kept_scales")
        self.scales = Flow(chip, "scales")

    def load(self, sp):
        sp.dma_start(self.wr, self.p["Wr"]).then_inc(self.w_in, 16)
        sp.wait_ge(self.emptied, 2)

    def store(self, sp, n):
        rows = self.mixture.sorted.rearrange("(k p n) w -> p k n w", p=P, k=GROUPS)
        sp.dma_start(rows[:, bass.ds(n, 1), :, :].rearrange("p k n w -> p (k n) w"), self.empty
                     ).then_inc(self.cleared, 16)

    def close(self, sp):
        sp.wait_ge(self.cleared, 16 * GROUPS)

    def open_pool(self, pool):
        self.norm.open_pool(pool)
        pool.memset(self.mhalf, -0.5).then_inc(self.mhalf_made, 1)
        pool.wait_ge(self.mhalf_made, 1)

    def open_vector(self, dve):
        dve.memset(self.empty, 0.0).then_inc(self.emptied, 1)
        dve.wait_ge(self.emptied, 1)
        dve.memset(self.empty[:, :, E + 1:ROW].bitcast(U32), NOWHERE).then_inc(self.emptied, 1)

    def open_tensor(self, pe):
        self.norm.open_pe(pe)
        self.routed.open(pe)
        pe.wait_ge(self.w_in, 16)

    def gpsimd(self, pool):
        def both(n, u):
            self.kept_scales.ready(pool, n)
            scale = self.mixture.scale[:, bass.ds(n * G, G)]
            self.scales.done(pool.tensor_tensor(scale, scale, self.mhalf, ALU.pow))
        return super().gpsimd(pool) + [(both, 9)]

    def vector(self, dve):
        def keep_scales(n, u):
            at = bass.ds(n * G, G)
            dve.tensor_copy(self.mixture.mean[:, at], self.norm.mv[:, u, :, 0])
            self.kept_scales.done(dve.tensor_scalar(self.mixture.scale[:, at], self.norm.mv[:, u, :, 1],
                                                    1.0 + EPS_LN, EPS_LN * EPS_LN, ALU.mult, ALU.add))

        return super().vector(dve) + [(keep_scales, 8)]

    def scalar(self, act):
        def keep(n, u):
            self.routed.free(act, n)
            self.norm.keep(act, n, u)

        def score(n, u):
            self.routed.ready(act, n)
            self.scored.done(act.copy(self.mixture.logits[:, bass.ds(n * G, G), :], self.logits))
        return [(score, 12), (lambda n, u: self.norm.apply_act(act, self.group(n), n, u), 8), (keep, 10)]

    def open_scalar(self, act):
        super().open_scalar(act)
        self.scored.open(act)

    def tensor(self, pe):
        def logit(n, u):
            self.norm.kept.ready(pe, n)
            self.scored.free(pe, n)
            for t in range(G):
                last = pe.matmul(self.logits[:, t, :], self.norm.zt[:, u % 2, t * P:(t + 1) * P], self.wr,
                                 start=True, stop=True)
            self.routed.done(last)
        return super().tensor(pe) + [(logit, 11)]


class Mixture:

    def __init__(self, nc, chip, p):
        self.nc, self.chip, self.p = nc, chip, p
        self.sorted = nc.dram_tensor("sorted_tokens", (SLOTS * SLOT, ROW), F32).ap()
        self.out = nc.dram_tensor("choices", (NP_ * NC_ * 2, E), F32).ap()
        ab = Carve(chip.ab[:, :, :, :].rearrange("p t s c -> p (t s c)"))
        self.pack = ab(EXPERTS, PACK)
        self.ab_rest = chip.ab[:, :, :, :].rearrange("p t s c -> p (t s c)")[:, ab.at:]
        small = Carve(chip.small)
        self.expert = small(SLOTS, dt=I32)
        self.small_rest = chip.small[:, small.at:]
        work = Carve(chip.work)
        self.mean, self.scale = work(TILES), work(TILES)
        self.tail = work(TILES, 2, TAIL)
        self.place = work(TILES, 2, dt=U32)
        self.work_rest = chip.work[:, work.at:]
        self.logits = self.work_rest[:, 0:TILES * EXPERTS].rearrange("p (t e) -> p t e", e=EXPERTS)
        self.tables = work.at + TILES * EXPERTS

    def w1(self, e):
        return self.pack[:, e, 0:HID]

    def w2(self, e):
        return self.pack[:, e, HID:HID + HC * E]

    def b1(self, e):
        return self.pack[:, e, HID + HC * E:HID + HC * E + HC]

    def b2(self, e):
        return self.pack[0:3, e, HID + HC * E + HC:PACK].bitcast(BF16)

    def group(self, n):
        return self.chip.x[:, bass.ds(n * G, G), :]

    def choose(self):
        nc, chip, p = self.nc, self.chip, self.p
        T = TILES
        with chip.phase("choose"):
            work = Carve(self.work_rest)
            logits, br = work(T, EXPERTS), work(EXPERTS)
            same, rest, at = work(T, EXPERTS), work(T, EXPERTS), work(T, EXPERTS)
            pick = [work(T, EXPERTS) for _ in range(2)]
            best = [work(T) for _ in range(2)]
            which, lead, share = work(T), work(T), work(T)
            chosen = work(T, EXPERTS, dt=BF16)
            before_f, before, ones = work(P), work(P, dt=BF16), work(P, dt=BF16)
            lane8 = work(EXPERTS)
            steps = work(NP_ * NC_ // SLOT)
            slot_no = work(SLOTS)
            place_out = work(T, 2)
            sofar = work(EXPERTS, T)
            fills = work(EXPERTS, NP_ * NC_ // SLOT)
            slots, ends, base = work(EXPERTS), work(EXPERTS), work(EXPERTS)
            done = work(SLOTS, EXPERTS)
            zeros = work(T)
            expert = work(SLOTS)
            made, led, bounded, counted, picked = (chip.sem(s) for s in ("made", "led", "bounded", "counted", "picked"))
            chain = Chain(chip, "chain")
            b_in = chip.sem("b_in")

            def by_token(v):
                return v.unsqueeze(2).to_broadcast([P, T, EXPERTS])

            def by_expert(v):
                return v.unsqueeze(1).to_broadcast([P, T, EXPERTS])

            with nc.Block() as block:
                @block.sync
                def _(sp):
                    sp.dma_start(br, row(p["br"]).to_broadcast([P, EXPERTS])).then_inc(b_in, 16)

                @block.gpsimd
                def _(pool):
                    def iota(out, pattern, base, step):
                        pool.iota(out, pattern=pattern, base=base, channel_multiplier=step,
                                  allow_small_or_imprecise_dtypes=True)
                    iota(lane8, [[1, EXPERTS]], -EXPERTS, 0)
                    iota(steps, [[SLOT, NP_ * NC_ // SLOT]], 0, 0)
                    iota(slot_no, [[1, SLOTS]], 0, 0)
                    iota(place_out, [[2, T], [1, 2]], 0, 2 * T)
                    pool.memset(before_f, 1.0).then_inc(made, 1)
                    pool.wait_ge(made, 1)
                    pool.affine_select(out=before_f, in_=before_f, compare_op=ALU.is_gt, fill=0.0, base=0,
                                       pattern=[[1, P]], channel_multiplier=-1).then_inc(made, 1)

                @block.vector
                def _(dve):
                    c = chain.on(dve)
                    dve.memset(ones, 1.0)
                    dve.memset(zeros, 0.0)
                    dve.wait_ge(b_in, 16)
                    c(dve.tensor_tensor(logits, logits, by_expert(br), ALU.add))
                    dve.wait_ge(made, 2)
                    c(dve.tensor_copy(before, before_f))
                    src = logits
                    for k in range(2):
                        c(dve.tensor_reduce(best[k], src, AX.X, ALU.max))
                        c(dve.tensor_tensor(same, src, by_token(best[k]), ALU.is_equal))
                        c(dve.tensor_tensor(same, same, by_expert(lane8), ALU.mult))
                        c(dve.tensor_reduce(which, same, AX.X, ALU.min))
                        c(dve.tensor_tensor(pick[k], by_expert(lane8), by_token(which), ALU.is_equal))
                        if k == 0:
                            c(dve.scalar_tensor_tensor(rest, pick[k], -1e30, logits, ALU.mult, ALU.add))
                            src = rest
                    dve.tensor_tensor(chosen, pick[0], pick[1], ALU.add).then_inc(picked, 1)
                    dve.tensor_tensor(lead, best[0], best[1], ALU.subtract).then_inc(led, 1)
                    dve.wait_ge(counted, 1)
                    for h in range(2):
                        part = slice(h * T // 2, (h + 1) * T // 2)
                        counts = chip.banks[:, 2 + h, :].rearrange("p (t e) -> p t e", e=EXPERTS)
                        c(dve.tensor_copy(same[:, part, :], counts))
                        c(dve.tensor_tensor(at[:, part, :], chip.banks[:, h, :].rearrange("p (t e) -> p t e", e=EXPERTS),
                                            same[:, part, :], ALU.subtract))
                    for e in range(EXPERTS):
                        last = dve.tensor_tensor_scan(sofar[:, e, :], same[:, :, e], zeros, 0.0, ALU.add, ALU.add)
                    c(last)
                    c(dve.tensor_tensor(fills, sofar[:, :, T - 1:T].to_broadcast([P, EXPERTS, NP_ * NC_ // SLOT]),
                                        steps.unsqueeze(1).to_broadcast([P, EXPERTS, NP_ * NC_ // SLOT]), ALU.is_gt))
                    c(dve.tensor_reduce(slots, fills, AX.X, ALU.add))
                    c(dve.tensor_tensor_scan(ends, slots, zeros[:, 0:EXPERTS], 0.0, ALU.add, ALU.add))
                    c(dve.tensor_tensor(base, ends, slots, ALU.subtract))
                    c(dve.tensor_scalar(base, base, float(SLOT), None, ALU.mult))
                    c(dve.tensor_tensor(done, slot_no.unsqueeze(2).to_broadcast([P, SLOTS, EXPERTS]),
                                        ends.unsqueeze(1).to_broadcast([P, SLOTS, EXPERTS]), ALU.is_ge))
                    c(dve.tensor_reduce(expert, done, AX.X, ALU.add))
                    c(dve.tensor_scalar(expert, expert, float(EXPERTS - 1), None, ALU.min))
                    dve.tensor_copy(self.expert, expert)
                    c(dve.tensor_tensor(at, at, sofar.rearrange("p e t -> p t e"), ALU.add))
                    c(dve.tensor_tensor(at, at, by_expert(base), ALU.add))
                    for k in range(2):
                        c(dve.tensor_tensor(same, at, pick[k], ALU.mult))
                        c(dve.tensor_reduce(which, same, AX.X, ALU.add))
                        dve.tensor_copy(self.place[:, :, k], which)
                        dve.tensor_copy(self.tail[:, :, k, 1].bitcast(U32), place_out[:, :, k])
                    dve.wait_ge(bounded, 1)
                    for k, sign in enumerate((0.5, -0.5)):
                        dve.tensor_scalar(self.tail[:, :, k, 0], share, sign, 0.5, ALU.mult, ALU.add)

                @block.scalar
                def _(act):
                    act.wait_ge(led, 1)
                    act.activation(share, lead, ACT.Tanh, scale=0.5).then_inc(bounded, 1)

                @block.tensor
                def _(pe):
                    pe.wait_ge(picked, 1)
                    flat = chosen.rearrange("p t e -> p (t e)")
                    for m, w in enumerate((before, ones)):
                        for h in range(2):
                            last = pe.matmul(chip.bank(2 * m + h), w, flat[:, h * 512:(h + 1) * 512], start=True, stop=True)
                    last.then_inc(counted, 1)

    def dispatch(self):
        nc, chip, p = self.nc, self.chip, self.p
        with chip.phase("dispatch"):
            work = Carve(self.work_rest)
            rows = work(2, G, 2, ROW)
            where = work(2, G, 2, dt=U32)
            total, left = work(EXPERTS * E, parts=1), work(EXPERTS * E, parts=1)
            pieces = [work(EXPERTS * E, parts=1, dt=BF16) for _ in range(3)]
            w_in, b_in, shifted, cut, spread = (chip.sem(s) for s in ("w_in", "b_in", "shifted", "cut", "spread"))
            prep = Chain(chip, "prep")
            built = Flow(chip, "built")
            paced, paced_pool = chip.sem("paced"), chip.sem("paced_pool")
            sent = [chip.sem(f"sent{u}") for u in range(2)]

            with nc.Block() as block:
                @block.sync
                def _(sp):
                    sp.dma_start(total, p["b2"].rearrange("(a e) d -> a (e d)", a=1)).then_inc(b_in, 16)
                    for e in range(EXPERTS):
                        sp.dma_start(self.w1(e), p["W1"][e]).then_inc(w_in, 16)
                        sp.dma_start(self.w2(e).rearrange("p (h d) -> p h d", d=E),
                                     p["W2"][e].rearrange("(h p) d -> p h d", p=P)).then_inc(w_in, 16)
                    sp.wait_ge(cut, 1)
                    for e in range(EXPERTS):
                        for k in range(3):
                            sp.dma_start(self.b2(e)[k:k + 1, :], pieces[k][:, e * E:(e + 1) * E]).then_inc(spread, 16)
                    sp.wait_ge(spread, 16 * 3 * EXPERTS)

                @block.tensor
                def _(pe):
                    pe.wait_ge(w_in, 32 * EXPERTS)
                    for e in range(EXPERTS):
                        for h in range(HC):
                            last = pe.matmul(chip.banks[:, 4, e * HC + h:e * HC + h + 1],
                                             self.w1(e)[:, h * P:(h + 1) * P],
                                             col(chip, "moe_b", e), start=True, stop=True)
                    last.then_inc(shifted, 1)

                @block.vector
                def _(dve):
                    def prepare():
                        c = prep.on(dve)
                        dve.wait_ge(shifted, 1)
                        dve.tensor_tensor(self.pack[:, :, HID + HC * E:HID + HC * E + HC],
                                          chip.banks[:, 4, 0:EXPERTS * HC].rearrange("p (e h) -> p e h", e=EXPERTS),
                                          chip.cols[:, COL["moe_b1"]:COL["moe_b1"] + EXPERTS * HC]
                                          .rearrange("p (e h) -> p e h", e=EXPERTS), ALU.add)
                        for e in range(EXPERTS):
                            dve.tensor_scalar(self.w1(e), self.w1(e), col(chip, "moe_g", e), None, ALU.mult)
                        dve.wait_ge(b_in, 16)
                        for k in range(3):
                            piece = dve.tensor_copy(pieces[k], total)
                            if k == 2:
                                piece.then_inc(cut, 1)
                            else:
                                c(piece)
                                c(dve.tensor_tensor(left, total, pieces[k], ALU.subtract))
                                c(dve.tensor_copy(total, left))

                    dve.memset(self.pack[:, :, HID + HC * E + HC:PACK], 0.0)

                    PEEL = 4

                    def build(n, u):
                        if not isinstance(n, int) or n >= 2:
                            dve.wait_ge(sent[u], (n - u) * (2 * G * 16 // 2))
                            dve.sem_inc(paced, 1)
                        dve.tensor_copy(where[:, u, :, :], self.place[:, bass.ds(n * G, G), :])
                        dve.tensor_copy(rows[:, u, :, :, E:ROW], self.tail[:, bass.ds(n * G, G), :, :])
                        for t in range(G):
                            tile = n * G + t
                            last = dve.tensor_scalar(rows[:, u, t, :, 0:E],
                                                     chip.x[:, bass.ds(tile, 1), :].to_broadcast([P, 2, E]),
                                                     self.mean[:, bass.ds(tile, 1)], self.scale[:, bass.ds(tile, 1)],
                                                     ALU.subtract, ALU.mult)
                        built.done(last)
                        if isinstance(n, int) and n == PEEL - 1:
                            prepare()
                    engine_loop(dve, GROUPS, 2, [(build, 0)], peel=PEEL)

                @block.gpsimd
                def _(pool):
                    def send(n, u):
                        built.ready(pool, n)
                        pool.sem_inc(paced_pool, 1)
                        for t in range(G):
                            for k in range(2):
                                pool.indirect_dma_start(
                                    out=self.sorted,
                                    out_offset=bass.IndirectOffsetOnAxis(ap=where[:, u, t, k:k + 1], axis=0),
                                    in_=rows[:, u, t, k, :], in_offset=None).then_inc(sent[u], 16)
                    engine_loop(pool, GROUPS, 2, [(send, 0)])
                    for u in range(2):
                        pool.wait_ge(sent[u], 16 * 8 * GROUPS // 2)

    def experts(self):
        nc, chip = self.nc, self.chip
        chip.give_work()
        with chip.phase("experts"), ExitStack() as own:
            def split(name, *dims):
                return [own.enter_context(nc.sbuf_tensor(f"{name}_{part}", [P, *dims], F32R)) for part in ("hi", "lo")]

            w1, z = split("w1", 2, HID), split("z", 2, G * P)
            hidden = own.enter_context(nc.sbuf_tensor("hidden", [P, 2, HC, G * P], F32))
            w2 = own.enter_context(nc.sbuf_tensor("w2", [P, 2, HID], F32))
            ab, small = Carve(self.ab_rest), Carve(self.small_rest)
            rows = ab(8, G, ROW)
            y = ab(4, G, P)
            bias = ab(4, PACK - 2 * HID)
            now = small(2, dt=I32)
            rows_in = [chip.sem(f"rows_in{u}") for u in range(8)]
            sent = [chip.sem(f"sent{u}") for u in range(4)]
            named = Flow(chip, "named")
            paced, paced_act, paced_pool = (chip.sem(f"paced_{k}") for k in ("vector", "scalar", "gpsimd"))
            w1_hi = Flow(chip, "w1_hi")
            w1_ready, w2_ready = Flow(chip, "w1_ready"), Flow(chip, "w2_ready")
            turned = Flow(chip, "turned")
            z_hi = Flow(chip, "z_hi")
            z_lo = Flow(chip, "z_lo", 2)
            lifted = Flow(chip, "lifted", 2 * HC)
            bent = Flow(chip, "bent", HC)
            lowered = Flow(chip, "lowered", 2)
            mixed = Flow(chip, "mixed", 2)

            with nc.Block() as block:
                @block.sync
                def _(sp):
                    def load(s, u):
                        if not isinstance(s, int) or s >= 8:
                            sp.wait_ge(sent[u % 4], (s - (4 + u % 4)) * (G * 16 // 4))
                        sp.dma_start(rows[:, u, :, :], self.sorted[bass.ds(s * SLOT, SLOT), :]
                                     .rearrange("(g p) w -> p g w", p=P)).then_inc(rows_in[u], 16)
                    engine_loop(sp, SLOTS, 8, [(load, 0)], peel=8)

                @block.vector
                def _(dve):
                    z_lo.open(dve)

                    def weights(s, u, at):
                        dve.sem_inc(paced, 1)
                        e = dve.value_load(now[0:1, u % 2:u % 2 + 1], min_val=0, max_val=EXPERTS - 1)
                        return e, self.pack[:, bass.ds(e, 1), at:at + HID].rearrange("p a n -> p (a n)")

                    def first_weights(s, u):
                        named.done(dve.tensor_copy(now[0:1, u % 2:u % 2 + 1], self.expert[0:1, bass.ds(s, 1)]))
                        lifted.free(dve, s * HC + (HC - 1))
                        named.ready(dve, s)
                        e, whole = weights(s, u, 0)
                        w1_hi.done(dve.tensor_copy(w1[0][:, u % 2, :], whole))
                        w1_hi.ready(dve, s)
                        dve.tensor_tensor(w1[1][:, u % 2, :], whole, w1[0][:, u % 2, :].bitcast(F32), ALU.subtract)
                        w1_ready.done(dve.tensor_copy(bias[:, u % 4, :], self.pack[:, bass.ds(e, 1), 2 * HID:PACK]
                                                      .rearrange("p a n -> p (a n)")))

                    def second_weights(s, u):
                        lowered.free(dve, s)
                        w2_ready.done(dve.tensor_copy(w2[:, u % 2, :], weights(s, u, HID)[1]))

                    def low_z(s, u):
                        z_hi.ready(dve, s)
                        z_lo.done(dve.tensor_tensor(z[1][:, u % 2, :], chip.bank(6 + u % 2),
                                                    z[0][:, u % 2, :].bitcast(F32), ALU.subtract))

                    engine_loop(dve, SLOTS, 8, [(first_weights, 0), (low_z, 0), (second_weights, 1)])

                @block.gpsimd
                def _(pool):
                    def send(s, u):
                        mixed.ready(pool, s)
                        pool.sem_inc(paced_pool, 1)
                        for t in range(G):
                            pool.indirect_dma_start(
                                out=self.out,
                                out_offset=bass.IndirectOffsetOnAxis(ap=rows[:, u, t, E + 1:ROW].bitcast(U32), axis=0),
                                in_=y[:, u % 4, t, :], in_offset=None, bounds_check=2 * NP_ * NC_ - 1,
                                oob_is_err=False).then_inc(sent[u % 4], 16)
                    engine_loop(pool, SLOTS, 8, [(send, 0)])
                    for u in range(4):
                        pool.wait_ge(sent[u], G * 16 * SLOTS // 4)

                @block.scalar
                def _(act):
                    bent.open(act)
                    mixed.open(act)

                    def high_z(s, u):
                        lifted.free(act, s * HC + (HC - 1))
                        turned.ready(act, s)
                        z_hi.done(act.copy(z[0][:, u % 2, :], chip.bank(6 + u % 2)))

                    def bend(s, u):
                        w1_ready.ready(act, s)
                        lowered.free(act, s)
                        act.sem_inc(paced_act, 1)
                        for h in range(HC):
                            lifted.ready(act, s * HC + h)
                            bent.done(act.activation(hidden[:, u % 2, h, :], chip.bank(h), ACT.Gelu,
                                                     bias=bias[:, u % 4, h:h + 1]))

                    def mix(s, u):
                        if not isinstance(s, int) or s >= 4:
                            act.wait_ge(sent[u % 4], (s - u % 4) * (G * 16 // 4))
                            act.sem_inc(paced_act, 1)
                        lowered.ready(act, s)
                        for t in range(G):
                            last = act.activation(y[:, u % 4, t, :], chip.banks[:, 4 + u % 2, t * P:(t + 1) * P],
                                                  ACT.Identity, scale=rows[:, u, t, E:E + 1])
                        mixed.done(last)
                    engine_loop(act, SLOTS, 8, [(mix, 3), (high_z, 0), (bend, 1)])

                @block.tensor
                def _(pe):
                    lowered.open(pe)
                    lifted.open(pe)

                    def turn(s, u):
                        pe.wait_ge(rows_in[u], s * 2 + (16 - 2 * u))
                        z_lo.free(pe, s)
                        for t in range(G):
                            last = pe.transpose(chip.banks[:, 6 + u % 2, t * P:(t + 1) * P], rows[:, u, t, 0:E], chip.ident[:, :])
                        turned.done(last)

                    def lift(s, u):
                        z_lo.ready(pe, s)
                        w1_ready.ready(pe, s)
                        for h in range(HC):
                            bent.free(pe, s * HC + h)
                            for n, (a, b) in enumerate(((0, 0), (0, 1), (1, 0))):
                                last = pe.matmul(chip.bank(h), w1[a][:, u % 2, h * P:(h + 1) * P], z[b][:, u % 2, :],
                                                 start=n == 0, stop=n == 2)
                            lifted.done(last)

                    def lower(s, u):
                        mixed.free(pe, s)
                        w2_ready.ready(pe, s)
                        out = chip.bank(4 + u % 2)
                        b2 = bias[0:3, u % 4, HC:].bitcast(BF16)
                        pe.matmul(out.rearrange("p (g n) -> p g n", g=G), chip.ones3[:, :],
                                  b2.unsqueeze(1).to_broadcast([3, G, E]), start=True, stop=False)
                        for h in range(HC):
                            bent.ready(pe, s * HC + h)
                            for t in range(G):
                                last = pe.matmul(out[:, t * P:(t + 1) * P], hidden[:, u % 2, h, t * P:(t + 1) * P],
                                                 w2[:, u % 2, h * P:(h + 1) * P], start=False,
                                                 stop=h == HC - 1 and t == G - 1)
                        lowered.done(last)
                    engine_loop(pe, SLOTS, 8, [(turn, 0), (lift, 1), (lower, 2)])
        chip.take_work("work_again")

    def run(self):
        self.choose()
        self.dispatch()
        self.experts()


GATES = ("c", "i", "o")
UNROLL = 8
HALVES = 2
CHUNKS, STEPS = NP_, NC_


class Pass:

    def __init__(self, cell, tag, first, stores):
        self.cell, self.first, self.stores = cell, first, stores
        self.steps = STEPS - first
        chip = cell.chip
        self.summed = Flow(chip, f"{tag}_summed")
        self.opened = Flow(chip, f"{tag}_opened")
        self.read = Flow(chip, f"{tag}_read", 4)
        self.carried = Flow(chip, f"{tag}_carried")
        self.bounded = Flow(chip, f"{tag}_bounded")
        self.stepped = Flow(chip, f"{tag}_stepped")
        self.links = chip.sem(f"{tag}_links")
        self.saved = Flow(chip, f"{tag}_saved", 4)

    def each_step(self, eng, stage):
        with eng.Fori(self.first // UNROLL, STEPS // UNROLL) as i:
            for u in range(UNROLL):
                step = i * UNROLL + u
                stage(step - self.first if self.first else step, step, u % 2)

    def tensor(self, pe, base, base_h):
        cell, banks = self.cell, self.cell.chip.banks

        def bank(s, par, g):
            return banks[:, 2 * s + par, g * P:(g + 1) * P] if g < 2 else banks[:, 4 + 2 * s + par, 0:P]

        def prime(k, step, par, s):
            self.read.free(pe, base + (k * HALVES + s))
            for g, gate in enumerate(GATES):
                pe.matmul(bank(s, par, g), cell.u_w[gate], cell.xt[:, bass.ds(step + s * STEPS, 1), :]
                          .rearrange("p a n -> p (a n)"), start=g != 1, stop=False)

        def finish(k, par, s):
            self.stepped.ready(pe, base_h + (k * HALVES + s))
            for g, gate in enumerate(GATES):
                last = pe.matmul(bank(s, par, g), cell.v_w[gate], cell.h[:, 1 - par, s, :], start=False, stop=g > 0)
                if g > 0:
                    self.summed.done(last)

        def body(i, last):
            for u in range(UNROLL):
                step = i * UNROLL + u
                k = step - self.first
                for s in range(HALVES):
                    finish(k, u % 2, s)
                    if not (last and u == UNROLL - 1):
                        prime(k + 1, step + 1, (u + 1) % 2, s)

        for s in range(HALVES):
            prime(0, self.first, 0, s)
        with pe.Fori(self.first // UNROLL, STEPS // UNROLL - 1) as i:
            body(i, False)
        body(STEPS // UNROLL - 1, True)

    def scalar(self, act, base):
        cell, banks = self.cell, self.cell.chip.banks

        def stage(k, step, par):
            for s in range(HALVES):
                n = base + (k * HALVES + s)
                self.summed.ready(act, n * 2)
                act.activation(cell.g[:, s, :], banks[:, 2 * s + par, 0:P], ACT.Tanh, bias=col(cell.chip, "cell_c"))
                self.opened.done(act.activation(cell.io[:, s, 0, :], banks[:, 2 * s + par, P:2 * P], ACT.Sigmoid,
                                                bias=col(cell.chip, "cell_i")))
                self.summed.ready(act, n * 2 + 1)
                self.read.done(act.activation(cell.io[:, s, 1, :], banks[:, 4 + 2 * s + par, 0:P], ACT.Sigmoid,
                                              bias=col(cell.chip, "cell_o")))
                self.carried.ready(act, n)
                self.bounded.done(act.activation(cell.g[:, s, :], cell.c[:, s, :], ACT.Tanh))
        self.each_step(act, stage)

    def vector(self, dve, base, base_h):
        cell = self.cell

        def stage(k, step, par):
            for s in range(HALVES):
                n, nh = base + (k * HALVES + s), base_h + (k * HALVES + s)
                i, o = cell.io[:, s, 0, :], cell.io[:, s, 1, :]
                self.stepped.ready(dve, nh)
                dve.tensor_tensor(cell.hc[:, s, :], cell.h[:, 1 - par, s, :], cell.c[:, s, :], ALU.mult
                                  ).then_inc(self.links, 1)
                self.opened.ready(dve, n)
                dve.tensor_tensor(cell.ig[:, s, :], i, cell.g[:, s, :], ALU.mult).then_inc(self.links, 1)
                dve.wait_ge(self.links, n * 2 + 2)
                self.carried.done(dve.tensor_tensor(cell.c[:, s, :], cell.hc[:, s, :], cell.ig[:, s, :], ALU.add))
                self.bounded.ready(dve, n)
                if self.stores:
                    self.saved.free(dve, n)
                    dve.sem_inc(cell.paced, 1)
                self.stepped.done(dve.tensor_tensor(cell.h[:, par, s, :], o, cell.g[:, s, :], ALU.mult))
        self.each_step(dve, stage)

    def gpsimd(self, pool, base, base_h):
        cell = self.cell
        if not self.stores:
            return

        def stage(k, step, par):
            for s in range(HALVES):
                self.stepped.ready(pool, base_h + (k * HALVES + (s + HALVES)))
                self.saved.done(pool.tensor_copy(cell.hs[:, bass.ds(step + s * STEPS, 1), :].rearrange("p a n -> p (a n)"),
                                                 cell.h[:, par, s, :]))
        self.each_step(pool, stage)

    def begin(self, dve, fresh, base_h):
        cell = self.cell
        if fresh:
            dve.memset(cell.start, 0.0).then_inc(cell.begun, 1)
            dve.wait_ge(cell.begun, 1)
        else:
            ends = self.ends()
            cell.chain(dve.tensor_copy(cell.start[:, 0, 1:CHUNKS], ends[0][:, 0:CHUNKS - 1]))
            cell.chain(dve.tensor_copy(cell.start[:, 1, 1:CHUNKS], ends[1][:, 0:CHUNKS - 1]))
        dve.tensor_copy(self.ends()[1], cell.start[:, 1, :])
        for s in range(HALVES):
            self.stepped.done(dve.tensor_copy(cell.h[:, 1, s, :], cell.start[:, 0, s * P:(s + 1) * P]))

    def ends(self):
        cell = self.cell
        return (cell.h[:, 1, :, :].rearrange("p s n -> p (s n)"), cell.c.rearrange("p s n -> p (s n)"))


class Links:

    def __init__(self, sem):
        self.sem, self.eng, self.base, self.n = sem, None, 0, 0

    def at(self, eng, base):
        self.eng, self.base, self.n = eng, base, 0

    def __call__(self, ins):
        self.n += 1
        ins.then_inc(self.sem, 1)
        self.eng.wait_ge(self.sem, self.base + self.n)


class Cell:

    def __init__(self, chip):
        self.chip = chip
        carve = Carve(chip.small)
        self.u_w = {g: carve(P) for g in GATES}
        self.v_w = {g: carve(P) for g in GATES}
        self.start = carve(2, CHUNKS)
        self.h = carve(2, HALVES, P)
        self.c = carve(HALVES, P)
        self.io = carve(HALVES, 2, P)
        self.g = carve(HALVES, P)
        products = carve(2, HALVES, P)
        self.ig, self.hc = products[:, 0, :, :], products[:, 1, :, :]
        self.flag = carve(1, dt=I32)
        self.met, self.ones = carve(1), carve(1)
        self.xt = chip.ab[:, :, :, :].rearrange("p t s c -> p t (s c)")
        self.hs = chip.work[:, :].rearrange("p (t n) -> p t n", n=P)
        self.moved = self.io.rearrange("p s a n -> p (s a n)").rearrange("p (q n) -> p q n", q=2)[:, :, 0:CHUNKS - 1]
        self.size = products.rearrange("p a s n -> p a (s n)")[:, :, 0:CHUNKS - 1]
        self.paced, self.begun = chip.sem("paced"), chip.sem("begun")
        self.chain = Links(chip.sem("chain"))
        self.tested = chip.sem("tested")
        self.counted = chip.sem("counted")
        self.flagged = chip.sem("flagged")

    def compare(self, dve, run, turn):
        chain = self.chain
        ends = run.ends()
        for q in range(2):
            last = dve.tensor_tensor(self.moved[:, q, :], ends[q][:, 0:CHUNKS - 1], self.start[:, q, 1:CHUNKS],
                                     ALU.subtract)
        chain(last)
        for q in range(2):
            last = dve.tensor_tensor(self.size[:, q, :], ends[q][:, 0:CHUNKS - 1], ends[q][:, 0:CHUNKS - 1], ALU.mult)
        chain(last)
        chain(dve.tensor_tensor(self.moved, self.moved, self.moved, ALU.mult))
        chain(dve.tensor_scalar(self.size, self.size, 1.0, CHUNK_TOL ** 2, ALU.add, ALU.mult))
        chain(dve.tensor_tensor(self.moved, self.moved, self.size, ALU.is_le))
        dve.tensor_reduce(self.met, self.moved, AX.XY, ALU.min).then_inc(self.tested, 1)
        dve.wait_ge(self.counted, turn + 1)
        dve.tensor_copy(self.flag[0:1, :], self.chip.banks[0:1, 0, 0:1]).then_inc(self.flagged, 1)

    TEST_LINKS = 5

    def count(self, pe, turn):
        pe.wait_ge(self.tested, turn + 1)
        pe.matmul(self.chip.banks[0:1, 0, 0:1], self.met, self.ones, start=True, stop=True).then_inc(self.counted, 1)

    def flag_value(self, eng, turn):
        eng.wait_ge(self.flagged, turn + 1)
        eng.sem_inc(self.paced, 1)
        return eng.value_load(self.flag[0:1, 0:1], min_val=0, max_val=P)


def recur(nc, chip, p):
    with chip.phase("cell"):
        cell = Cell(chip)
        w_in, zeroed = chip.sem("w_in"), chip.sem("zeroed")
        warm = Pass(cell, "warm", STEPS - WARM, False)
        main = Pass(cell, "main", 0, True)
        more = Pass(cell, "more", 0, True)
        per, per_h = STEPS * HALVES, (STEPS + 1) * HALVES

        def rounds(eng, run, skipped=None):
            with eng.If(cell.flag_value(eng, 0) < P):
                run(0)
                with eng.If(cell.flag_value(eng, 1) < P):
                    with eng.Fori(1, CHUNKS - 2) as t:
                        with eng.If(cell.flag_value(eng, t) < P):
                            run(t)
                        with eng.Else():
                            if skipped is not None:
                                skipped()
                            else:
                                eng.sem_inc(cell.paced, 1)
                        eng.sem_inc(cell.paced, 1)
                    eng.sem_inc(cell.paced, 1)
                eng.sem_inc(cell.paced, 1)

        with nc.Block() as block:
            @block.sync
            def _(sp):
                for gate in GATES:
                    sp.dma_start(cell.u_w[gate], p[f"U_{gate}"]).then_inc(w_in, 16)
                    sp.dma_start(cell.v_w[gate], p[f"V_{gate}"]).then_inc(w_in, 16)

            @block.gpsimd
            def _(pool):
                main.saved.open(pool)
                more.saved.open(pool)
                main.gpsimd(pool, 0, 0)
                rounds(pool, lambda t: more.gpsimd(pool, t * per, t * per_h))

            @block.vector
            def _(dve):
                dve.memset(cell.ones, 1.0).then_inc(zeroed, 1)
                warm.begin(dve, True, 0)
                warm.vector(dve, 0, 0)
                cell.chain.at(dve, 0)
                warm.stepped.ready(dve, (WARM + 1) * HALVES - 1)
                main.begin(dve, False, 0)
                main.vector(dve, 0, 0)
                main.stepped.ready(dve, per_h - 1)
                cell.compare(dve, main, 0)
                main.saved.ready(dve, per - 1)

                def again(t):
                    cell.chain.at(dve, t * (2 + cell.TEST_LINKS) + (2 + cell.TEST_LINKS))
                    more.begin(dve, False, t * per_h)
                    more.vector(dve, t * per, t * per_h)
                    more.stepped.ready(dve, t * per_h + (per_h - 1))
                    cell.compare(dve, more, t + 1)
                    more.saved.ready(dve, t * per + (per - 1))
                    dve.sem_inc(cell.paced, 1)
                rounds(dve, again, skipped=lambda: dve.sem_inc(cell.flagged, 1))

            @block.scalar
            def _(act):
                for run in (warm, main, more):
                    run.read.open(act)
                warm.scalar(act, 0)
                main.scalar(act, 0)
                rounds(act, lambda t: more.scalar(act, t * per))

            @block.tensor
            def _(pe):
                pe.wait_ge(w_in, 96)
                pe.wait_ge(zeroed, 1)
                warm.tensor(pe, 0, 0)
                main.tensor(pe, 0, 0)
                cell.count(pe, 0)

                def again(t):
                    more.tensor(pe, t * per, t * per_h)
                    cell.count(pe, t + 1)
                rounds(pe, again)


def finish(nc, chip, out):
    hs = chip.work[:, :].rearrange("p (t n) -> p t n", n=P)
    carve = Carve(chip.small)
    with chip.phase("finish"):
        flat = carve(2, G, P)
        copied = Flow(chip, "copied")
        turned = Flow(chip, "turned", 2)
        added = Flow(chip, "added", 2)
        stored = [chip.sem(f"stored{u}") for u in range(2)]

        def group(n):
            return chip.x[:, bass.ds(n * G, G), :]

        with nc.Block() as block:
            @block.sync
            def _(sp):
                for ic in range(ICS):
                    with sp.Fori(0, GROUPS // ICS // 2) as i:
                        for u in range(2):
                            n = i * 2 + (u + ic * (GROUPS // ICS))
                            added.ready(sp, n)
                            sp.dma_start(out[:, ic, bass.ds((i * 2 + u) * G, G), :], group(n)).then_inc(stored[u], 16)
                for u in range(2):
                    sp.wait_ge(stored[u], 16 * GROUPS // 2)

            @block.scalar
            def _(act):
                def copy(n, u):
                    turned.free(act, n)
                    copied.done(act.copy(flat[:, u, :, :], hs[:, bass.ds(n * G, G), :]))
                engine_loop(act, GROUPS, 2, [(copy, 0)])

            @block.tensor
            def _(pe):
                turned.open(pe)

                def turn(n, u):
                    copied.ready(pe, n)
                    added.free(pe, n)
                    for t in range(G):
                        last = pe.transpose(chip.banks[:, u, t * P:(t + 1) * P], flat[:, u, t, :], chip.ident[:, :])
                    turned.done(last)
                engine_loop(pe, GROUPS, 2, [(turn, 0)])

            @block.vector
            def _(dve):
                added.open(dve)

                def add(n, u):
                    turned.ready(dve, n)
                    added.done(dve.tensor_tensor(group(n), group(n), chip.bank(u).rearrange("p (g e) -> p g e", g=G), ALU.add))
                engine_loop(dve, GROUPS, 2, [(add, 0)])


def metaformer(nc, D, out):
    tokens = "(i p) j e -> p i j e"
    x0 = D["x"][0].rearrange(tokens, p=P)
    x1 = nc.dram_tensor("after_mixture", (P, TILES, E), F32).ap()
    with ExitStack() as ctx:
        chip = Chip(nc, ctx)
        setup(nc, chip, setup_par(D))
        par = conv_par(chip, D, "l0")
        project_tokens(nc, chip, "l0", par, x0)
        compound_sums(nc, chip, "l0", par, False)
        protein_sums(nc, chip, "l0", par, False)
        chip.recycle()
        ffn = {k.removeprefix("L0_ffn_"): v for k, v in D.items() if k.startswith("L0_ffn_")}
        mixture = Mixture(nc, chip, ffn)
        combine(nc, chip, "l0", par, x0, Router(chip, mixture, ffn))
        mixture.run()
        chip.recycle()
        par = conv_par(chip, D, "l1")
        project_tokens(nc, chip, "l1", par, None, mixture.out.rearrange("(p t k) e -> p t k e", p=P, k=2), x1)
        chunk_in = compound_sums(nc, chip, "l1", par, True)
        protein_sums(nc, chip, "l1", par, True, chunk_in)
        combine(nc, chip, "l1", par, x1.rearrange("p (i j) e -> p i j e", i=ICS), TurnTokens(chip))
        recur(nc, chip, {k.removeprefix("L1_ffn_"): v for k, v in D.items() if k.startswith("L1_ffn_")})
        finish(nc, chip, out[0].rearrange(tokens, p=P))


def setup_par(D):
    return {"l0_ln_w": D["L0_conv_ln_w"], "l1_ln_w": D["L1_conv_ln_w"], "l1_ln_b": D["L1_conv_ln_b"],
            "l0_lnc_w": D["L0_conv_lnc_w"], "l1_lnc_w": D["L1_conv_lnc_w"], "l1_lnc_b": D["L1_conv_lnc_b"],
            "moe_ln_g": D["L0_ffn_ln_g"], "moe_ln_b": D["L0_ffn_ln_b"], "moe_b1": D["L0_ffn_b1"],
            "cell_c": D["L1_ffn_b_c"], "cell_i": D["L1_ffn_b_i"], "cell_o": D["L1_ffn_b_o"]}


def conv_par(chip, D, layer):
    if layer == "l0":
        q = {k.removeprefix("L0_conv_"): v for k, v in D.items() if k.startswith("L0_conv_")}
        return {"gates": [(q["gw1"], None), (q["gw2"], None)], "lins": [(q["w1"], q["b1"]), (q["w2"], q["b2"])],
                "edge": (q["we"], q["be"]), "out": (q["ws"], q["bs"]), "mask": q["z_mask"].rearrange("b i j c -> (b i) (j c)"),
                "ln_w": col(chip, "l0_ln_w"), "ln_b": None, "lnc_w": col(chip, "l0_lnc_w"), "lnc_b": None,
                "protein": q["protein_pair"], "compound": q["compound_pair"]}
    q = {k.removeprefix("L1_conv_"): v for k, v in D.items() if k.startswith("L1_conv_")}
    return {"gates": [(q["gate_w"], q["gate_b"])], "lins": [(q["lin_w"], q["lin_b"])],
            "edge": (q["eg_w"], q["eg_b"]), "out": (q["as_w"], q["as_b"]), "mask": q["z_mask"].rearrange("b i j c -> (b i) (j c)"),
            "ln_w": col(chip, "l1_ln_w"), "ln_b": col(chip, "l1_ln_b"),
            "lnc_w": col(chip, "l1_lnc_w"), "lnc_b": col(chip, "l1_lnc_b", hi=C),
            "protein": q["protein_pair"], "compound": q["compound_pair"]}


def kernel(**inputs):
    import numpy as np
    import concourse.bacc as bacc
    from concourse.bass_utils import run_bass_kernel_spmd

    nc = bacc.Bacc("TRN2", target_bir_lowering=False, num_devices=1)
    arrays, D = {}, {}
    for name, a in inputs.items():
        if name in ("L1_ffn_U_f", "L1_ffn_V_f", "L1_ffn_b_f"):
            continue
        arrays[name] = np.ascontiguousarray(a)
        D[name] = nc.dram_tensor(name, arrays[name].shape, F32, kind="ExternalInput").ap()
    out = nc.dram_tensor("out", (1, NP_, NC_, E), F32, kind="ExternalOutput").ap()
    metaformer(nc, D, out)
    return run_bass_kernel_spmd(nc, [arrays], core_ids=[0]).results[0]["out"]
```
